# Optimizing a Trainium2 kernel written in Bass

```python
import numpy as np
import jax
import jax.numpy as jnp

def _softmax(x, axis=-1):
    return jax.nn.softmax(x, axis=axis)

def _gelu(x):
    return jax.nn.gelu(x, approximate=True)

def _silu(x):
    return jax.nn.silu(x)

def _sigmoid(x):
    return jax.nn.sigmoid(x)

def _layernorm(x, axis=-1, eps=1e-05):
    m = jnp.mean(x, axis=axis, keepdims=True)
    v = jnp.var(x, axis=axis, keepdims=True)
    return (x - m) / jnp.sqrt(v + eps)

def _scatter_add(tgt, idx, src, axis=0):
    return tgt.at[idx].add(src)

def _segment_sum(src, seg, n):
    return jax.ops.segment_sum(src, seg, n)
kernel_name = 'mk_xattn_seq_d4_seqx_r4_3fb1d8'

def setup_inputs(seed: int=0):
    np.random.seed(seed)
    _w = jnp.asarray

    def _rec_inputs():
        import jax
        import jax.numpy as jnp
        _rk = jax.random.key(seed)
        x = 7.22e-05 + 1 * jax.random.normal(jax.random.fold_in(_rk, 1), (16, 100, 512), jnp.float32)
        _lenS = 100 - jax.random.randint(jax.random.fold_in(_rk, 7), (16,), 0, max(1, 100 // 4) + 1, jnp.int32)
        _lenS2 = 361 - jax.random.randint(jax.random.fold_in(_rk, 8), (16,), 0, max(1, 361 // 4) + 1, jnp.int32)
        _ctx_2048P = jax.random.normal(jax.random.fold_in(_rk, 11), (16, 16, 512), jnp.float32)
        _ctx_2048c = jax.random.dirichlet(jax.random.fold_in(_rk, 511), 0.3 * jnp.ones((16,), jnp.float32), (16, 361))
        _ctx_2048t = jnp.einsum('bsk,bkd->bsd', _ctx_2048c, _ctx_2048P)
        _ctx_2048t = _ctx_2048t * jax.lax.rsqrt(jnp.mean(jnp.square(_ctx_2048t)) + 1e-12) * 0.953939
        ctx_2048 = 4.13588e-05 + 0.999923 * (_ctx_2048t + 0.3 * jax.random.normal(jax.random.fold_in(_rk, 611), (16, 361, 512), jnp.float32))
        _validS = jnp.arange(100)[None, :] < _lenS[:, None]
        _validS2 = jnp.arange(361)[None, :] < _lenS2[:, None]
        _causal = jnp.tril(jnp.ones((100, 100), dtype=bool))
        mask_Bx1xSxS2_ff0 = jnp.where(jnp.ones((16, 1, 100, 361), dtype=bool), 0.0, -1000000000.0).astype(jnp.float32)
        mask_BxS2_bf1 = jnp.ones((16, 361), dtype=bool)
        return (x, ctx_2048, mask_Bx1xSxS2_ff0, mask_BxS2_bf1)
    x, ctx_2048, mask_Bx1xSxS2_ff0, mask_BxS2_bf1 = _rec_inputs()

    def _L0_xattn_setup():
        import jax, jax.numpy as jnp
        import numpy as np
        H = 512
        NH = 32
        KVH = 8
        HD = H // NH
        GROUPS = NH // KVH
        EPS = 1e-06
        B, L, S = (4, 256, 256)

        def _gqa_forward(hidden_state, encoder_hidden_state, encoder_attention_mask, Wq, bq, Wk, bk, Wv, bv, Wo, bo, gamma, beta):
            b, l, _ = hidden_state.shape
            s = encoder_hidden_state.shape[1]
            q = hidden_state @ Wq + bq
            k = encoder_hidden_state @ Wk + bk
            v = encoder_hidden_state @ Wv + bv
            q = q.reshape(b, l, KVH, GROUPS, HD).transpose(0, 2, 3, 1, 4)
            k = k.reshape(b, s, KVH, HD).transpose(0, 2, 1, 3)
            v = v.reshape(b, s, KVH, HD).transpose(0, 2, 1, 3)
            scale = 1.0 / jnp.sqrt(jnp.asarray(HD, q.dtype))
            scores = jnp.einsum('bkgld,bksd->bkgls', q, k) * scale
            scores = scores + encoder_attention_mask[:, :, None, :, :]
            attn = jax.nn.softmax(scores, axis=-1)
            out = jnp.einsum('bkgls,bksd->bkgld', attn, v)
            out = out.transpose(0, 3, 1, 2, 4).reshape(b, l, H)
            out = out @ Wo + bo
            x = out + hidden_state
            mu = jnp.mean(x, axis=-1, keepdims=True)
            var = jnp.var(x, axis=-1, keepdims=True)
            return (x - mu) * jax.lax.rsqrt(var + EPS) * gamma + beta
        key = jax.random.key(seed)
        ks = jax.random.split(key, 12)
        sd = 0.02
        return {'hidden_state': jax.random.normal(ks[0], (B, L, H), jnp.float32), 'encoder_hidden_state': jax.random.normal(ks[1], (B, S, H), jnp.float32), 'encoder_attention_mask': jnp.zeros((B, 1, L, S), jnp.float32), 'Wq': jax.random.normal(ks[2], (H, H), jnp.float32) * sd, 'bq': jnp.zeros((H,), jnp.float32), 'Wk': jax.random.normal(ks[3], (H, KVH * HD), jnp.float32) * sd, 'bk': jnp.zeros((KVH * HD,), jnp.float32), 'Wv': jax.random.normal(ks[4], (H, KVH * HD), jnp.float32) * sd, 'bv': jnp.zeros((KVH * HD,), jnp.float32), 'Wo': jax.random.normal(ks[5], (H, H), jnp.float32) * sd, 'bo': jnp.zeros((H,), jnp.float32), 'gamma': jnp.ones((H,), jnp.float32), 'beta': jnp.zeros((H,), jnp.float32)}
    _L0_xattn_all = _L0_xattn_setup()
    _L0_xattn_in = {k: v for k, v in _L0_xattn_all.items() if k in ('Wq', 'bq', 'Wk', 'bk', 'Wv', 'bv', 'Wo', 'bo', 'gamma', 'beta')}
    del _L0_xattn_all

    def _L1_xattn_setup():
        import jax, jax.numpy as jnp
        import numpy as np
        E, H, L, B = (512, 32, 256, 4)
        S = E // H
        DM, DD = (32, 64)

        def _ln(x, w, b, eps=1e-05):
            m = x.mean(-1, keepdims=True)
            v = ((x - m) ** 2).mean(-1, keepdims=True)
            return (x - m) / jnp.sqrt(v + eps) * w + b

        def _block(x, state, ln1_w, ln1_b, ln2_w, ln2_b, maa_x, maa_w1, maa_w2, maa_stack, time_decay, td_w1, td_w2, u, Wr, Wk, Wv, Wg, Wo, gn_w, gn_b, ffn_maa_k, ffn_maa_r, Wfk, Wfr, Wfv):
            b, l, e = x.shape
            h = u.shape[0]
            s_ = e // h
            xa = _ln(x, ln1_w, ln1_b)
            sx = jnp.concatenate([state[:, 1:2] - xa[:, :1], xa[:, :-1] - xa[:, 1:]], axis=1)
            xxx = jnp.tanh((xa + sx * maa_x) @ maa_w1).reshape(b, l, 5, DM)
            xxx = jnp.einsum('blfd,fde->blfe', xxx, maa_w2)
            xm = xa[:, :, None] + sx[:, :, None] * (maa_stack + xxx)
            xk, xw, xv, xr, xg = (xm[:, :, j] for j in range(5))
            w = jnp.exp(-jnp.exp(time_decay + jnp.tanh(xw @ td_w1) @ td_w2)).reshape(b, l, h, s_)
            r = (xr @ Wr.T).reshape(b, l, h, s_)
            k = (xk @ Wk.T).reshape(b, l, h, s_)
            v = (xv @ Wv.T).reshape(b, l, h, s_)
            g = jax.nn.silu(xg @ Wg.T)
            s0 = state[:, 2:2 + s_].reshape(b, h, s_, s_)

            def step(s, rkvw):
                r_t, k_t, v_t, w_t = rkvw
                a = k_t[..., :, None] * v_t[..., None, :]
                out = jnp.einsum('bhi,bhij->bhj', r_t, u * a + s)
                s = a + w_t[..., :, None] * s
                return (s, out)
            rkvw = tuple((jnp.moveaxis(t, 1, 0) for t in (r, k, v, w)))
            _, out = jax.lax.scan(step, s0, rkvw)
            out = jnp.moveaxis(out, 0, 1).reshape(b, l, e)
            og = out.reshape(b, l, h, s_)
            m = og.mean(-1, keepdims=True)
            va = ((og - m) ** 2).mean(-1, keepdims=True)
            og = ((og - m) / jnp.sqrt(va + 1e-05)).reshape(b, l, e) * gn_w + gn_b
            x1 = x + og * g @ Wo.T
            xc = _ln(x1, ln2_w, ln2_b)
            sx2 = jnp.concatenate([state[:, 0:1] - xc[:, :1], xc[:, :-1] - xc[:, 1:]], axis=1)
            xk2 = xc + sx2 * ffn_maa_k
            xr2 = xc + sx2 * ffn_maa_r
            rr = jax.nn.sigmoid(xr2 @ Wfr.T)
            kk = jnp.square(jax.nn.relu(xk2 @ Wfk.T))
            return x1 + rr * (kk @ Wfv.T)
        key = jax.random.key(seed)
        ks = jax.random.split(key, 24)
        sc = 0.02
        d = {'x': jax.random.normal(ks[0], (B, L, E), jnp.float32), 'state': jax.random.normal(ks[1], (B, 2 + S, E), jnp.float32) * 0.1, 'ln1_w': jnp.ones((E,), jnp.float32), 'ln1_b': jnp.zeros((E,), jnp.float32), 'ln2_w': jnp.ones((E,), jnp.float32), 'ln2_b': jnp.zeros((E,), jnp.float32), 'maa_x': jax.random.normal(ks[2], (E,), jnp.float32) * 0.1, 'maa_w1': jax.random.normal(ks[3], (E, 5 * DM), jnp.float32) * sc, 'maa_w2': jax.random.normal(ks[4], (5, DM, E), jnp.float32) * sc, 'maa_stack': jax.random.normal(ks[5], (1, 5, E), jnp.float32) * 0.1, 'time_decay': jax.random.normal(ks[6], (E,), jnp.float32) * 0.5, 'td_w1': jax.random.normal(ks[7], (E, DD), jnp.float32) * sc, 'td_w2': jax.random.normal(ks[8], (DD, E), jnp.float32) * sc, 'u': jax.random.normal(ks[9], (H, S, 1), jnp.float32) * 0.1, 'Wr': jax.random.normal(ks[10], (E, E), jnp.float32) * sc, 'Wk': jax.random.normal(ks[11], (E, E), jnp.float32) * sc, 'Wv': jax.random.normal(ks[12], (E, E), jnp.float32) * sc, 'Wg': jax.random.normal(ks[13], (E, E), jnp.float32) * sc, 'Wo': jax.random.normal(ks[14], (E, E), jnp.float32) * sc, 'gn_w': jnp.ones((E,), jnp.float32), 'gn_b': jnp.zeros((E,), jnp.float32), 'ffn_maa_k': jax.random.normal(ks[15], (E,), jnp.float32) * 0.1, 'ffn_maa_r': jax.random.normal(ks[16], (E,), jnp.float32) * 0.1, 'Wfk': jax.random.normal(ks[17], (E, E), jnp.float32) * sc, 'Wfr': jax.random.normal(ks[18], (E, E), jnp.float32) * sc, 'Wfv': jax.random.normal(ks[19], (E, E), jnp.float32) * sc}
        return d
    _L1_xattn_all = _L1_xattn_setup()
    _L1_xattn_in = {k: v for k, v in _L1_xattn_all.items() if k in ('ln1_w', 'ln1_b', 'ln2_w', 'ln2_b', 'maa_x', 'maa_w1', 'maa_w2', 'maa_stack', 'time_decay', 'td_w1', 'td_w2', 'u', 'Wr', 'Wk', 'Wv', 'Wg', 'Wo', 'gn_w', 'gn_b', 'ffn_maa_k', 'ffn_maa_r', 'Wfk', 'Wfr', 'Wfv')}
    del _L1_xattn_all

    def _L2_xattn_setup():
        import jax, jax.numpy as jnp
        import numpy as np
        D = 512
        H = 16
        HD = D // H
        INNER = 4 * D
        EPS = 1e-05

        def layer_norm(x, w, b):
            mu = jnp.mean(x, axis=-1, keepdims=True)
            var = jnp.mean(jnp.square(x - mu), axis=-1, keepdims=True)
            return (x - mu) * jax.lax.rsqrt(var + EPS) * w + b
        key = jax.random.key(seed)
        ks = jax.random.split(key, 12)
        B, LQ, LK = (4, 256, 512)
        std = 0.02
        inp = {'hidden_states': jax.random.normal(ks[0], (B, LQ, D), jnp.float32), 'encoder_hidden_states': jax.random.normal(ks[1], (B, LK, D), jnp.float32), 'encoder_attention_mask': jnp.ones((B, LK), dtype=bool), 'ln1_w': jnp.ones((D,), jnp.float32), 'ln1_b': jnp.zeros((D,), jnp.float32), 'q_w': jax.random.normal(ks[2], (D, D), jnp.float32) * std, 'q_b': jnp.zeros((D,), jnp.float32), 'k_w': jax.random.normal(ks[3], (D, D), jnp.float32) * std, 'k_b': jnp.zeros((D,), jnp.float32), 'v_w': jax.random.normal(ks[4], (D, D), jnp.float32) * std, 'v_b': jnp.zeros((D,), jnp.float32), 'cproj_w': jax.random.normal(ks[5], (D, D), jnp.float32) * std, 'cproj_b': jnp.zeros((D,), jnp.float32), 'ln2_w': jnp.ones((D,), jnp.float32), 'ln2_b': jnp.zeros((D,), jnp.float32), 'fc_w': jax.random.normal(ks[6], (D, INNER), jnp.float32) * std, 'fc_b': jnp.zeros((INNER,), jnp.float32), 'proj_w': jax.random.normal(ks[7], (INNER, D), jnp.float32) * std, 'proj_b': jnp.zeros((D,), jnp.float32)}
        return inp
    _L2_xattn_all = _L2_xattn_setup()
    _L2_xattn_in = {k: v for k, v in _L2_xattn_all.items() if k in ('ln1_w', 'ln1_b', 'q_w', 'q_b', 'k_w', 'k_b', 'v_w', 'v_b', 'cproj_w', 'cproj_b', 'ln2_w', 'ln2_b', 'fc_w', 'fc_b', 'proj_w', 'proj_b')}
    del _L2_xattn_all

    def _L3_xattn_setup():
        import jax, jax.numpy as jnp
        import numpy as np
        E, H, L, B = (512, 32, 256, 4)
        S = E // H
        DM, DD = (32, 64)

        def _ln(x, w, b, eps=1e-05):
            m = x.mean(-1, keepdims=True)
            v = ((x - m) ** 2).mean(-1, keepdims=True)
            return (x - m) / jnp.sqrt(v + eps) * w + b

        def _block(x, state, ln1_w, ln1_b, ln2_w, ln2_b, maa_x, maa_w1, maa_w2, maa_stack, time_decay, td_w1, td_w2, u, Wr, Wk, Wv, Wg, Wo, gn_w, gn_b, ffn_maa_k, ffn_maa_r, Wfk, Wfr, Wfv):
            b, l, e = x.shape
            h = u.shape[0]
            s_ = e // h
            xa = _ln(x, ln1_w, ln1_b)
            sx = jnp.concatenate([state[:, 1:2] - xa[:, :1], xa[:, :-1] - xa[:, 1:]], axis=1)
            xxx = jnp.tanh((xa + sx * maa_x) @ maa_w1).reshape(b, l, 5, DM)
            xxx = jnp.einsum('blfd,fde->blfe', xxx, maa_w2)
            xm = xa[:, :, None] + sx[:, :, None] * (maa_stack + xxx)
            xk, xw, xv, xr, xg = (xm[:, :, j] for j in range(5))
            w = jnp.exp(-jnp.exp(time_decay + jnp.tanh(xw @ td_w1) @ td_w2)).reshape(b, l, h, s_)
            r = (xr @ Wr.T).reshape(b, l, h, s_)
            k = (xk @ Wk.T).reshape(b, l, h, s_)
            v = (xv @ Wv.T).reshape(b, l, h, s_)
            g = jax.nn.silu(xg @ Wg.T)
            s0 = state[:, 2:2 + s_].reshape(b, h, s_, s_)

            def step(s, rkvw):
                r_t, k_t, v_t, w_t = rkvw
                a = k_t[..., :, None] * v_t[..., None, :]
                out = jnp.einsum('bhi,bhij->bhj', r_t, u * a + s)
                s = a + w_t[..., :, None] * s
                return (s, out)
            rkvw = tuple((jnp.moveaxis(t, 1, 0) for t in (r, k, v, w)))
            _, out = jax.lax.scan(step, s0, rkvw)
            out = jnp.moveaxis(out, 0, 1).reshape(b, l, e)
            og = out.reshape(b, l, h, s_)
            m = og.mean(-1, keepdims=True)
            va = ((og - m) ** 2).mean(-1, keepdims=True)
            og = ((og - m) / jnp.sqrt(va + 1e-05)).reshape(b, l, e) * gn_w + gn_b
            x1 = x + og * g @ Wo.T
            xc = _ln(x1, ln2_w, ln2_b)
            sx2 = jnp.concatenate([state[:, 0:1] - xc[:, :1], xc[:, :-1] - xc[:, 1:]], axis=1)
            xk2 = xc + sx2 * ffn_maa_k
            xr2 = xc + sx2 * ffn_maa_r
            rr = jax.nn.sigmoid(xr2 @ Wfr.T)
            kk = jnp.square(jax.nn.relu(xk2 @ Wfk.T))
            return x1 + rr * (kk @ Wfv.T)
        key = jax.random.key(seed)
        ks = jax.random.split(key, 24)
        sc = 0.02
        d = {'x': jax.random.normal(ks[0], (B, L, E), jnp.float32), 'state': jax.random.normal(ks[1], (B, 2 + S, E), jnp.float32) * 0.1, 'ln1_w': jnp.ones((E,), jnp.float32), 'ln1_b': jnp.zeros((E,), jnp.float32), 'ln2_w': jnp.ones((E,), jnp.float32), 'ln2_b': jnp.zeros((E,), jnp.float32), 'maa_x': jax.random.normal(ks[2], (E,), jnp.float32) * 0.1, 'maa_w1': jax.random.normal(ks[3], (E, 5 * DM), jnp.float32) * sc, 'maa_w2': jax.random.normal(ks[4], (5, DM, E), jnp.float32) * sc, 'maa_stack': jax.random.normal(ks[5], (1, 5, E), jnp.float32) * 0.1, 'time_decay': jax.random.normal(ks[6], (E,), jnp.float32) * 0.5, 'td_w1': jax.random.normal(ks[7], (E, DD), jnp.float32) * sc, 'td_w2': jax.random.normal(ks[8], (DD, E), jnp.float32) * sc, 'u': jax.random.normal(ks[9], (H, S, 1), jnp.float32) * 0.1, 'Wr': jax.random.normal(ks[10], (E, E), jnp.float32) * sc, 'Wk': jax.random.normal(ks[11], (E, E), jnp.float32) * sc, 'Wv': jax.random.normal(ks[12], (E, E), jnp.float32) * sc, 'Wg': jax.random.normal(ks[13], (E, E), jnp.float32) * sc, 'Wo': jax.random.normal(ks[14], (E, E), jnp.float32) * sc, 'gn_w': jnp.ones((E,), jnp.float32), 'gn_b': jnp.zeros((E,), jnp.float32), 'ffn_maa_k': jax.random.normal(ks[15], (E,), jnp.float32) * 0.1, 'ffn_maa_r': jax.random.normal(ks[16], (E,), jnp.float32) * 0.1, 'Wfk': jax.random.normal(ks[17], (E, E), jnp.float32) * sc, 'Wfr': jax.random.normal(ks[18], (E, E), jnp.float32) * sc, 'Wfv': jax.random.normal(ks[19], (E, E), jnp.float32) * sc}
        return d
    _L3_xattn_all = _L3_xattn_setup()
    _L3_xattn_in = {k: v for k, v in _L3_xattn_all.items() if k in ('ln1_w', 'ln1_b', 'ln2_w', 'ln2_b', 'maa_x', 'maa_w1', 'maa_w2', 'maa_stack', 'time_decay', 'td_w1', 'td_w2', 'u', 'Wr', 'Wk', 'Wv', 'Wg', 'Wo', 'gn_w', 'gn_b', 'ffn_maa_k', 'ffn_maa_r', 'Wfk', 'Wfr', 'Wfv')}
    del _L3_xattn_all
    return {'x': x, 'ctx_2048': ctx_2048, 'mask_Bx1xSxS2_ff0': mask_Bx1xSxS2_ff0, 'mask_BxS2_bf1': mask_BxS2_bf1, 'L0_xattn_Wq': _L0_xattn_in['Wq'], 'L0_xattn_bq': _L0_xattn_in['bq'], 'L0_xattn_Wk': _L0_xattn_in['Wk'], 'L0_xattn_bk': _L0_xattn_in['bk'], 'L0_xattn_Wv': _L0_xattn_in['Wv'], 'L0_xattn_bv': _L0_xattn_in['bv'], 'L0_xattn_Wo': _L0_xattn_in['Wo'], 'L0_xattn_bo': _L0_xattn_in['bo'], 'L0_xattn_gamma': _L0_xattn_in['gamma'], 'L0_xattn_beta': _L0_xattn_in['beta'], 'L1_xattn_ln1_w': _L1_xattn_in['ln1_w'], 'L1_xattn_ln1_b': _L1_xattn_in['ln1_b'], 'L1_xattn_ln2_w': _L1_xattn_in['ln2_w'], 'L1_xattn_ln2_b': _L1_xattn_in['ln2_b'], 'L1_xattn_maa_x': _L1_xattn_in['maa_x'], 'L1_xattn_maa_w1': _L1_xattn_in['maa_w1'], 'L1_xattn_maa_w2': _L1_xattn_in['maa_w2'], 'L1_xattn_maa_stack': _L1_xattn_in['maa_stack'], 'L1_xattn_time_decay': _L1_xattn_in['time_decay'], 'L1_xattn_td_w1': _L1_xattn_in['td_w1'], 'L1_xattn_td_w2': _L1_xattn_in['td_w2'], 'L1_xattn_u': _L1_xattn_in['u'], 'L1_xattn_Wr': _L1_xattn_in['Wr'], 'L1_xattn_Wk': _L1_xattn_in['Wk'], 'L1_xattn_Wv': _L1_xattn_in['Wv'], 'L1_xattn_Wg': _L1_xattn_in['Wg'], 'L1_xattn_Wo': _L1_xattn_in['Wo'], 'L1_xattn_gn_w': _L1_xattn_in['gn_w'], 'L1_xattn_gn_b': _L1_xattn_in['gn_b'], 'L1_xattn_ffn_maa_k': _L1_xattn_in['ffn_maa_k'], 'L1_xattn_ffn_maa_r': _L1_xattn_in['ffn_maa_r'], 'L1_xattn_Wfk': _L1_xattn_in['Wfk'], 'L1_xattn_Wfr': _L1_xattn_in['Wfr'], 'L1_xattn_Wfv': _L1_xattn_in['Wfv'], 'L2_xattn_ln1_w': _L2_xattn_in['ln1_w'], 'L2_xattn_ln1_b': _L2_xattn_in['ln1_b'], 'L2_xattn_q_w': _L2_xattn_in['q_w'], 'L2_xattn_q_b': _L2_xattn_in['q_b'], 'L2_xattn_k_w': _L2_xattn_in['k_w'], 'L2_xattn_k_b': _L2_xattn_in['k_b'], 'L2_xattn_v_w': _L2_xattn_in['v_w'], 'L2_xattn_v_b': _L2_xattn_in['v_b'], 'L2_xattn_cproj_w': _L2_xattn_in['cproj_w'], 'L2_xattn_cproj_b': _L2_xattn_in['cproj_b'], 'L2_xattn_ln2_w': _L2_xattn_in['ln2_w'], 'L2_xattn_ln2_b': _L2_xattn_in['ln2_b'], 'L2_xattn_fc_w': _L2_xattn_in['fc_w'], 'L2_xattn_fc_b': _L2_xattn_in['fc_b'], 'L2_xattn_proj_w': _L2_xattn_in['proj_w'], 'L2_xattn_proj_b': _L2_xattn_in['proj_b'], 'L3_xattn_ln1_w': _L3_xattn_in['ln1_w'], 'L3_xattn_ln1_b': _L3_xattn_in['ln1_b'], 'L3_xattn_ln2_w': _L3_xattn_in['ln2_w'], 'L3_xattn_ln2_b': _L3_xattn_in['ln2_b'], 'L3_xattn_maa_x': _L3_xattn_in['maa_x'], 'L3_xattn_maa_w1': _L3_xattn_in['maa_w1'], 'L3_xattn_maa_w2': _L3_xattn_in['maa_w2'], 'L3_xattn_maa_stack': _L3_xattn_in['maa_stack'], 'L3_xattn_time_decay': _L3_xattn_in['time_decay'], 'L3_xattn_td_w1': _L3_xattn_in['td_w1'], 'L3_xattn_td_w2': _L3_xattn_in['td_w2'], 'L3_xattn_u': _L3_xattn_in['u'], 'L3_xattn_Wr': _L3_xattn_in['Wr'], 'L3_xattn_Wk': _L3_xattn_in['Wk'], 'L3_xattn_Wv': _L3_xattn_in['Wv'], 'L3_xattn_Wg': _L3_xattn_in['Wg'], 'L3_xattn_Wo': _L3_xattn_in['Wo'], 'L3_xattn_gn_w': _L3_xattn_in['gn_w'], 'L3_xattn_gn_b': _L3_xattn_in['gn_b'], 'L3_xattn_ffn_maa_k': _L3_xattn_in['ffn_maa_k'], 'L3_xattn_ffn_maa_r': _L3_xattn_in['ffn_maa_r'], 'L3_xattn_Wfk': _L3_xattn_in['Wfk'], 'L3_xattn_Wfr': _L3_xattn_in['Wfr'], 'L3_xattn_Wfv': _L3_xattn_in['Wfv']}

def reference(x, ctx_2048, mask_Bx1xSxS2_ff0, mask_BxS2_bf1, L0_xattn_Wq, L0_xattn_bq, L0_xattn_Wk, L0_xattn_bk, L0_xattn_Wv, L0_xattn_bv, L0_xattn_Wo, L0_xattn_bo, L0_xattn_gamma, L0_xattn_beta, L1_xattn_ln1_w, L1_xattn_ln1_b, L1_xattn_ln2_w, L1_xattn_ln2_b, L1_xattn_maa_x, L1_xattn_maa_w1, L1_xattn_maa_w2, L1_xattn_maa_stack, L1_xattn_time_decay, L1_xattn_td_w1, L1_xattn_td_w2, L1_xattn_u, L1_xattn_Wr, L1_xattn_Wk, L1_xattn_Wv, L1_xattn_Wg, L1_xattn_Wo, L1_xattn_gn_w, L1_xattn_gn_b, L1_xattn_ffn_maa_k, L1_xattn_ffn_maa_r, L1_xattn_Wfk, L1_xattn_Wfr, L1_xattn_Wfv, L2_xattn_ln1_w, L2_xattn_ln1_b, L2_xattn_q_w, L2_xattn_q_b, L2_xattn_k_w, L2_xattn_k_b, L2_xattn_v_w, L2_xattn_v_b, L2_xattn_cproj_w, L2_xattn_cproj_b, L2_xattn_ln2_w, L2_xattn_ln2_b, L2_xattn_fc_w, L2_xattn_fc_b, L2_xattn_proj_w, L2_xattn_proj_b, L3_xattn_ln1_w, L3_xattn_ln1_b, L3_xattn_ln2_w, L3_xattn_ln2_b, L3_xattn_maa_x, L3_xattn_maa_w1, L3_xattn_maa_w2, L3_xattn_maa_stack, L3_xattn_time_decay, L3_xattn_td_w1, L3_xattn_td_w2, L3_xattn_u, L3_xattn_Wr, L3_xattn_Wk, L3_xattn_Wv, L3_xattn_Wg, L3_xattn_Wo, L3_xattn_gn_w, L3_xattn_gn_b, L3_xattn_ffn_maa_k, L3_xattn_ffn_maa_r, L3_xattn_Wfk, L3_xattn_Wfr, L3_xattn_Wfv):
    import jax
    import jax.numpy as jnp

    def _L0_xattn_ref(hidden_state, encoder_hidden_state, encoder_attention_mask, Wq, bq, Wk, bk, Wv, bv, Wo, bo, gamma, beta):
        import jax, jax.numpy as jnp
        import numpy as np
        H = 512
        NH = 32
        KVH = 8
        HD = H // NH
        GROUPS = NH // KVH
        EPS = 1e-06
        B, L, S = (4, 256, 256)

        def _gqa_forward(hidden_state, encoder_hidden_state, encoder_attention_mask, Wq, bq, Wk, bk, Wv, bv, Wo, bo, gamma, beta):
            b, l, _ = hidden_state.shape
            s = encoder_hidden_state.shape[1]
            q = hidden_state @ Wq + bq
            k = encoder_hidden_state @ Wk + bk
            v = encoder_hidden_state @ Wv + bv
            q = q.reshape(b, l, KVH, GROUPS, HD).transpose(0, 2, 3, 1, 4)
            k = k.reshape(b, s, KVH, HD).transpose(0, 2, 1, 3)
            v = v.reshape(b, s, KVH, HD).transpose(0, 2, 1, 3)
            scale = 1.0 / jnp.sqrt(jnp.asarray(HD, q.dtype))
            scores = jnp.einsum('bkgld,bksd->bkgls', q, k) * scale
            scores = scores + encoder_attention_mask[:, :, None, :, :]
            attn = jax.nn.softmax(scores, axis=-1)
            out = jnp.einsum('bkgls,bksd->bkgld', attn, v)
            out = out.transpose(0, 3, 1, 2, 4).reshape(b, l, H)
            out = out @ Wo + bo
            x = out + hidden_state
            mu = jnp.mean(x, axis=-1, keepdims=True)
            var = jnp.var(x, axis=-1, keepdims=True)
            return (x - mu) * jax.lax.rsqrt(var + EPS) * gamma + beta
        return _gqa_forward(hidden_state, encoder_hidden_state, encoder_attention_mask, Wq, bq, Wk, bk, Wv, bv, Wo, bo, gamma, beta)

    def _L1_xattn_ref(x, state, ln1_w, ln1_b, ln2_w, ln2_b, maa_x, maa_w1, maa_w2, maa_stack, time_decay, td_w1, td_w2, u, Wr, Wk, Wv, Wg, Wo, gn_w, gn_b, ffn_maa_k, ffn_maa_r, Wfk, Wfr, Wfv):
        import jax, jax.numpy as jnp
        import numpy as np
        E, H, L, B = (512, 32, 256, 4)
        S = E // H
        DM, DD = (32, 64)

        def _ln(x, w, b, eps=1e-05):
            m = x.mean(-1, keepdims=True)
            v = ((x - m) ** 2).mean(-1, keepdims=True)
            return (x - m) / jnp.sqrt(v + eps) * w + b

        def _block(x, state, ln1_w, ln1_b, ln2_w, ln2_b, maa_x, maa_w1, maa_w2, maa_stack, time_decay, td_w1, td_w2, u, Wr, Wk, Wv, Wg, Wo, gn_w, gn_b, ffn_maa_k, ffn_maa_r, Wfk, Wfr, Wfv):
            b, l, e = x.shape
            h = u.shape[0]
            s_ = e // h
            xa = _ln(x, ln1_w, ln1_b)
            sx = jnp.concatenate([state[:, 1:2] - xa[:, :1], xa[:, :-1] - xa[:, 1:]], axis=1)
            xxx = jnp.tanh((xa + sx * maa_x) @ maa_w1).reshape(b, l, 5, DM)
            xxx = jnp.einsum('blfd,fde->blfe', xxx, maa_w2)
            xm = xa[:, :, None] + sx[:, :, None] * (maa_stack + xxx)
            xk, xw, xv, xr, xg = (xm[:, :, j] for j in range(5))
            w = jnp.exp(-jnp.exp(time_decay + jnp.tanh(xw @ td_w1) @ td_w2)).reshape(b, l, h, s_)
            r = (xr @ Wr.T).reshape(b, l, h, s_)
            k = (xk @ Wk.T).reshape(b, l, h, s_)
            v = (xv @ Wv.T).reshape(b, l, h, s_)
            g = jax.nn.silu(xg @ Wg.T)
            s0 = state[:, 2:2 + s_].reshape(b, h, s_, s_)

            def step(s, rkvw):
                r_t, k_t, v_t, w_t = rkvw
                a = k_t[..., :, None] * v_t[..., None, :]
                out = jnp.einsum('bhi,bhij->bhj', r_t, u * a + s)
                s = a + w_t[..., :, None] * s
                return (s, out)
            rkvw = tuple((jnp.moveaxis(t, 1, 0) for t in (r, k, v, w)))
            _, out = jax.lax.scan(step, s0, rkvw)
            out = jnp.moveaxis(out, 0, 1).reshape(b, l, e)
            og = out.reshape(b, l, h, s_)
            m = og.mean(-1, keepdims=True)
            va = ((og - m) ** 2).mean(-1, keepdims=True)
            og = ((og - m) / jnp.sqrt(va + 1e-05)).reshape(b, l, e) * gn_w + gn_b
            x1 = x + og * g @ Wo.T
            xc = _ln(x1, ln2_w, ln2_b)
            sx2 = jnp.concatenate([state[:, 0:1] - xc[:, :1], xc[:, :-1] - xc[:, 1:]], axis=1)
            xk2 = xc + sx2 * ffn_maa_k
            xr2 = xc + sx2 * ffn_maa_r
            rr = jax.nn.sigmoid(xr2 @ Wfr.T)
            kk = jnp.square(jax.nn.relu(xk2 @ Wfk.T))
            return x1 + rr * (kk @ Wfv.T)
        return _block(x, state, ln1_w, ln1_b, ln2_w, ln2_b, maa_x, maa_w1, maa_w2, maa_stack, time_decay, td_w1, td_w2, u, Wr, Wk, Wv, Wg, Wo, gn_w, gn_b, ffn_maa_k, ffn_maa_r, Wfk, Wfr, Wfv)

    def _L2_xattn_ref(hidden_states, encoder_hidden_states, encoder_attention_mask, ln1_w, ln1_b, q_w, q_b, k_w, k_b, v_w, v_b, cproj_w, cproj_b, ln2_w, ln2_b, fc_w, fc_b, proj_w, proj_b):
        import jax, jax.numpy as jnp
        import numpy as np
        D = 512
        H = 16
        HD = D // H
        INNER = 4 * D
        EPS = 1e-05

        def layer_norm(x, w, b):
            mu = jnp.mean(x, axis=-1, keepdims=True)
            var = jnp.mean(jnp.square(x - mu), axis=-1, keepdims=True)
            return (x - mu) * jax.lax.rsqrt(var + EPS) * w + b
        B, LQ, _ = hidden_states.shape
        LK = encoder_hidden_states.shape[1]
        residual = hidden_states
        x = layer_norm(hidden_states, ln1_w, ln1_b)
        q = (x @ q_w + q_b).reshape(B, LQ, H, HD).transpose(0, 2, 1, 3)
        k = (encoder_hidden_states @ k_w + k_b).reshape(B, LK, H, HD).transpose(0, 2, 1, 3)
        v = (encoder_hidden_states @ v_w + v_b).reshape(B, LK, H, HD).transpose(0, 2, 1, 3)
        scale = 1.0 / np.sqrt(HD).astype(np.float32)
        scores = jnp.einsum('bhqd,bhkd->bhqk', q, k) * scale
        mask = encoder_attention_mask[:, None, None, :]
        mask_value = jnp.finfo(scores.dtype).min
        scores = jnp.where(mask, scores, mask_value)
        attn = jax.nn.softmax(scores, axis=-1)
        out = jnp.einsum('bhqk,bhkd->bhqd', attn, v)
        out = out.transpose(0, 2, 1, 3).reshape(B, LQ, D)
        out = out @ cproj_w + cproj_b
        hidden = out + residual
        residual = hidden
        y = layer_norm(hidden, ln2_w, ln2_b)
        y = jax.nn.gelu(y @ fc_w + fc_b, approximate=True)
        y = y @ proj_w + proj_b
        return residual + y

    def _L3_xattn_ref(x, state, ln1_w, ln1_b, ln2_w, ln2_b, maa_x, maa_w1, maa_w2, maa_stack, time_decay, td_w1, td_w2, u, Wr, Wk, Wv, Wg, Wo, gn_w, gn_b, ffn_maa_k, ffn_maa_r, Wfk, Wfr, Wfv):
        import jax, jax.numpy as jnp
        import numpy as np
        E, H, L, B = (512, 32, 256, 4)
        S = E // H
        DM, DD = (32, 64)

        def _ln(x, w, b, eps=1e-05):
            m = x.mean(-1, keepdims=True)
            v = ((x - m) ** 2).mean(-1, keepdims=True)
            return (x - m) / jnp.sqrt(v + eps) * w + b

        def _block(x, state, ln1_w, ln1_b, ln2_w, ln2_b, maa_x, maa_w1, maa_w2, maa_stack, time_decay, td_w1, td_w2, u, Wr, Wk, Wv, Wg, Wo, gn_w, gn_b, ffn_maa_k, ffn_maa_r, Wfk, Wfr, Wfv):
            b, l, e = x.shape
            h = u.shape[0]
            s_ = e // h
            xa = _ln(x, ln1_w, ln1_b)
            sx = jnp.concatenate([state[:, 1:2] - xa[:, :1], xa[:, :-1] - xa[:, 1:]], axis=1)
            xxx = jnp.tanh((xa + sx * maa_x) @ maa_w1).reshape(b, l, 5, DM)
            xxx = jnp.einsum('blfd,fde->blfe', xxx, maa_w2)
            xm = xa[:, :, None] + sx[:, :, None] * (maa_stack + xxx)
            xk, xw, xv, xr, xg = (xm[:, :, j] for j in range(5))
            w = jnp.exp(-jnp.exp(time_decay + jnp.tanh(xw @ td_w1) @ td_w2)).reshape(b, l, h, s_)
            r = (xr @ Wr.T).reshape(b, l, h, s_)
            k = (xk @ Wk.T).reshape(b, l, h, s_)
            v = (xv @ Wv.T).reshape(b, l, h, s_)
            g = jax.nn.silu(xg @ Wg.T)
            s0 = state[:, 2:2 + s_].reshape(b, h, s_, s_)

            def step(s, rkvw):
                r_t, k_t, v_t, w_t = rkvw
                a = k_t[..., :, None] * v_t[..., None, :]
                out = jnp.einsum('bhi,bhij->bhj', r_t, u * a + s)
                s = a + w_t[..., :, None] * s
                return (s, out)
            rkvw = tuple((jnp.moveaxis(t, 1, 0) for t in (r, k, v, w)))
            _, out = jax.lax.scan(step, s0, rkvw)
            out = jnp.moveaxis(out, 0, 1).reshape(b, l, e)
            og = out.reshape(b, l, h, s_)
            m = og.mean(-1, keepdims=True)
            va = ((og - m) ** 2).mean(-1, keepdims=True)
            og = ((og - m) / jnp.sqrt(va + 1e-05)).reshape(b, l, e) * gn_w + gn_b
            x1 = x + og * g @ Wo.T
            xc = _ln(x1, ln2_w, ln2_b)
            sx2 = jnp.concatenate([state[:, 0:1] - xc[:, :1], xc[:, :-1] - xc[:, 1:]], axis=1)
            xk2 = xc + sx2 * ffn_maa_k
            xr2 = xc + sx2 * ffn_maa_r
            rr = jax.nn.sigmoid(xr2 @ Wfr.T)
            kk = jnp.square(jax.nn.relu(xk2 @ Wfk.T))
            return x1 + rr * (kk @ Wfv.T)
        return _block(x, state, ln1_w, ln1_b, ln2_w, ln2_b, maa_x, maa_w1, maa_w2, maa_stack, time_decay, td_w1, td_w2, u, Wr, Wk, Wv, Wg, Wo, gn_w, gn_b, ffn_maa_k, ffn_maa_r, Wfk, Wfr, Wfv)
    x = _L0_xattn_ref(x, ctx_2048, mask_Bx1xSxS2_ff0, L0_xattn_Wq, L0_xattn_bq, L0_xattn_Wk, L0_xattn_bk, L0_xattn_Wv, L0_xattn_bv, L0_xattn_Wo, L0_xattn_bo, L0_xattn_gamma, L0_xattn_beta)
    x = _L1_xattn_ref(x, ctx_2048, L1_xattn_ln1_w, L1_xattn_ln1_b, L1_xattn_ln2_w, L1_xattn_ln2_b, L1_xattn_maa_x, L1_xattn_maa_w1, L1_xattn_maa_w2, L1_xattn_maa_stack, L1_xattn_time_decay, L1_xattn_td_w1, L1_xattn_td_w2, L1_xattn_u, L1_xattn_Wr, L1_xattn_Wk, L1_xattn_Wv, L1_xattn_Wg, L1_xattn_Wo, L1_xattn_gn_w, L1_xattn_gn_b, L1_xattn_ffn_maa_k, L1_xattn_ffn_maa_r, L1_xattn_Wfk, L1_xattn_Wfr, L1_xattn_Wfv)
    x = _L2_xattn_ref(x, ctx_2048, mask_BxS2_bf1, L2_xattn_ln1_w, L2_xattn_ln1_b, L2_xattn_q_w, L2_xattn_q_b, L2_xattn_k_w, L2_xattn_k_b, L2_xattn_v_w, L2_xattn_v_b, L2_xattn_cproj_w, L2_xattn_cproj_b, L2_xattn_ln2_w, L2_xattn_ln2_b, L2_xattn_fc_w, L2_xattn_fc_b, L2_xattn_proj_w, L2_xattn_proj_b)
    x = _L3_xattn_ref(x, ctx_2048, L3_xattn_ln1_w, L3_xattn_ln1_b, L3_xattn_ln2_w, L3_xattn_ln2_b, L3_xattn_maa_x, L3_xattn_maa_w1, L3_xattn_maa_w2, L3_xattn_maa_stack, L3_xattn_time_decay, L3_xattn_td_w1, L3_xattn_td_w2, L3_xattn_u, L3_xattn_Wr, L3_xattn_Wk, L3_xattn_Wv, L3_xattn_Wg, L3_xattn_Wo, L3_xattn_gn_w, L3_xattn_gn_b, L3_xattn_ffn_maa_k, L3_xattn_ffn_maa_r, L3_xattn_Wfk, L3_xattn_Wfr, L3_xattn_Wfv)
    return x

_drawn_inputs = setup_inputs


def setup_inputs(seed=0):
    import zlib

    import numpy as np

    out = dict(_drawn_inputs(seed))
    spreads = {'L0_xattn_bq': (0.0, 0.8),
     'L0_xattn_bk': (0.0, 0.8),
     'L0_xattn_bv': (0.0, 0.1),
     'L0_xattn_bo': (0.0, 0.1),
     'L0_xattn_gamma': (1.0, 0.2),
     'L0_xattn_beta': (0.0, 0.1),
     'L1_xattn_ln1_w': (1.0, 0.2),
     'L1_xattn_ln1_b': (0.0, 0.285),
     'L1_xattn_ln2_w': (1.0, 0.6),
     'L1_xattn_ln2_b': (0.0, 0.8),
     'L1_xattn_gn_w': (1.0, 0.6),
     'L1_xattn_gn_b': (0.0, 0.715),
     'L2_xattn_ln1_w': (1.0, 0.6),
     'L2_xattn_ln1_b': (0.0, 0.8),
     'L2_xattn_q_b': (0.0, 0.8),
     'L2_xattn_k_b': (0.0, 0.8),
     'L2_xattn_v_b': (0.0, 0.1),
     'L2_xattn_cproj_b': (0.0, 0.1),
     'L2_xattn_ln2_w': (1.0, 0.2),
     'L2_xattn_ln2_b': (0.0, 0.33),
     'L2_xattn_fc_b': (0.0, 0.1),
     'L2_xattn_proj_b': (0.0, 0.1),
     'L3_xattn_ln1_w': (1.0, 0.2),
     'L3_xattn_ln1_b': (0.0, 0.304),
     'L3_xattn_ln2_w': (1.0, 0.6),
     'L3_xattn_ln2_b': (0.0, 0.8),
     'L3_xattn_gn_w': (1.0, 0.6),
     'L3_xattn_gn_b': (0.0, 0.8)}
    factors = {'L0_xattn_Wq': 7.007,
     'L0_xattn_Wk': 6.87,
     'L1_xattn_maa_x': 8.0,
     'L1_xattn_maa_w1': 3.038,
     'L1_xattn_maa_w2': 3.086,
     'L1_xattn_td_w1': 8.0,
     'L1_xattn_td_w2': 8.0,
     'L1_xattn_u': 3.152,
     'L1_xattn_ffn_maa_k': 5.816,
     'L1_xattn_ffn_maa_r': 8.0,
     'L1_xattn_Wfr': 4.174,
     'L2_xattn_q_w': 7.533,
     'L2_xattn_k_w': 7.388,
     'L3_xattn_maa_x': 8.0,
     'L3_xattn_maa_w1': 3.125,
     'L3_xattn_maa_w2': 3.196,
     'L3_xattn_td_w1': 8.0,
     'L3_xattn_td_w2': 8.0,
     'L3_xattn_u': 3.173,
     'L3_xattn_ffn_maa_k': 5.905,
     'L3_xattn_ffn_maa_r': 8.0,
     'L3_xattn_Wfr': 4.089}
    for name, (base, spread) in spreads.items():
        noise = np.random.default_rng([zlib.crc32(name.encode()), seed]).standard_normal(out[name].shape)
        drawn = base * np.exp(spread * noise) if base else spread * noise
        out[name] = jnp.asarray(drawn.astype(out[name].dtype))
    for name, factor in factors.items():
        out[name] = (out[name] * factor).astype(out[name].dtype)
    return out
```

```python
from contextlib import ExitStack

import numpy as np

import concourse.bass as bass
from concourse import mybir

F32 = mybir.dt.float32
MASK = mybir.dt.from_np(np.dtype(bool))
ALU = mybir.AluOpType
ACT = mybir.ActivationFunctionType

B, L, S, D = 16, 100, 361, 512
P = 128
C = D // P
T = B * L
NB = 2
N = NB * L
G = B // NB
E = L + 1
HS = 16
HC = P // HS
DM, DD = 32, 64
F = 2048
SC = [(0, 128), (128, 128), (256, S - 256)]
FLT = float(np.finfo(np.float32).max)
ARENA = 53096
GELU = ACT.Gelu_apprx_tanh


class Signal:

    def __init__(self, sem, per):
        self.sem, self.per = sem, per

    def at(self, i, n=0):
        return i * self.per + n + 1


def ds(i, n):
    return bass.ds(i * n, n)


class Region:

    def __init__(self, arena, start):
        self.arena, self.at = arena, start

    def take(self, *shape):
        n = int(np.prod(shape))
        v = self.arena[:, self.at:self.at + n]
        self.at += (n + 7) // 8 * 8
        assert self.at <= ARENA, self.at
        if len(shape) == 2:
            v = v.rearrange("p (a b) -> p a b", a=shape[0])
        elif len(shape) == 3:
            v = v.rearrange("p (a b c) -> p a b c", a=shape[0], b=shape[1])
        elif len(shape) == 4:
            v = v.rearrange("p (a b c d) -> p a b c d", a=shape[0], b=shape[1], c=shape[2])
        return v


class Core:

    def __init__(self, nc, ctx, dram):
        self.nc, self.ctx, self.dram, self.signals = nc, ctx, dram, []
        self.arena = ctx.enter_context(nc.sbuf_tensor("arena", [P, ARENA], F32))
        r = Region(self.arena, 0)
        self.X = r.take(C, T)
        self.ident = r.take(P)
        self.mean_w = r.take(P)
        self.gmean_w = r.take(P)
        self.heads_w = r.take(P)
        self.red_w = r.take(56)
        self.spread_w = r.take(HS, P)
        self.hmask = r.take(8)
        self.qmask = r.take(4)
        self.epsc = r.take(2)
        self.st = r.take(C, 2, B)
        self.own = r.at
        self.psum = ctx.enter_context(nc.psum_tensor("psum", [P, 8, 512], F32))
        self.bank = [self.psum[:, i, :] for i in range(8)]
        self.wide = [self.psum[:, 2 * i:2 * i + 2, 0:2 * N] for i in range(4)]
        self.loaded = self.new_signal("loaded", 32)
        self.stored = self.new_signal("stored", 16)

    def new_signal(self, name, per=1):
        self.signals.append(Signal(self.ctx.enter_context(self.nc.semaphore(name)), per))
        return self.signals[-1]

    def part(self, w, m, rows=P):
        return self.psum[0:rows, 2 * w + m // 2, (m % 2) * N:(m % 2) * N + N]

    def load(self, sp):
        sp.dma_start(self.arena[:, 0:C * T], self.dram["xT"]).then_inc(self.loaded.sem, 16)
        sp.dma_start(self.arena[:, C * T:self.own], self.dram["const"]).then_inc(self.loaded.sem, 16)

    def lead(self, sp):
        for s in self.signals:
            sp.sem_inc(s.sem, 1)

    def wait_loaded(self, eng):
        eng.wait_ge(self.loaded.sem, self.loaded.at(1))


class Layer:

    def __init__(self, sync, tensor, vector, scalar, gpsimd, done):
        self.sync, self.tensor, self.vector, self.scalar, self.gpsimd = sync, tensor, vector, scalar, gpsimd
        self.done = done


def two(v):
    return v.rearrange("p (a b) n -> p a (b n)", a=2)


def program(nc, dram, out_dram, layers=(0, 1, 2, 3)):
    with ExitStack() as ctx:
        core = Core(nc, ctx, dram)
        shared = rwkv_memory(core)
        stack, after = [], None
        for n in layers:
            if n % 2 == 0:
                stack.append(attention(core, f"L{n}", after))
            else:
                stack.append(rwkv(core, shared, f"L{n}", 0 if n == 1 else G, after))
            after = stack[-1].done
        block = ctx.enter_context(nc.Block())

        @block.sync
        def _(sp):
            core.load(sp)
            core.lead(sp)
            for layer in stack:
                layer.sync(sp)
            sp.wait_ge(*after)
            sp.dma_start(out_dram, core.arena[:, 0:C * T]).then_inc(core.stored.sem, 16)
            sp.wait_ge(core.stored.sem, core.stored.at(1))

        @block.gpsimd
        def _(pool):
            core.wait_loaded(pool)
            for layer in stack:
                layer.gpsimd(pool)

        @block.tensor
        def _(pe):
            core.wait_loaded(pe)
            for layer in stack:
                layer.tensor(pe)

        @block.vector
        def _(dve):
            core.wait_loaded(dve)
            for layer in stack:
                layer.vector(dve)

        @block.scalar
        def _(act):
            core.wait_loaded(act)
            for layer in stack:
                layer.scalar(act)



def norm_signals(core, name):
    return [core.new_signal(f"{name}_{n}", 2) for n in ("mu", "cen", "sq", "var", "lnv", "rstd", "nrm")]


class Norm:

    def __init__(self, core, told, nth, w, eps):
        self.core, self.nth, self.w, self.eps = core, nth + 1, w, eps
        self.mu, self.cen, self.sq, self.var, self.lnv, self.rstd, self.nrm = told

    def memory(self, r):
        self.yc, self.s2, self.rs = r.take(C, N), r.take(C, N), r.take(N)
        return self

    def pe_mean(self, pe, src, i):
        for c in range(C):
            mm = pe.matmul(self.core.part(self.w, 0), self.core.mean_w, src(c), start=c == 0, stop=c == C - 1)
        mm.then_inc(self.mu.sem, 1)

    def dve_center(self, dve, src, i):
        dve.wait_ge(self.mu.sem, self.mu.at(i, self.nth))
        mu = self.core.part(self.w, 0).unsqueeze(1).broadcast_to([P, C, N])
        dve.tensor_tensor(self.yc, src, mu, ALU.subtract).then_inc(self.cen.sem, 1)

    def act_square(self, act, i):
        act.wait_ge(self.cen.sem, self.cen.at(i, self.nth))
        act.activation(self.s2, self.yc, ACT.Square).then_inc(self.sq.sem, 1)

    def pe_var(self, pe, i):
        pe.wait_ge(self.sq.sem, self.sq.at(i, self.nth))
        for c in range(C):
            mm = pe.matmul(self.core.part(self.w, 2), self.core.mean_w, self.s2[:, c, :], start=c == 0,
                           stop=c == C - 1)
        mm.then_inc(self.var.sem, 1)

    def act_rstd(self, act, i):
        act.wait_ge(self.var.sem, self.var.at(i, self.nth))
        act.activation(self.rs, self.core.part(self.w, 2), ACT.Ln,
                       bias=self.core.epsc[:, self.eps:self.eps + 1]).then_inc(self.lnv.sem, 1)
        act.wait_ge(self.lnv.sem, self.lnv.at(i, self.nth))
        act.activation(self.rs, self.rs, ACT.Exp, scale=-0.5).then_inc(self.rstd.sem, 1)

    def dve_scale(self, dve, i):
        dve.wait_ge(self.rstd.sem, self.rstd.at(i, self.nth))
        rs = self.rs.unsqueeze(1).broadcast_to([P, C, N])
        dve.tensor_tensor(self.yc, self.yc, rs, ALU.mult).then_inc(self.nrm.sem, 1)

    def wait_scaled(self, eng, i):
        eng.wait_ge(self.nrm.sem, self.nrm.at(i, self.nth))


def project(pe, core, w, weight, src, k_chunks=C, m_chunks=C):
    for m in range(m_chunks):
        for k in range(k_chunks):
            mm = pe.matmul(core.part(w, m), weight[:, k, m * P:(m + 1) * P], src(k), start=k == 0,
                           stop=k == k_chunks - 1)
    return mm



def rwkv_memory(core):
    class M:
        pass

    m = M()
    r = Region(core.arena, core.own)
    m.W = {}
    start = r.at
    for n in ("r", "k", "v", "g", "o", "fr", "fk", "fv"):
        m.W[n] = r.take(C, D)
    m.w1 = r.take(C, 5 * DM)
    m.w2 = r.take(4, D)
    m.w2b = r.take(D)
    m.td1 = r.take(C, DD)
    m.td2 = r.take(D)
    m.vec = r.take(17, C)
    m.s0 = r.take(C, 16, B)
    m.wspan = (start, r.at)
    told = norm_signals(core, "rw")
    m.n1 = Norm(core, told, 0, 0, 0).memory(r)
    m.n2 = Norm(core, told, 1, 0, 0).memory(r)
    m.xs = r.take(C, NB, E)
    m.sx = r.take(C, N)
    m.xx = r.take(C, N)
    m.tha, m.thb = r.take(N), r.take(N)
    m.xm = [r.take(C, N) for _ in range(5)]
    m.r, m.k, m.v, m.g = (r.take(C, N) for _ in range(4))
    m.gt = m.n1.s2
    m.tdh = r.take(N)
    m.e1 = r.take(C, N)
    m.we = r.take(C, 4, NB * E)
    m.ring = [r.take(4, NB * E) for _ in range(4)]
    m.rk, m.bon, m.og, m.og2 = m.xx, m.xm[2], m.xm[0], m.xm[1]
    m.oc, m.osq, m.ors = m.n2.yc, m.n2.s2, m.n1.yc
    m.xs2 = r.take(C, NB, E)
    m.sx2, m.xk2, m.xr2, m.thr, m.ff, m.kk = m.sx, m.r, m.v, m.k, m.xm[3], m.xm[4]
    m.s = {}
    for name, per in dict(
            weights=16 * 8, decay_zeros=2, state1_in_xs=1, xa=4, shift=1, xa_shifted=4, mix_hidden_sum=1, mix_hidden=2, mix_sum=5, mix_term=20, mixed=5, r_sum=1, k_sum=1, v_sum=1,
            gate_sum=1, decay_hidden_sum=1, decay_sum=1, r=1, k=1, v=1, gate_tanh=1, gate=1, decay_hidden=1, decay_rate=4, decay=4, ruk=4, bonus_sum=1, bonus=1,
            v_spread=16, ring_start=16, kv=16, states=16, r_states=16, r_states_sum=16, head_out=1, head_mean=1, head_centred=1, head_squares=1, head_var=1, head_log_var=1, head_rstd=1,
            head_normed=1, head_affine=4, gated=1, out_sum=1, x1=1, state0_in_xs2=1, xc=4, shift2=1, ffn_mix=8, ffn_r_sum=1, ffn_k_sum=1, ffn_tanh=1, ffn_relu=1, ffn_squared=1,
            ffn_v_sum=1, ffn_gated=1, group_done=1).items():
        m.s[name] = core.new_signal("rw_" + name, per)
    return m


VEC = ["ln1_w", "ln1_b", "maa_x", "stack0", "stack1", "stack2", "stack3", "stack4", "time_decay", "u", "gn_w",
       "gn_b", "ln2_w", "ln2_b", "ffn_maa_k", "ffn_maa_r", "zero"]


def rwkv(core, m, name, base, after):
    X, part, wide, dram = core.X, core.part, core.wide, core.dram

    def vec(n, c):
        j = VEC.index(n)
        return m.vec[:, j, c:c + 1]

    def xg(g):
        return X[:, :, ds(g, N)]

    def xgc(g):
        return lambda c: X[:, c, ds(g, N)]

    def seq(v):
        return v.rearrange("p c (b t) -> p c b t", b=NB)

    def sync(sp):
        if after:
            sp.wait_ge(*after)
        w = core.arena[:, m.wspan[0]:m.wspan[1]]
        n = (m.wspan[1] - m.wspan[0])
        step = -(-n // 8)
        for q in range(8):
            a, b = q * step, min(n, (q + 1) * step)
            sp.dma_start(w[:, a:b], dram[name + "_w"][:, a:b]).then_inc(m.s["weights"].sem, 16)

    occ = base // G

    def weights_there(eng):
        eng.wait_ge(m.s["weights"].sem, m.s["weights"].at(occ + 1))

    def tensor(pe):
        weights_there(pe)
        with pe.Fori(0, G) as g:
            i = g + base
            pe.wait_ge(m.s["group_done"].sem, m.s["group_done"].at(i))
            m.n1.pe_mean(pe, xgc(g), i)
            m.n1.pe_var(pe, i)
            pe.wait_ge(m.s["xa_shifted"].sem, m.s["xa_shifted"].at(i, 4))
            for k in range(C):
                pe.matmul(part(1, 0), m.w1[:, k, 0:P], m.xx[:, k, :], start=k == 0, stop=k == C - 1)
            for k in range(C):
                mm = pe.matmul(part(1, 2, DM), m.w1[:, k, P:P + DM], m.xx[:, k, :], start=k == 0, stop=k == C - 1)
            mm.then_inc(m.s["mix_hidden_sum"].sem, 1)
            for f in range(5):
                if f == 0:
                    pe.wait_ge(m.s["mix_hidden"].sem, m.s["mix_hidden"].at(i, 2))
                if f >= 2:
                    pe.wait_ge(m.s["mix_term"].sem, m.s["mix_term"].at(i, 4 * (f - 1)))
                for c in range(C):
                    if f < 4:
                        mm = pe.matmul(part(2 + f % 2, c), m.w2[:, f, c * P:(c + 1) * P], m.tha, start=True, stop=True)
                    else:
                        mm = pe.matmul(part(2 + f % 2, c), m.w2b[0:DM, c * P:(c + 1) * P], m.thb[0:DM, :],
                                       start=True, stop=True)
                mm.then_inc(m.s["mix_sum"].sem, 1)
            pe.wait_ge(m.s["mixed"].sem, m.s["mixed"].at(i, 1))
            project(pe, core, 0, m.W["k"], lambda k: m.xm[0][:, k, :]).then_inc(m.s["k_sum"].sem, 1)
            pe.wait_ge(m.s["mixed"].sem, m.s["mixed"].at(i, 2))
            for k in range(C):
                mm = pe.matmul(part(1, 0, DD), m.td1[:, k, :], m.xm[1][:, k, :], start=k == 0, stop=k == C - 1)
            mm.then_inc(m.s["decay_hidden_sum"].sem, 1)
            pe.wait_ge(m.s["mixed"].sem, m.s["mixed"].at(i, 3))
            pe.wait_ge(m.s["mix_term"].sem, m.s["mix_term"].at(i, 20))
            project(pe, core, 2, m.W["v"], lambda k: m.xm[2][:, k, :]).then_inc(m.s["v_sum"].sem, 1)
            pe.wait_ge(m.s["decay_hidden"].sem, m.s["decay_hidden"].at(i, 1))
            for c in range(C):
                mm = pe.matmul(part(1, c), m.td2[0:DD, c * P:(c + 1) * P], m.tdh[0:DD, :], start=True, stop=True)
            mm.then_inc(m.s["decay_sum"].sem, 1)
            pe.wait_ge(m.s["mixed"].sem, m.s["mixed"].at(i, 4))
            project(pe, core, 3, m.W["r"], lambda k: m.xm[3][:, k, :]).then_inc(m.s["r_sum"].sem, 1)
            pe.wait_ge(m.s["mixed"].sem, m.s["mixed"].at(i, 5))
            pe.wait_ge(m.s["k"].sem, m.s["k"].at(i, 1))
            project(pe, core, 0, m.W["g"], lambda k: m.xm[4][:, k, :]).then_inc(m.s["gate_sum"].sem, 1)
            pe.wait_ge(m.s["ruk"].sem, m.s["ruk"].at(i, 4))
            pe.wait_ge(m.s["r"].sem, m.s["r"].at(i, 1))
            for c in range(C):
                mm = pe.matmul(part(3, c), core.heads_w, m.rk[:, c, :], start=True, stop=True)
            mm.then_inc(m.s["bonus_sum"].sem, 1)
            pe.wait_ge(m.s["v"].sem, m.s["v"].at(i, 1))
            pe.wait_ge(m.s["gate"].sem, m.s["gate"].at(i, 1))
            pe.wait_ge(m.s["decay_rate"].sem, m.s["decay_rate"].at(i, 4))
            pe.wait_ge(m.s["bonus"].sem, m.s["bonus"].at(i, 1))

            def reduce(n):
                c, q = n // 4, n % 4
                pe.wait_ge(m.s["r_states"].sem, m.s["r_states"].at(i, n + 1))
                rv = m.ring[n % 4].rearrange("p j (b e) -> p j b e", b=NB)
                for jt in range(4):
                    o = core.psum[32 * jt:32 * jt + 32, 6 + c // 2, (c % 2) * N:(c % 2) * N + N]
                    mm = pe.matmul(o, core.red_w[:, 24 - 8 * q:56 - 8 * q], rv[:, jt, :, 0:L],
                                   start=q == 0, stop=q == 3)
                mm.then_inc(m.s["r_states_sum"].sem, 1)

            for n in range(16 + 2):
                if n < 16:
                    c, q = n // 4, n % 4
                    if n >= 3:
                        pe.wait_ge(m.s["kv"].sem, m.s["kv"].at(i, n - 2))
                    for jt in range(4):
                        j = 4 * jt + q
                        sel = core.spread_w[:, j, :]
                        mm = pe.matmul(part(n % 3, jt), sel, m.v[:, c, :], start=True, stop=True)
                    mm.then_inc(m.s["v_spread"].sem, 1)
                if n >= 2:
                    reduce(n - 2)
            pe.wait_ge(m.s["head_out"].sem, m.s["head_out"].at(i, 1))
            for c in range(C):
                mm = pe.matmul(part(0, c), core.gmean_w, m.og[:, c, :], start=True, stop=True)
            mm.then_inc(m.s["head_mean"].sem, 1)
            pe.wait_ge(m.s["head_squares"].sem, m.s["head_squares"].at(i, 1))
            for c in range(C):
                mm = pe.matmul(part(1, c), core.gmean_w, m.osq[:, c, :], start=True, stop=True)
            mm.then_inc(m.s["head_var"].sem, 1)
            pe.wait_ge(m.s["gated"].sem, m.s["gated"].at(i, 1))
            project(pe, core, 2, m.W["o"], lambda k: m.og2[:, k, :]).then_inc(m.s["out_sum"].sem, 1)
            pe.wait_ge(m.s["x1"].sem, m.s["x1"].at(i, 1))
            m.n2.pe_mean(pe, xgc(g), i)
            m.n2.pe_var(pe, i)
            pe.wait_ge(m.s["ffn_mix"].sem, m.s["ffn_mix"].at(i, 4))
            project(pe, core, 2, m.W["fk"], lambda k: m.xk2[:, k, :]).then_inc(m.s["ffn_k_sum"].sem, 1)
            pe.wait_ge(m.s["ffn_mix"].sem, m.s["ffn_mix"].at(i, 8))
            project(pe, core, 1, m.W["fr"], lambda k: m.xr2[:, k, :]).then_inc(m.s["ffn_r_sum"].sem, 1)
            pe.wait_ge(m.s["ffn_squared"].sem, m.s["ffn_squared"].at(i, 1))
            project(pe, core, 3, m.W["fv"], lambda k: m.kk[:, k, :]).then_inc(m.s["ffn_v_sum"].sem, 1)

    def vector(dve):
        weights_there(dve)
        dve.memset(m.we.rearrange("p c j (b e) -> p (c j b) e", b=NB)[:, :, 0:1], 0.0).then_inc(m.s["decay_zeros"].sem, 2)
        with dve.Fori(0, G) as g:
            i = g + base
            s1 = core.st[:, :, 1, ds(g, NB)]
            s0 = core.st[:, :, 0, ds(g, NB)]
            m.n1.dve_center(dve, xg(g), i)
            dve.wait_ge(m.s["ffn_gated"].sem, m.s["ffn_gated"].at(i))
            dve.tensor_copy(m.xs[:, :, :, 0], s1).then_inc(m.s["state1_in_xs"].sem, 1)
            m.n1.dve_scale(dve, i)
            dve.wait_ge(m.s["state1_in_xs"].sem, m.s["state1_in_xs"].at(i, 1))
            dve.wait_ge(m.s["xa"].sem, m.s["xa"].at(i, 4))
            dve.tensor_tensor(seq(m.sx), m.xs[:, :, :, 0:L], m.xs[:, :, :, 1:E], ALU.subtract).then_inc(m.s["shift"].sem, 1)
            dve.wait_ge(m.s["shift"].sem, m.s["shift"].at(i, 1))
            for c in range(C):
                dve.scalar_tensor_tensor(seq(m.xx)[:, c], seq(m.sx)[:, c], vec("maa_x", c), m.xs[:, c, :, 1:E],
                                         ALU.mult, ALU.add).then_inc(m.s["xa_shifted"].sem, 1)
            for f in range(5):
                dve.wait_ge(m.s["mix_sum"].sem, m.s["mix_sum"].at(i, f + 1))
                for c in range(C):
                    dve.scalar_tensor_tensor(m.xm[f][:, c, :], part(2 + f % 2, c), vec(f"stack{f}", c), m.sx[:, c, :],
                                             ALU.add, ALU.mult).then_inc(m.s["mix_term"].sem, 1)
            dve.wait_ge(m.s["k_sum"].sem, m.s["k_sum"].at(i, 1))
            dve.tensor_copy(two(m.k), wide[0]).then_inc(m.s["k"].sem, 1)
            dve.wait_ge(m.s["r_sum"].sem, m.s["r_sum"].at(i, 1))
            dve.tensor_copy(two(m.r), wide[3]).then_inc(m.s["r"].sem, 1)
            dve.wait_ge(m.s["k"].sem, m.s["k"].at(i, 1))
            dve.wait_ge(m.s["r"].sem, m.s["r"].at(i, 1))
            for c in range(C):
                dve.scalar_tensor_tensor(m.rk[:, c, :], m.r[:, c, :], vec("u", c), m.k[:, c, :],
                                         ALU.mult, ALU.mult).then_inc(m.s["ruk"].sem, 1)
            dve.wait_ge(m.s["v"].sem, m.s["v"].at(i, 1))
            dve.wait_ge(m.s["bonus_sum"].sem, m.s["bonus_sum"].at(i, 1))
            dve.tensor_tensor(two(m.bon), wide[3], two(m.v), ALU.mult).then_inc(m.s["bonus"].sem, 1)
            dve.wait_ge(m.s["gate_tanh"].sem, m.s["gate_tanh"].at(i, 1))
            dve.scalar_tensor_tensor(two(m.g), two(m.gt), 1.0, wide[0], ALU.add, ALU.mult).then_inc(m.s["gate"].sem, 1)

            for n in range(16):
                c, q = n // 4, n % 4
                av = m.ring[n % 4].rearrange("p j (b e) -> p j b e", b=NB)
                if n >= 4:
                    dve.wait_ge(m.s["r_states_sum"].sem, m.s["r_states_sum"].at(i, n - 3))
                st0 = m.s0[:, c, q:16:4, ds(g, NB)]
                dve.tensor_copy(av[:, :, :, 0], st0).then_inc(m.s["ring_start"].sem, 1)
                dve.wait_ge(m.s["v_spread"].sem, m.s["v_spread"].at(i, n + 1))
                w = n % 3
                for h in range(2):
                    kb = m.k[:, c, :].rearrange("p (b t) -> p b t", b=NB).unsqueeze(1).broadcast_to([P, 2, NB, L])
                    vb = core.psum[:, 2 * w + h, 0:2 * N].rearrange("p (j b t) -> p j b t", j=2, b=NB)
                    ins = dve.tensor_tensor(av[:, 2 * h:2 * h + 2, :, 1:E], kb, vb, ALU.mult)
                    if h == 1:
                        ins.then_inc(m.s["kv"].sem, 1)
                dve.wait_ge(m.s["kv"].sem, m.s["kv"].at(i, n + 1))
                dve.wait_ge(m.s["decay"].sem, m.s["decay"].at(i, c + 1))
                flat = m.ring[n % 4].rearrange("p j e -> p (j e)")
                dve.tensor_tensor_scan(flat, m.we[:, c].rearrange("p j e -> p (j e)"), flat, 0.0,
                                       ALU.mult, ALU.add).then_inc(m.s["states"].sem, 1)
            dve.wait_ge(m.s["r_states_sum"].sem, m.s["r_states_sum"].at(i, 16))
            dve.tensor_tensor(two(m.og), wide[3], two(m.bon), ALU.add).then_inc(m.s["head_out"].sem, 1)
            dve.wait_ge(m.s["head_out"].sem, m.s["head_out"].at(i, 1))
            dve.wait_ge(m.s["head_mean"].sem, m.s["head_mean"].at(i, 1))
            dve.tensor_tensor(two(m.oc), two(m.og), wide[0], ALU.subtract).then_inc(m.s["head_centred"].sem, 1)
            dve.wait_ge(m.s["head_rstd"].sem, m.s["head_rstd"].at(i, 1))
            dve.tensor_tensor(m.oc, m.oc, m.ors, ALU.mult).then_inc(m.s["head_normed"].sem, 1)
            dve.wait_ge(m.s["head_affine"].sem, m.s["head_affine"].at(i, 4))
            dve.scalar_tensor_tensor(m.og2, m.oc, 0.5, m.g, ALU.mult, ALU.mult).then_inc(m.s["gated"].sem, 1)
            dve.wait_ge(m.s["out_sum"].sem, m.s["out_sum"].at(i, 1))
            dve.tensor_tensor(xg(g), pall4(core, 2), xg(g), ALU.add).then_inc(m.s["x1"].sem, 1)
            dve.wait_ge(m.s["x1"].sem, m.s["x1"].at(i, 1))
            m.n2.dve_center(dve, xg(g), i)
            dve.tensor_copy(m.xs2[:, :, :, 0], s0).then_inc(m.s["state0_in_xs2"].sem, 1)
            m.n2.dve_scale(dve, i)
            dve.wait_ge(m.s["state0_in_xs2"].sem, m.s["state0_in_xs2"].at(i, 1))
            dve.wait_ge(m.s["xc"].sem, m.s["xc"].at(i, 4))
            dve.tensor_tensor(seq(m.sx2), m.xs2[:, :, :, 0:L], m.xs2[:, :, :, 1:E],
                              ALU.subtract).then_inc(m.s["shift2"].sem, 1)
            dve.wait_ge(m.s["shift2"].sem, m.s["shift2"].at(i, 1))
            for v, n in ((m.xk2, "ffn_maa_k"), (m.xr2, "ffn_maa_r")):
                for c in range(C):
                    dve.scalar_tensor_tensor(seq(v)[:, c], seq(m.sx2)[:, c], vec(n, c), m.xs2[:, c, :, 1:E],
                                             ALU.mult, ALU.add).then_inc(m.s["ffn_mix"].sem, 1)
            dve.wait_ge(m.s["ffn_relu"].sem, m.s["ffn_relu"].at(i, 1))
            dve.tensor_tensor(m.kk, m.ff, m.ff, ALU.mult).then_inc(m.s["ffn_squared"].sem, 1)
            dve.wait_ge(m.s["ffn_squared"].sem, m.s["ffn_squared"].at(i, 1))
            dve.wait_ge(m.s["ffn_tanh"].sem, m.s["ffn_tanh"].at(i, 1))
            dve.wait_ge(m.s["ffn_v_sum"].sem, m.s["ffn_v_sum"].at(i, 1))
            dve.scalar_tensor_tensor(two(m.ff), two(m.thr), 1.0, wide[3], ALU.add, ALU.mult).then_inc(m.s["ffn_gated"].sem, 1)
            dve.wait_ge(m.s["ffn_gated"].sem, m.s["ffn_gated"].at(i, 1))
            dve.scalar_tensor_tensor(xg(g), m.ff, 0.5, xg(g), ALU.mult, ALU.add).then_inc(m.s["group_done"].sem, 1)

    def scalar(act):
        weights_there(act)
        with act.Fori(0, G) as g:
            i = g + base
            m.n1.act_square(act, i)
            m.n1.act_rstd(act, i)
            m.n1.wait_scaled(act, i)
            for c in range(C):
                act.activation(m.xs[:, c, :, 1:E], seq(m.n1.yc)[:, c], ACT.Identity, bias=vec("ln1_b", c),
                               scale=vec("ln1_w", c)).then_inc(m.s["xa"].sem, 1)
            act.wait_ge(m.s["mix_hidden_sum"].sem, m.s["mix_hidden_sum"].at(i, 1))
            act.activation(m.tha, part(1, 0), ACT.Tanh).then_inc(m.s["mix_hidden"].sem, 1)
            act.activation(m.thb[0:DM, :], part(1, 2, DM), ACT.Tanh).then_inc(m.s["mix_hidden"].sem, 1)
            act.wait_ge(m.s["decay_hidden_sum"].sem, m.s["decay_hidden_sum"].at(i, 1))
            act.activation(m.tdh[0:DD, :], part(1, 0, DD), ACT.Tanh).then_inc(m.s["decay_hidden"].sem, 1)
            act.wait_ge(m.s["v_sum"].sem, m.s["v_sum"].at(i, 1))
            act.activation(two(m.v), wide[2], ACT.Copy).then_inc(m.s["v"].sem, 1)
            act.wait_ge(m.s["decay_sum"].sem, m.s["decay_sum"].at(i, 1))
            for c in range(C):
                act.activation(m.e1[:, c, :], part(1, c), ACT.Exp, bias=vec("time_decay", c)).then_inc(m.s["decay_rate"].sem, 1)
            act.wait_ge(m.s["decay_zeros"].sem, m.s["decay_zeros"].at(occ + 1))
            for c in range(C):
                act.wait_ge(m.s["decay_rate"].sem, m.s["decay_rate"].at(i, c + 1))
                src = m.e1[:, c, :].rearrange("p (b t) -> p b t", b=NB).unsqueeze(1).broadcast_to([P, 4, NB, L])
                dst = m.we[:, c].rearrange("p j (b e) -> p j b e", b=NB)[:, :, :, 1:E]
                for j in range(0, 4):
                    ins = act.activation(dst[:, j], src[:, j], ACT.Exp, scale=-1.0)
                ins.then_inc(m.s["decay"].sem, 1)
            act.wait_ge(m.s["gate_sum"].sem, m.s["gate_sum"].at(i, 1))
            act.activation(two(m.gt), wide[0], ACT.Tanh, scale=0.5).then_inc(m.s["gate_tanh"].sem, 1)
            act.wait_ge(m.s["head_centred"].sem, m.s["head_centred"].at(i, 1))
            act.activation(m.osq, m.oc, ACT.Square).then_inc(m.s["head_squares"].sem, 1)
            act.wait_ge(m.s["head_var"].sem, m.s["head_var"].at(i, 1))
            act.activation(two(m.ors), wide[1], ACT.Ln, bias=core.epsc[:, 0:1]).then_inc(m.s["head_log_var"].sem, 1)
            act.wait_ge(m.s["head_log_var"].sem, m.s["head_log_var"].at(i, 1))
            act.activation(m.ors, m.ors, ACT.Exp, scale=-0.5).then_inc(m.s["head_rstd"].sem, 1)
            act.wait_ge(m.s["head_normed"].sem, m.s["head_normed"].at(i, 1))
            for c in range(C):
                act.activation(m.oc[:, c, :], m.oc[:, c, :], ACT.Identity, bias=vec("gn_b", c),
                               scale=vec("gn_w", c)).then_inc(m.s["head_affine"].sem, 1)
            m.n2.act_square(act, i)
            m.n2.act_rstd(act, i)
            m.n2.wait_scaled(act, i)
            for c in range(C):
                act.activation(m.xs2[:, c, :, 1:E], seq(m.n2.yc)[:, c], ACT.Identity, bias=vec("ln2_b", c),
                               scale=vec("ln2_w", c)).then_inc(m.s["xc"].sem, 1)
            act.wait_ge(m.s["ffn_k_sum"].sem, m.s["ffn_k_sum"].at(i, 1))
            act.activation(two(m.ff), wide[2], ACT.Relu).then_inc(m.s["ffn_relu"].sem, 1)
            act.wait_ge(m.s["ffn_r_sum"].sem, m.s["ffn_r_sum"].at(i, 1))
            act.activation(two(m.thr), wide[1], ACT.Tanh, scale=0.5).then_inc(m.s["ffn_tanh"].sem, 1)

    def gpsimd(pool):
        with pool.Fori(0, G) as g:
            i = g + base
            for f in range(5):
                pool.wait_ge(m.s["mix_term"].sem, m.s["mix_term"].at(i, 4 * f + 4))
                pool.tensor_tensor(seq(m.xm[f]), seq(m.xm[f]), m.xs[:, :, :, 1:E], ALU.add).then_inc(m.s["mixed"].sem, 1)
            pool.wait_ge(m.s["r"].sem, m.s["r"].at(i, 1))
            for n in range(16):
                c = n // 4
                sv = m.ring[n % 4].rearrange("p j (b e) -> p j b e", b=NB)[:, :, :, 0:L]
                rb = m.r[:, c, :].rearrange("p (b t) -> p b t", b=NB).unsqueeze(1).broadcast_to([P, 4, NB, L])
                pool.wait_ge(m.s["states"].sem, m.s["states"].at(i, n + 1))
                pool.tensor_tensor(sv, sv, rb, ALU.mult).then_inc(m.s["r_states"].sem, 1)

    return Layer(sync, tensor, vector, scalar, gpsimd, (m.s["group_done"].sem, m.s["group_done"].at(base + G)))


def pall4(core, w):
    return core.psum[:, 2 * w:2 * w + 2, 0:2 * N].rearrange("p a (b n) -> p a b n", b=2)


def attention(core, name, after):
    X, part, dram, bank, ident = core.X, core.part, core.dram, core.bank, core.ident
    s = lambda n, per=1: core.new_signal(name + "_" + n, per)
    gqa = name == "L0"
    KC = 1 if gqa else C
    KV = KC * P
    NBLK = 8 if gqa else 4
    NB2 = 2 * NBLK
    NQ = 8 if gqa else 4
    TURNS = B // 2
    ORDER = (0, 2, 4, 6, 1, 3, 5, 7)
    scale = -1.0 / np.sqrt(D // (32 if gqa else 16))
    hm = core.hmask if gqa else core.qmask
    AVS = 4 if gqa else NB2

    r = Region(core.arena, core.own)
    w0 = r.at
    Wo = r.take(C, D)
    vec = r.take(26, C)
    w1 = r.at
    qT = r.take(C, T)
    told = norm_signals(core, name)
    norms = [Norm(core, told, u, u, 1 if gqa else 0).memory(r) for u in range(2)]
    behind = 0 if gqa else G // 2
    over = r.at
    Wq = r.take(C, D)
    Wk = r.take(C, KV)
    Wv = r.take(C, KV)
    w2 = r.at
    ctxt = [r.take(C, S) for _ in range(2)]
    kT = [r.take(KC, S) for _ in range(2)]
    raw = r.take(S)
    nmask = [r.take(S) for _ in range(2)]
    qm = [r.take(NQ, C, L) for _ in range(2)]
    vs = [r.take(3, NQ if gqa else 4, 32 if gqa else P) for _ in range(2)]
    sm = [r.take(S) for _ in range(3)]
    pr = [r.take(4, S) for _ in range(3)]
    pT = [r.take(3, 4, L) for _ in range(4)]
    nmx = r.take(4 * NB2)
    den = r.take(4 * NB2)
    rden = r.take(4 * NB2)
    carry = r.take(4 * NB2)
    if not gqa:
        r2 = Region(core.arena, over)
        fc = r2.take(C, F)
        pj = r2.take(F // P, D)
        hid = [r2.take(F // P, N) for _ in range(2)]
    if not gqa:
        masks = r.take(B * S // 4).bitcast(MASK)

    VN = (["bq", "bk", "bv", "bo", "gamma", "beta"] if gqa else
          ["ln1_w", "ln1_b", "q_b", "k_b", "v_b", "cproj_b", "ln2_w", "ln2_b", "proj_b"])

    def vec_(n, c):
        return vec[:, VN.index(n), c:c + 1]

    bq, bk, bv, bo = ("bq", "bk", "bv", "bo") if gqa else ("q_b", "k_b", "v_b", "cproj_b")
    gam, bet = ("gamma", "beta") if gqa else ("ln2_w", "ln2_b")

    weights = s("weights", 64)
    qp = s("qp", 2)
    qd = [s(f"qd{u}", 4) for u in range(2)]
    ctx_in = [s(f"ctx{u}", 16) for u in range(2)]
    mask_in = [s(f"mask{u}", 16) for u in range(2)] if gqa else s("mask", 16)
    nm, qmd = s("nm", 2), s("qm", 2 * NQ)
    kp, vp, kev = s("kp", 2 * KC), s("vp", 2 * 3), s("kev", 2 * KC)
    vev = s("vev", 2 * (4 if gqa else 3))
    if gqa:
        vzero = s("vzero", 2)
    else:
        wfc, wpj, yn, fcp, gel, pjp, fin = s("wfc", 64), s("wpj", 64), s("yn", 8), s("fcp", 8), s("gel", 32), s("pjp", 2), s("fin", 8)
    sc_, ttr, ex = s("scores", 4 * NB2), s("ttr", 4 * NB2), s("exp", 4 * NB2)
    rd, pn, tr, tea, ted = s("rd", NB2), s("pn", 4 * NB2), s("tr", NB2), s("tea", 2 * NB2), s("ted", NB2)
    av, oev = s("av", AVS), s("oev", 2 if gqa else 8)
    op, res, aff = s("op", 2), s("res", 8), s("aff", 8)
    OEV = 1 if gqa else 4
    VEV = 4 if gqa else 3
    pairs = G // 2

    def xg(j):
        return X[:, :, ds(j, N)]

    def spans(a, b, n):
        step = -(-(b - a) // n)
        return [(a + k * step, min(b, a + (k + 1) * step)) for k in range(n)]

    def sync(sp):
        if after:
            sp.wait_ge(*after)
        for at, (c, d) in ((0, (w0, w1)), (w1 - w0, (over, w2))):
            for a, b in spans(c, d, 2):
                sp.dma_start(core.arena[:, a:b], dram[name + "_w"][:, at + a - c:at + b - c]).then_inc(weights.sem, 16)
        if not gqa:
            sp.dma_start(masks[0:L], dram["mask2"].rearrange("b s -> (b s)").unsqueeze(0).broadcast_to([L, B * S])).then_inc(mask_in.sem, 16)
        with sp.Fori(0, TURNS) as t:
            for u in range(2):
                b = sp.snap(2 * t + u)
                sp.wait_ge(vp.sem, vp.at(t))
                sp.dma_start(ctxt[u], dram["ctxT"][bass.ds(b, 1)].rearrange("o p c s -> p (o c) s")).then_inc(ctx_in[u].sem, 16)
                if gqa:
                    sp.wait_ge(nm.sem, nm.at(t, u))
                    sp.dma_start(raw[0:L], dram["mask0"][bass.ds(b, 1)].rearrange("o l s -> (o l) s")).then_inc(mask_in[u].sem, 16)
        if not gqa:
            sp.wait_ge(oev.sem, oev.at(TURNS))
            for v, n, done in ((fc, "L2_fc", wfc), (pj, "L2_pj", wpj)):
                src = dram[n].rearrange("p (a b) -> p a b", b=v.shape[2])
                q = v.shape[1] // 4
                for j in range(4):
                    sp.dma_start(v[:, q * j:q * j + q], src[:, q * j:q * j + q]).then_inc(done.sem, 16)

    def tensor(pe):
        pe.wait_ge(weights.sem, weights.at(1))
        with pe.Fori(0, pairs) as t:
            if not gqa:
                for u in range(2):
                    pe.wait_ge(norms[u].nrm.sem, norms[u].nrm.at(t))
                    norms[u].pe_mean(pe, lambda c: X[:, c, bass.ds(t * (2 * N) + u * N, N)], t)
                for u in range(2):
                    norms[u].pe_var(pe, t)
            for u in range(2):
                pe.wait_ge(qd[u].sem, qd[u].at(t))
                if gqa:
                    src = lambda k: X[:, k, bass.ds(t * (2 * N) + u * N, N)]
                else:
                    pe.wait_ge(yn.sem, yn.at(t, 4 * u + 4))
                    src = lambda k: norms[u].yc[:, k, :]
                project(pe, core, 2 + u, Wq, src).then_inc(qp.sem, 1)
        for u in range(2):
            pe.wait_ge(qd[u].sem, qd[u].at(pairs))

        def keys_values(t, u):
            pe.wait_ge(ctx_in[u].sem, ctx_in[u].at(t, 16))
            for c in range(KC):
                if c >= 2:
                    pe.wait_ge(kev.sem, kev.at(t, u * KC + c - 1))
                elif u == 0:
                    pe.wait_ge(vev.sem, vev.at(t))
                else:
                    pe.wait_ge(vev.sem, vev.at(t, VEV))
                for k in range(C):
                    mm = pe.matmul(bank[6 + c % 2][:, 0:S], Wk[:, k, c * P:(c + 1) * P], ctxt[u][:, k, :],
                                   start=k == 0, stop=k == C - 1)
                mm.then_inc(kp.sem, 1)
            for j, (a, n) in enumerate(SC):
                if gqa:
                    o = bank[7][0:n, j * P:(j + 1) * P]
                    if j == 0:
                        pe.wait_ge(vev.sem, vev.at(t, u * VEV))
                else:
                    o = bank[6 + j % 2][0:n, :]
                    if j < 2:
                        pe.wait_ge(kev.sem, kev.at(t, u * KC + 3 + j))
                    else:
                        pe.wait_ge(vev.sem, vev.at(t, u * VEV + j - 1))
                for k in range(C):
                    mm = pe.matmul(o, ctxt[u][:, k, a:a + n], Wv[:, k, :], start=k == 0, stop=k == C - 1)
                mm.then_inc(vp.sem, 1)

        with pe.Fori(0, TURNS) as t:
            keys_values(t, 0)
            for n in range(NB2 + 3):
                if n < NB2:
                    u, nl = n // NBLK, n % NBLK
                    if nl == 0:
                        pe.wait_ge(qmd.sem, qmd.at(t, NQ * (u + 1)))
                        pe.wait_ge(kev.sem, kev.at(t, KC * (u + 1)))
                    for x in range(4):
                        k = 4 * n + x
                        if k >= 2:
                            pe.wait_ge(ttr.sem, ttr.at(t, k - 1))
                        q = qm[u][:, ORDER[nl], x, :] if gqa else qm[u][:, x, nl, :]
                        pe.matmul(bank[k % 2][0:L, 0:S], q, kT[u][:, 0 if gqa else nl, :], start=True,
                                  stop=True).then_inc(sc_.sem, 1)
                if n == 1:
                    keys_values(t, 1)
                m = n - 2
                if 0 <= m < NB2:
                    pe.wait_ge(pn.sem, pn.at(t, 4 * m + 4))
                    if m >= 1:
                        pe.wait_ge(tea.sem, tea.at(t, 2 * m))
                        pe.wait_ge(ted.sem, ted.at(t, m))
                    for j, (a, w) in enumerate(SC):
                        for x in range(4):
                            mm = pe.transpose(bank[2 + j][0:w, x * L:(x + 1) * L], pr[m % 3][0:L, x, a:a + w],
                                              ident[0:L, 0:L])
                    mm.then_inc(tr.sem, 1)
                m = n - 3
                if m < 0 or m >= NB2:
                    continue
                u, nl = m // NBLK, m % NBLK
                if gqa and nl % 4 != 3:
                    continue
                pe.wait_ge(tea.sem, tea.at(t, 2 * m + 2))
                pe.wait_ge(ted.sem, ted.at(t, m + 1))
                if nl == (3 if gqa else 0):
                    pe.wait_ge(vev.sem, vev.at(t, VEV * (u + 1)))
                    pe.wait_ge(oev.sem, oev.at(t, OEV * u))
                for j, (a, w) in enumerate(SC):
                    for x in range(4):
                        if gqa:
                            kv = ORDER[nl - 3 + x]
                            mm = pe.matmul(bank[5][32 * x:32 * x + 32, 0:4 * L], vs[u][0:w, j, kv, :],
                                           pT[(m - 3 + x) % 4][0:w, j].rearrange("p h l -> p (h l)"),
                                           start=nl == 3 and j == 0, stop=nl == 7 and j == 2)
                        else:
                            mm = pe.matmul(bank[5][32 * x:32 * x + 32, nl * L:(nl + 1) * L],
                                           vs[u][0:w, j, nl, 32 * x:32 * x + 32], pT[m % 4][0:w, j, x, :],
                                           start=j == 0, stop=j == 2)
                mm.then_inc(av.sem, 1)
        pe.wait_ge(oev.sem, oev.at(TURNS))
        with pe.Fori(0, pairs) as t:
            def xs(u):
                return lambda c: X[:, c, bass.ds(t * (2 * N) + u * N, N)]

            for u in range(2):
                if not gqa:
                    pe.wait_ge(gel.sem, gel.at(t))
                    pe.wait_ge(fin.sem, fin.at(t))
                pe.wait_ge(res.sem, res.at(t))
                project(pe, core, 2 + u, Wo, lambda k: qT[:, k, bass.ds(t * (2 * N) + u * N, N)]).then_inc(op.sem, 1)
            for u in range(2):
                pe.wait_ge(res.sem, res.at(t, 4 * u + 4))
                norms[u].pe_mean(pe, xs(u), t + behind)
            for u in range(2):
                norms[u].pe_var(pe, t + behind)
            if not gqa:
                for q in range(8):
                    u = q // 4
                    if q == 0:
                        pe.wait_ge(wfc.sem, wfc.at(1))
                        pe.wait_ge(gel.sem, gel.at(t))
                    if q % 4 == 0:
                        pe.wait_ge(aff.sem, aff.at(t, 4 * u + 4))
                    if q >= 2:
                        pe.wait_ge(gel.sem, gel.at(t, 4 * (q - 1)))
                    for m in range(4):
                        for k in range(C):
                            mm = pe.matmul(part(2 + q % 2, m), fc[:, k, ((q % 4) * 4 + m) * P:((q % 4) * 4 + m + 1) * P],
                                           norms[u].yc[:, k, :], start=k == 0, stop=k == C - 1)
                    mm.then_inc(fcp.sem, 1)
                pe.wait_ge(wpj.sem, wpj.at(1))
                for u in range(2):
                    pe.wait_ge(gel.sem, gel.at(t, 16 * (u + 1)))
                    project(pe, core, u, pj, lambda k: hid[u][:, k, :], k_chunks=F // P).then_inc(pjp.sem, 1)

    def vector(dve):
        dve.wait_ge(weights.sem, weights.at(1))
        for u in range(2):
            if gqa:
                dve.memset(vs[u], 0.0).then_inc(vzero.sem, 1)
        with dve.Fori(0, pairs) as t:
            if not gqa:
                for u in range(2):
                    dve.wait_ge(qp.sem, qp.at(t))
                    norms[u].dve_center(dve, X[:, :, bass.ds(t * (2 * N) + u * N, N)], t)
                for u in range(2):
                    norms[u].dve_scale(dve, t)
            for u in range(2):
                dve.wait_ge(qp.sem, qp.at(t, u + 1))
                for c in range(C):
                    dve.tensor_scalar(qT[:, c, bass.ds(t * (2 * N) + u * N, N)], part(2 + u, c), vec_(bq, c), scale,
                                      ALU.add, ALU.mult).then_inc(qd[u].sem, 1)
        with dve.Fori(0, TURNS) as t:
            def mask(u):
                if gqa:
                    dve.wait_ge(mask_in[u].sem, mask_in[u].at(t, 16))
                    dve.tensor_scalar(nmask[u][0:L], raw[0:L], -1.0, None, ALU.mult).then_inc(nm.sem, 1)
                else:
                    if u == 0:
                        dve.wait_ge(mask_in.sem, mask_in.at(1))
                    dve.tensor_scalar(nmask[u][0:L], masks[0:L, bass.ds(t * (2 * S) + u * S, S)], -FLT, FLT, ALU.mult, ALU.add).then_inc(nm.sem, 1)

            def values(u):
                if gqa:
                    if u == 0:
                        dve.wait_ge(vzero.sem, vzero.at(1))
                    for j0, j1, w in ((0, 2, P), (2, 3, SC[2][1])):
                        dve.wait_ge(vp.sem, vp.at(t, 3 * u + 3))
                        for odd in range(2):
                            src = bank[7][0:w, j0 * P:j1 * P].rearrange("p (j a o d) -> p j a o d", a=4, o=2, d=16)[:, :, :, odd]
                            dst = vs[u][0:w, j0:j1].rearrange("p j (a o) d -> p j a o d", o=2)[:, :, :, odd, 16 * odd:16 * odd + 16]
                            dve.tensor_copy(dst, src).then_inc(vev.sem, 1)
                else:
                    for j, (a, w) in enumerate(SC):
                        dve.wait_ge(vp.sem, vp.at(t, 3 * u + j + 1))
                        dve.tensor_copy(vs[u][0:w, j].rearrange("p a b -> p (a b)"), bank[6 + j % 2][0:w, :]).then_inc(vev.sem, 1)

            mask(0)
            mask(1)
            values(0)
            for n in range(NB2 + 4):
                if n < NB2:
                    u = n // NBLK
                    if n % NBLK == 0:
                        dve.wait_ge(nm.sem, nm.at(t, 2))
                    for x in range(4):
                        k = 4 * n + x
                        if k >= 3:
                            dve.wait_ge(ex.sem, ex.at(t, k - 2))
                        dve.wait_ge(sc_.sem, sc_.at(t, k + 1))
                        dve.memset(carry[0:1, k:k + 1], 0.0)
                        dve.tensor_tensor_reduce(out=sm[k % 3][0:L], in0=bank[k % 2][0:L, 0:S], in1=nmask[u][0:L],
                                                 scale=1.0, scalar=FLT, op0=ALU.add, op1=ALU.min,
                                                 accum_out=nmx[0:L, k:k + 1]).then_inc(ttr.sem, 1)
                if n == 1:
                    values(1)
                m = n - 1
                if 0 <= m < NB2:
                    dve.wait_ge(ex.sem, ex.at(t, 4 * m + 4))
                    dve.reciprocal(rden[0:L, 4 * m:4 * m + 4], den[0:L, 4 * m:4 * m + 4]).then_inc(rd.sem, 1)
                    dve.wait_ge(rd.sem, rd.at(t, m + 1))
                    for x in range(4):
                        p = pr[m % 3][0:L, x, :]
                        dve.tensor_scalar(p, p, rden[0:L, 4 * m + x:4 * m + x + 1], None, ALU.mult).then_inc(pn.sem, 1)
                m = n - 2
                if 0 <= m < NB2:
                    dve.wait_ge(tr.sem, tr.at(t, m + 1))
                    free_pt(dve, t, m)
                    w = SC[2][1]
                    dve.tensor_copy(pT[m % 4][0:w, 2].rearrange("p h l -> p (h l)"), bank[4][0:w, 0:4 * L]).then_inc(ted.sem, 1)
                m = n - 3
                if 0 <= m < NB2 and m % NBLK == NBLK - 1:
                    u = m // NBLK
                    dve.wait_ge(av.sem, av.at(t, AVS // 2 * (u + 1)))
                    o = bass.ds(t * (2 * L) + u * L, L)
                    if gqa:
                        dve.tensor_scalar(qT[:, :, o], bank[5][:, 0:4 * L].rearrange("p (h l) -> p h l", h=4),
                                          vec_(bv, 0), None, ALU.add).then_inc(oev.sem, 1)
                    else:
                        for c in range(C):
                            dve.tensor_scalar(qT[:, c, o], bank[5][:, c * L:(c + 1) * L], vec_(bv, c), None,
                                              ALU.add).then_inc(oev.sem, 1)
        with dve.Fori(0, pairs) as t:
            def xo(u):
                return bass.ds(t * (2 * N) + u * N, N)

            for u in range(2):
                dve.wait_ge(op.sem, op.at(t, u + 1))
                for c in range(C):
                    dve.scalar_tensor_tensor(X[:, c, xo(u)], part(2 + u, c), vec_(bo, c), X[:, c, xo(u)], ALU.add,
                                             ALU.add).then_inc(res.sem, 1)
            for u in range(2):
                dve.wait_ge(res.sem, res.at(t, 4 * u + 4))
                dve.wait_ge((aff if gqa else fcp).sem, (aff if gqa else fcp).at(t))
                norms[u].dve_center(dve, X[:, :, xo(u)], t + behind)
            for u in range(2):
                norms[u].dve_scale(dve, t + behind)
            if not gqa:
                for u in range(2):
                    dve.wait_ge(pjp.sem, pjp.at(t, u + 1))
                    for c in range(C):
                        dve.scalar_tensor_tensor(X[:, c, xo(u)], part(u, c), vec_("proj_b", c), X[:, c, xo(u)],
                                                 ALU.add, ALU.add).then_inc(fin.sem, 1)

    def free_pt(eng, t, m):
        if m >= 4:
            eng.wait_ge(av.sem, av.at(t, m // 4 if gqa else m - 3))

    def scalar(act):
        act.wait_ge(weights.sem, weights.at(1))
        if not gqa:
            with act.Fori(0, pairs) as t:
                for u in range(2):
                    norms[u].act_square(act, t)
                for u in range(2):
                    norms[u].act_rstd(act, t)
                for u in range(2):
                    norms[u].wait_scaled(act, t)
                    for c in range(C):
                        y = norms[u].yc[:, c, :]
                        act.activation(y, y, ACT.Identity, bias=vec_("ln1_b", c),
                                       scale=vec_("ln1_w", c)).then_inc(yn.sem, 1)
        with act.Fori(0, TURNS) as t:
            def keys(u):
                for c in range(KC):
                    act.wait_ge(kp.sem, kp.at(t, KC * u + c + 1))
                    act.activation(kT[u][:, c, :], bank[6 + c % 2][:, 0:S], ACT.Identity,
                                   bias=vec_(bk, c)).then_inc(kev.sem, 1)

            keys(0)
            for n in range(NB2 + 2):
                if n < NB2:
                    for x in range(4):
                        k = 4 * n + x
                        act.wait_ge(ttr.sem, ttr.at(t, k + 1))
                        if x == 0 and n >= 3:
                            act.wait_ge(tr.sem, tr.at(t, n - 2))
                        act.activation(pr[n % 3][0:L, x, :], sm[k % 3][0:L], ACT.Exp, bias=nmx[0:L, k:k + 1],
                                       scale=-1.0, accum_out=den[0:L, k:k + 1]).then_inc(ex.sem, 1)
                if n == 1:
                    keys(1)
                m = n - 2
                if 0 <= m < NB2:
                    act.wait_ge(tr.sem, tr.at(t, m + 1))
                    free_pt(act, t, m)
                    for j in range(2):
                        act.activation(pT[m % 4][:, j].rearrange("p h l -> p (h l)"), bank[2 + j][:, 0:4 * L],
                                       ACT.Copy).then_inc(tea.sem, 1)
        with act.Fori(0, pairs) as t:
            for u in range(2):
                norms[u].act_square(act, t + behind)
            for u in range(2):
                norms[u].act_rstd(act, t + behind)
            for u in range(2):
                norms[u].wait_scaled(act, t + behind)
                for c in range(C):
                    y = norms[u].yc[:, c, :]
                    o = X[:, c, bass.ds(t * (2 * N) + u * N, N)] if gqa else y
                    act.activation(o, y, ACT.Identity, bias=vec_(bet, c), scale=vec_(gam, c)).then_inc(aff.sem, 1)
            if not gqa:
                for q in range(8):
                    act.wait_ge(fcp.sem, fcp.at(t, q + 1))
                    for m in range(4):
                        j = (q % 4) * 4 + m
                        act.activation(hid[q // 4][:, j, :], part(2 + q % 2, m), GELU,
                                       bias=vec[:, 9 + j // 4, j % 4:j % 4 + 1]).then_inc(gel.sem, 1)

    def gpsimd(pool):
        for u in range(2):
            pool.wait_ge(qd[u].sem, qd[u].at(pairs))
        with pool.Fori(0, TURNS) as t:
            pool.wait_ge(sc_.sem, sc_.at(t))
            for u in range(2):
                for h in range(NQ):
                    pool.tensor_tensor(qm[u][:, h], qT[:, :, bass.ds(t * (2 * L) + u * L, L)],
                                       hm[:, h:h + 1].unsqueeze(2).broadcast_to([P, C, L]), ALU.mult).then_inc(qmd.sem, 1)

    last = aff if gqa else fin
    return Layer(sync, tensor, vector, scalar, gpsimd, (last.sem, last.at(pairs)))



def cols(v):
    return np.ascontiguousarray(v.reshape(C, P).T)


def rows(w):
    return w.reshape(-1, P, w.shape[1]).transpose(1, 0, 2)


PERM = np.arange(D).reshape(C, HC, HS).transpose(0, 2, 1).reshape(-1)


def pack(parts):
    outs = []
    for a in parts:
        a = a.reshape(a.shape[0], -1)
        n = -(-a.shape[1] // 8) * 8
        b = np.zeros((P, n), np.float32)
        b[:a.shape[0], :a.shape[1]] = a
        outs.append(b)
    return np.concatenate(outs, 1)


def rwkv_weights(d, n, ctx):
    w = {k[len(f"L{n}_xattn_"):]: v for k, v in d.items() if k.startswith(f"L{n}_xattn_")}
    parts = [rows(w["Wr"].T), rows(w["Wk"].T), rows(w["Wv"].T[:, PERM]), rows(w["Wg"].T[:, PERM]),
             rows(w["Wo"].T[PERM]), rows(w["Wfr"].T), rows(w["Wfk"].T), rows(w["Wfv"].T), rows(w["maa_w1"])]
    w2 = np.zeros((P, 4, D), np.float32)
    for f in range(4):
        w2[DM * f:DM * f + DM, f] = w["maa_w2"][f]
    parts += [w2, w["maa_w2"][4], rows(w["td_w1"]), w["td_w2"]]
    u = np.broadcast_to(w["u"].reshape(-1), (D,))
    table = {"ln1_w": w["ln1_w"], "ln1_b": w["ln1_b"], "maa_x": w["maa_x"], "time_decay": w["time_decay"], "u": u,
             "gn_w": w["gn_w"][PERM], "gn_b": w["gn_b"][PERM], "ln2_w": w["ln2_w"], "ln2_b": w["ln2_b"],
             "ffn_maa_k": w["ffn_maa_k"], "ffn_maa_r": w["ffn_maa_r"], "zero": np.zeros(D, np.float32)}
    for f in range(5):
        table[f"stack{f}"] = w["maa_stack"].reshape(5, D)[f]
    parts.append(np.stack([cols(table[k]) for k in VEC], 1))
    s0 = ctx[:, 2:2 + HS].reshape(B, C, P, HS)
    parts.append(s0.transpose(2, 1, 3, 0))
    return pack(parts)


def constants(ctx):
    p = np.arange(P)
    ident = np.eye(P, dtype=np.float32)
    mean_w = np.full((P, P), 1 / D, np.float32)
    gmean = (p[:, None] % HC == p[None, :] % HC).astype(np.float32) / HS
    heads = (p[:, None] // HS == p[None, :] % HC).astype(np.float32)
    red = np.zeros((P, 56), np.float32)
    red[p, 24 + p // HS] = 1
    spread = np.zeros((P, HS, P), np.float32)
    for j in range(HS):
        spread[:, j] = p[:, None] == HC * j + p[None] // HS
    hm = (p[:, None] // 16 == np.arange(8)[None]).astype(np.float32)
    qm = (p[:, None] // 32 == np.arange(4)[None]).astype(np.float32)
    eps = np.broadcast_to(np.array([1e-5, 1e-6], np.float32), (P, 2))
    st = ctx[:, 0:2].reshape(B, 2, C, P).transpose(3, 2, 1, 0)
    return pack([ident, mean_w, gmean, heads, red, spread, hm, qm, eps, st])


def attention_weights(w, names, q_perm, o_perm, vectors, fc_b=None):
    q, k, v, o = (w[n] for n in names)
    vec = np.zeros((P, 26, C), np.float32)
    for j, b in enumerate(vectors):
        c = b.reshape(-1, P).T
        vec[:, j, :c.shape[1]] = c
    if fc_b is not None:
        vec[:, 9:13] = fc_b.reshape(C, C, P).transpose(2, 0, 1)
    return pack([rows(o[o_perm]), vec, rows(q[:, q_perm]), rows(k), rows(v)])


GQA = np.arange(D).reshape(8, 4, 16).transpose(1, 0, 2).reshape(-1)


def lay_out(inputs):
    d = {k: np.asarray(v) for k, v in inputs.items()}
    ctx = d["ctx_2048"]
    w0 = {k[9:]: v for k, v in d.items() if k.startswith("L0_xattn_")}
    w2 = {k[9:]: v for k, v in d.items() if k.startswith("L2_xattn_")}
    same = np.arange(D)
    return {
        "ctxT": np.ascontiguousarray(ctx.reshape(B, S, C, P).transpose(0, 3, 2, 1)),
        "mask0": np.ascontiguousarray(d["mask_Bx1xSxS2_ff0"].reshape(B, L, S)),
        "mask2": np.ascontiguousarray(d["mask_BxS2_bf1"]),
        "L0_w": attention_weights(w0, ("Wq", "Wk", "Wv", "Wo"), GQA, GQA,
                                  [w0["bq"][GQA], w0["bk"], w0["bv"], w0["bo"], w0["gamma"], w0["beta"]]),
        "L2_w": attention_weights(w2, ("q_w", "k_w", "v_w", "cproj_w"), same, same,
                                  [w2[n] for n in ("ln1_w", "ln1_b", "q_b", "k_b", "v_b", "cproj_b", "ln2_w", "ln2_b",
                                                   "proj_b")], w2["fc_b"]),
        "L2_fc": pack([rows(w2["fc_w"])]),
        "L2_pj": pack([rows(w2["proj_w"])]),
        "xT": np.ascontiguousarray(d["x"].reshape(T, C, P).transpose(2, 1, 0)).reshape(P, C * T),
        "const": constants(ctx),
        "L1_w": rwkv_weights(d, 1, ctx),
        "L3_w": rwkv_weights(d, 3, ctx),
    }


LAYERS = (0, 1, 2, 3)


def kernel(**inputs):
    import concourse.bacc as _bacc
    from concourse.bass_utils import run_bass_kernel_spmd as _run

    nc = _bacc.Bacc("TRN2", target_bir_lowering=False, num_devices=1)
    arrays = lay_out(inputs)
    dram = {n: nc.dram_tensor(n, a.shape, mybir.dt.from_np(a.dtype), kind="ExternalInput").ap()
            for n, a in arrays.items()}
    out = nc.dram_tensor("outT", [P, C * T], F32, kind="ExternalOutput").ap()
    program(nc, dram, out, LAYERS)
    r = _run(nc, [arrays], core_ids=[0])
    got = np.asarray(r.results[0]["outT"])
    return np.ascontiguousarray(got.reshape(P, C, T).transpose(2, 1, 0)).reshape(B, L, D)
```

```python
from contextlib import ExitStack

import numpy as np

import concourse.bass as bass
from concourse import mybir

F32 = mybir.dt.float32
F32R = mybir.dt.float32r
MASK = mybir.dt.from_np(np.dtype(bool))
ALU = mybir.AluOpType
ACT = mybir.ActivationFunctionType

B, L, S, D = 16, 100, 361, 512
P = 128
C = D // P
T = B * L
NB = 2
N = NB * L
G = B // NB
E = L + 1
HS = 16
HC = P // HS
DM, DD = 32, 64
F = 2048
SC = [(0, 128), (128, 128), (256, S - 256)]
FLT = float(np.finfo(np.float32).max)
ARENA = 49552
GELU = ACT.Gelu_apprx_tanh


class Signal:

    def __init__(self, sem, per):
        self.sem, self.per = sem, per

    def at(self, i, n=0):
        return i * self.per + n + 1


def ds(i, n):
    return bass.ds(i * n, n)


class Region:

    def __init__(self, arena, start):
        self.arena, self.at = arena, start

    def take(self, *shape):
        n = int(np.prod(shape))
        v = self.arena[:, self.at:self.at + n]
        self.at += (n + 7) // 8 * 8
        assert self.at <= ARENA, self.at
        if len(shape) == 2:
            v = v.rearrange("p (a b) -> p a b", a=shape[0])
        elif len(shape) == 3:
            v = v.rearrange("p (a b c) -> p a b c", a=shape[0], b=shape[1])
        elif len(shape) == 4:
            v = v.rearrange("p (a b c d) -> p a b c d", a=shape[0], b=shape[1], c=shape[2])
        return v


class Core:

    def __init__(self, nc, ctx, dram):
        self.nc, self.ctx, self.dram, self.signals = nc, ctx, dram, []
        self.arena = ctx.enter_context(nc.sbuf_tensor("arena", [P, ARENA], F32))
        r = Region(self.arena, 0)
        self.X = r.take(C, T)
        self.ident = r.take(P)
        self.mean_w = r.take(P)
        self.gmean_w = r.take(P)
        self.heads_w = r.take(P)
        self.red_w = r.take(56)
        self.hmask = r.take(8)
        self.qmask = r.take(4)
        self.epsc = r.take(2)
        self.st = r.take(C, 2, B)
        self.own = r.at
        self.psum = ctx.enter_context(nc.psum_tensor("psum", [P, 8, 512], F32))
        self.bank = [self.psum[:, i, :] for i in range(8)]
        self.wide = [self.psum[:, 2 * i:2 * i + 2, 0:2 * N] for i in range(4)]
        self.loaded = self.new_signal("loaded", 32)
        self.stored = self.new_signal("stored", 16)

    def new_signal(self, name, per=1):
        self.signals.append(Signal(self.ctx.enter_context(self.nc.semaphore(name)), per))
        return self.signals[-1]

    def part(self, w, m, rows=P):
        return self.psum[0:rows, 2 * w + m // 2, (m % 2) * N:(m % 2) * N + N]

    def load(self, sp):
        sp.dma_start(self.arena[:, 0:C * T], self.dram["xT"]).then_inc(self.loaded.sem, 16)
        sp.dma_start(self.arena[:, C * T:self.own], self.dram["const"]).then_inc(self.loaded.sem, 16)

    def lead(self, sp):
        for s in self.signals:
            sp.sem_inc(s.sem, 1)

    def wait_loaded(self, eng):
        eng.wait_ge(self.loaded.sem, self.loaded.at(1))


class Layer:

    def __init__(self, sync, tensor, vector, scalar, gpsimd, done):
        self.sync, self.tensor, self.vector, self.scalar, self.gpsimd = sync, tensor, vector, scalar, gpsimd
        self.done = done


def two(v):
    return v.rearrange("p (a b) n -> p a (b n)", a=2)


def program(nc, dram, out_dram, layers=(0, 1, 2, 3)):
    with ExitStack() as ctx:
        core = Core(nc, ctx, dram)
        shared = RwkvMemory(core)
        stack, after = [], None
        for n in layers:
            if n % 2 == 0:
                stack.append(attention(core, f"L{n}", after))
            else:
                stack.append(rwkv(core, shared, f"L{n}", 0 if n == 1 else G, after))
            after = stack[-1].done
        block = ctx.enter_context(nc.Block())

        @block.sync
        def _(sp):
            core.load(sp)
            core.lead(sp)
            for layer in stack:
                layer.sync(sp)
            sp.wait_ge(*after)
            sp.dma_start(out_dram, core.arena[:, 0:C * T]).then_inc(core.stored.sem, 16)
            sp.wait_ge(core.stored.sem, core.stored.at(1))

        @block.gpsimd
        def _(pool):
            core.wait_loaded(pool)
            for layer in stack:
                layer.gpsimd(pool)

        @block.tensor
        def _(pe):
            core.wait_loaded(pe)
            for layer in stack:
                layer.tensor(pe)

        @block.vector
        def _(dve):
            core.wait_loaded(dve)
            for layer in stack:
                layer.vector(dve)

        @block.scalar
        def _(act):
            core.wait_loaded(act)
            for layer in stack:
                layer.scalar(act)



def norm_signals(core, name, per=2):
    return [core.new_signal(f"{name}_{n}", per) for n in ("mu", "cen", "sq", "var", "lnv", "rstd", "nrm")]


class Norm:

    def __init__(self, core, told, nth, w, eps):
        self.core, self.nth, self.w, self.eps = core, nth + 1, w, eps
        self.mu, self.cen, self.sq, self.var, self.lnv, self.rstd, self.nrm = told

    def memory(self, r, rs=None):
        self.yc, self.s2 = r.take(C, N), r.take(C, N)
        self.rs = r.take(N) if rs is None else rs
        return self

    def pe_mean(self, pe, src, i):
        for c in range(C):
            mm = pe.matmul(self.core.part(self.w, 0), self.core.mean_w, src(c), start=c == 0, stop=c == C - 1)
        mm.then_inc(self.mu.sem, 1)

    def dve_center(self, dve, src, i):
        dve.wait_ge(self.mu.sem, self.mu.at(i, self.nth))
        mu = self.core.part(self.w, 0).unsqueeze(1).broadcast_to([P, C, N])
        dve.tensor_tensor(self.yc, src, mu, ALU.subtract).then_inc(self.cen.sem, 1)

    def act_square(self, act, i):
        act.wait_ge(self.cen.sem, self.cen.at(i, self.nth))
        act.activation(self.s2, self.yc, ACT.Square).then_inc(self.sq.sem, 1)

    def pe_var(self, pe, i):
        pe.wait_ge(self.sq.sem, self.sq.at(i, self.nth))
        for c in range(C):
            mm = pe.matmul(self.core.part(self.w, 2), self.core.mean_w, self.s2[:, c, :], start=c == 0,
                           stop=c == C - 1)
        mm.then_inc(self.var.sem, 1)

    def act_rstd(self, act, i):
        act.wait_ge(self.var.sem, self.var.at(i, self.nth))
        act.activation(self.rs, self.core.part(self.w, 2), ACT.Ln,
                       bias=self.core.epsc[:, self.eps:self.eps + 1]).then_inc(self.lnv.sem, 1)
        act.wait_ge(self.lnv.sem, self.lnv.at(i, self.nth))
        act.activation(self.rs, self.rs, ACT.Exp, scale=-0.5).then_inc(self.rstd.sem, 1)

    def dve_scale(self, dve, i):
        dve.wait_ge(self.rstd.sem, self.rstd.at(i, self.nth))
        rs = self.rs.unsqueeze(1).broadcast_to([P, C, N])
        dve.tensor_tensor(self.yc, self.yc, rs, ALU.mult).then_inc(self.nrm.sem, 1)

    def wait_scaled(self, eng, i):
        eng.wait_ge(self.nrm.sem, self.nrm.at(i, self.nth))


def project(pe, core, w, weight, src, k_chunks=C, m_chunks=C):
    for m in range(m_chunks):
        for k in range(k_chunks):
            mm = pe.matmul(core.part(w, m), weight[:, k, m * P:(m + 1) * P], src(k), start=k == 0,
                           stop=k == k_chunks - 1)
    return mm



VEC = ["ln1_w", "ln1_b", "maa_x", "stack0", "stack1", "stack2", "stack3", "stack4", "time_decay", "u", "gn_w",
       "gn_b", "ln2_w", "ln2_b", "ffn_maa_k", "ffn_maa_r", "zero"]
RWKV_SIGNALS = dict(
    weights=16 * 8, spread_in=16, spread=1, decay_zeros=2,
    state1_in_xs=1, xa=4, shift=1, xa_shifted=4, mix_hidden_sum=1, mix_hidden=2, mix_sum=5, mix_term=20, mixed=5,
    r_sum=1, k_sum=1, v_sum=1, gate_sum=1, decay_hidden_sum=1, decay_sum=1, r=1, k=1, v=2, v_low=1, gate_tanh=1,
    gate=1, decay_hidden=1, decay_rate=4, decay=4, ruk=4, bonus_sum=1, bonus=1,
    v_spread=16, kv=16, states=16, r_states=16, r_states_sum=8,
    head_out=1, head_mean=1, head_centred=1, head_squares=1, head_var=1, head_log_var=1, head_rstd=1,
    head_normed=1, head_affine=4, gated=1, out_sum=1, x1=1,
    state0_in_xs2=1, xc=4, shift2=1, ffn_mix=8, ffn_r_sum=1, ffn_k_sum=1, ffn_tanh=1, ffn_relu=1, ffn_squared=1,
    ffn_v_sum=1, ffn_gated=1, group_done=1)


class RwkvMemory:

    def __init__(self, core):
        r = Region(core.arena, core.own)
        start = r.at
        self.W = {}
        for n in ("r", "k", "v", "g", "o", "fr", "fk", "fv"):
            self.W[n] = r.take(C, D)
        self.w1 = r.take(C, 5 * DM)
        self.w2 = r.take(4, D)
        self.w2b = r.take(D)
        self.td1 = r.take(C, DD)
        self.td2 = r.take(D)
        self.vec = r.take(17, C)
        self.s0 = r.take(C, 16, B)
        self.weights = core.arena[:, start:r.at]
        self.n1 = Norm(core, norm_signals(core, "rw1", 1), 0, 2, 0).memory(r)
        self.xs = r.take(C, NB, E)
        self.sx, self.xx = r.take(C, N), r.take(C, N)
        self.tha, self.thb, self.tdh = r.take(N), r.take(N), r.take(N)
        self.xm = [r.take(C, N) for _ in range(5)]
        self.rk, self.gt, self.e1 = self.xx, self.n1.s2, self.xm[1]
        self.r, self.k, self.v, self.g, self.bon = (r.take(C, N) for _ in range(5))
        self.we = r.take(2, 4, NB * E)
        self.ring_at = r.at
        self.ring = [r.take(4, NB * E) for _ in range(4)]
        self.n2 = Norm(core, norm_signals(core, "rw2", 1), 0, 1, 0).memory(r, self.n1.rs)
        self.xs2 = r.take(C, NB, E)
        a, b, c, d = (v.rearrange("p a b -> p (a b)")[:, 0:C * N].rearrange("p (c n) -> p c n", c=C) for v in self.ring)
        self.og, self.oc, self.osq, self.ors, self.og2 = a, self.n2.yc, self.n2.s2, b, c
        self.sx2, self.xk2, self.xr2, self.ff, self.kk, self.thr = d, a, b, c, self.n2.s2, d
        self.v_high, self.v_low = (core.ctx.enter_context(core.nc.sbuf_tensor(n, [P, C, N], F32R))
                                   for n in ("v_high", "v_low"))
        self.spread_w = core.ctx.enter_context(core.nc.sbuf_tensor("spread_w", [P, HS, P], F32R))
        self.spread_in = core.arena[:, self.ring_at:self.ring_at + HS * P]
        self.s = {n: core.new_signal("rw_" + n, per) for n, per in RWKV_SIGNALS.items()}


def rwkv(core, m, name, base, after):
    X, part, wide, dram, psum = core.X, core.part, core.wide, core.dram, core.psum

    def vec(n, c):
        j = VEC.index(n)
        return m.vec[:, j, c:c + 1]

    def wait(eng, n, i, k=0):
        eng.wait_ge(m.s[n].sem, m.s[n].at(i, k))

    def sem(n):
        return m.s[n].sem

    def xg(g):
        return X[:, :, ds(g, N)]

    def seq(v):
        return v.rearrange("p c (b t) -> p c b t", b=NB)

    def pairs(v, cc):
        return v[:, 2 * cc:2 * cc + 2, :].rearrange("p c (b t) -> p (c b) t", b=NB)

    def item(n):
        cc, q, odd = n // 8, n % 8 // 2, n % 2
        return cc, q, 8 * odd + q, 2 * odd

    def sync(sp):
        if after:
            sp.wait_ge(*after)
        if occ == 0:
            sp.dma_start(m.spread_in, dram["spread"]).then_inc(sem("spread_in"), 16)
        n = m.weights.shape[1]
        step = -(-n // 8)
        for q in range(8):
            a, b = q * step, min(n, (q + 1) * step)
            sp.dma_start(m.weights[:, a:b], dram[name + "_w"][:, a:b]).then_inc(sem("weights"), 16)

    occ = base // G

    def turns(eng, body):
        wait(eng, "weights", occ + 1)
        body(base - 1, -1, False, True)
        with eng.Fori(0, G - 1) as g:
            body(g + base, g, True, True)
        body(base + G - 1, G - 1, True, False)

    def tensor(pe):
        def body(i, g, back, front):
            f_ = i + 1

            def mix(f):
                w = (2, 2, 2, 3, 3)[f]
                for c in range(C):
                    if f < 4:
                        mm = pe.matmul(part(w, c), m.w2[:, f, c * P:(c + 1) * P], m.tha, start=True, stop=True)
                    else:
                        mm = pe.matmul(part(w, c), m.w2b[0:DM, c * P:(c + 1) * P], m.thb[0:DM, :], start=True,
                                       stop=True)
                mm.then_inc(sem("mix_sum"), 1)

            def reduce(pair):
                wait(pe, "r_states", i, 2 * pair + 2)
                for n in (2 * pair, 2 * pair + 1):
                    cc, q, _, t0 = item(n)
                    rv = m.ring[n % 4].rearrange("p (h c) (b e) -> p h (c b) e", h=2, b=NB)
                    for h in range(2):
                        r0 = 32 * (t0 + h)
                        mm = pe.matmul(psum[r0:r0 + 32, 6 + cc, 0:2 * N], core.red_w[:, 24 - 8 * q:56 - 8 * q],
                                       rv[:, h, :, 0:L], start=q == 0, stop=q == 3)
                mm.then_inc(sem("r_states_sum"), 1)

            for n in range(17):
                if back and n < 16:
                    cc, _, j0, _ = item(n)
                    w = (n + 1) % 2
                    if n == 0:
                        wait(pe, "v", i, 2)
                        wait(pe, "v_low", i, 1)
                        pe.wait_ge(sem("spread"), m.s["spread"].at(1))
                        wait(pe, "ffn_tanh", i)
                    elif n == 1:
                        wait(pe, "ffn_gated", i)
                    else:
                        wait(pe, "kv", i, n - 1)
                    for h in range(2):
                        sel = m.spread_w[:, j0 + 4 * h, :]
                        o = psum[:, 2 * w + h, 0:2 * N]
                        for v, first in ((m.v_high, True), (m.v_low, False)):
                            mv = v[:, 2 * cc:2 * cc + 2, :].rearrange("p c n -> p (c n)")
                            mm = pe.matmul(o, sel, mv, start=first, stop=not first)
                    mm.then_inc(sem("v_spread"), 1)
                if back and n == 4:
                    wait(pe, "bonus", i, 1)
                if back and n >= 4 and n % 2 == 0:
                    reduce(n // 2 - 2)
                if front and n == 1:
                    wait(pe, "gate", f_)
                    m.n1.pe_mean(pe, lambda c: X[:, c, ds(g + 1, N)], f_)
                if front and n == 4:
                    m.n1.pe_var(pe, f_)
                if front and n == 10:
                    wait(pe, "xa_shifted", f_, 4)
                    for k in range(C):
                        pe.matmul(part(2, 0), m.w1[:, k, 0:P], m.xx[:, k, :], start=k == 0, stop=k == C - 1)
                    for k in range(C):
                        mm = pe.matmul(part(2, 2, DM), m.w1[:, k, P:P + DM], m.xx[:, k, :], start=k == 0,
                                       stop=k == C - 1)
                    mm.then_inc(sem("mix_hidden_sum"), 1)
                if front and n == 11:
                    wait(pe, "mix_hidden", f_, 2)
                    mix(0)
                if front and n == 13:
                    wait(pe, "mix_term", f_, 4)
                    mix(1)
            if front:
                wait(pe, "mixed", f_, 1)
                wait(pe, "mix_term", f_, 8)
                project(pe, core, 2, m.W["k"], lambda k: m.xm[0][:, k, :]).then_inc(sem("k_sum"), 1)
            if back:
                reduce(7)
                wait(pe, "head_out", i, 1)
                for c in range(C):
                    mm = pe.matmul(part(0, c), core.gmean_w, m.og[:, c, :], start=True, stop=True)
                mm.then_inc(sem("head_mean"), 1)
            if front:
                wait(pe, "mixed", f_, 2)
                for k in range(C):
                    mm = pe.matmul(part(3, 0, DD), m.td1[:, k, :], m.xm[1][:, k, :], start=k == 0, stop=k == C - 1)
                mm.then_inc(sem("decay_hidden_sum"), 1)
            if back:
                wait(pe, "head_squares", i, 1)
                for c in range(C):
                    mm = pe.matmul(part(1, c), core.gmean_w, m.osq[:, c, :], start=True, stop=True)
                mm.then_inc(sem("head_var"), 1)
            if front:
                wait(pe, "k", f_, 1)
                mix(2)
                wait(pe, "decay_hidden", f_, 1)
                mix(3)
                wait(pe, "mix_term", f_, 12)
                for c in range(C):
                    mm = pe.matmul(part(2, c), m.td2[0:DD, c * P:(c + 1) * P], m.tdh[0:DD, :], start=True, stop=True)
                mm.then_inc(sem("decay_sum"), 1)
            if back:
                wait(pe, "gated", i, 1)
                project(pe, core, 0, m.W["o"], lambda k: m.og2[:, k, :]).then_inc(sem("out_sum"), 1)
            if front:
                wait(pe, "mix_term", f_, 16)
                mix(4)
            if back:
                wait(pe, "x1", i, 1)
                m.n2.pe_mean(pe, lambda c: X[:, c, ds(g, N)], i)
            if front:
                wait(pe, "mixed", f_, 3)
                wait(pe, "decay_rate", f_, 4)
                project(pe, core, 2, m.W["v"], lambda k: m.xm[2][:, k, :]).then_inc(sem("v_sum"), 1)
            if back:
                m.n2.pe_var(pe, i)
            if front:
                wait(pe, "mixed", f_, 4)
                wait(pe, "mix_term", f_, 20)
                project(pe, core, 3, m.W["r"], lambda k: m.xm[3][:, k, :]).then_inc(sem("r_sum"), 1)
                wait(pe, "mixed", f_, 5)
                wait(pe, "v", f_, 2)
                project(pe, core, 2, m.W["g"], lambda k: m.xm[4][:, k, :]).then_inc(sem("gate_sum"), 1)
            if back:
                wait(pe, "ffn_mix", i, 4)
                project(pe, core, 0, m.W["fk"], lambda k: m.xk2[:, k, :]).then_inc(sem("ffn_k_sum"), 1)
                wait(pe, "ffn_mix", i, 8)
                project(pe, core, 1, m.W["fr"], lambda k: m.xr2[:, k, :]).then_inc(sem("ffn_r_sum"), 1)
            if front:
                wait(pe, "r", f_, 1)
                wait(pe, "ruk", f_, 4)
                for c in range(C):
                    mm = pe.matmul(part(3, c), core.heads_w, m.rk[:, c, :], start=True, stop=True)
                mm.then_inc(sem("bonus_sum"), 1)
            if back:
                wait(pe, "ffn_squared", i, 1)
                project(pe, core, 0, m.W["fv"], lambda k: m.kk[:, k, :]).then_inc(sem("ffn_v_sum"), 1)

        turns(pe, body)

    def vector(dve):
        def body(i, g, back, front):
            f_ = i + 1

            def mix_term(f):
                wait(dve, "mix_sum", f_, f + 1)
                for c in range(C):
                    dve.scalar_tensor_tensor(m.xm[f][:, c, :], part((2, 2, 2, 3, 3)[f], c), vec(f"stack{f}", c),
                                             m.sx[:, c, :], ALU.add, ALU.mult).then_inc(sem("mix_term"), 1)

            def step(n):
                cc, _, j0, _ = item(n)
                av = m.ring[n % 4].rearrange("p (h c) (b e) -> p h c b e", h=2, b=NB)
                if n >= 4:
                    wait(dve, "r_states_sum", i, (n - 4) // 2 + 1)
                s0 = m.s0[:, 2 * cc:2 * cc + 2, j0:j0 + 5:4, ds(g, NB)].rearrange("p c h b -> p h c b")
                dve.tensor_copy(av[:, :, :, :, 0], s0)
                wait(dve, "v_spread", i, n + 1)
                w = (n + 1) % 2
                kb = pairs(m.k, cc).unsqueeze(1).broadcast_to([P, 2, 2 * NB, L])
                vb = psum[:, 2 * w:2 * w + 2, 0:2 * N].rearrange("p h (a t) -> p h a t", t=L)
                dst = m.ring[n % 4].rearrange("p (h c) (b e) -> p h (c b) e", h=2, b=NB)[:, :, :, 1:E]
                dve.tensor_tensor(dst, kb, vb, ALU.mult).then_inc(sem("kv"), 1)
                wait(dve, "kv", i, n + 1)
                if n % 8 == 0:
                    wait(dve, "decay", i, 2 * cc + 2)
                flat = m.ring[n % 4].rearrange("p j e -> p (j e)")
                dve.tensor_tensor_scan(flat, m.we[:, cc].rearrange("p j e -> p (j e)"), flat, 0.0,
                                       ALU.mult, ALU.add).then_inc(sem("states"), 1)

            for n in range(16):
                if back:
                    step(n)
                if front and n == 2:
                    dve.tensor_copy(m.xs[:, :, :, 0], core.st[:, :, 1, ds(g + 1, NB)]).then_inc(sem("state1_in_xs"), 1)
                    m.n1.dve_center(dve, xg(g + 1), f_)
                if front and n == 5:
                    m.n1.dve_scale(dve, f_)
                if front and n == 7:
                    wait(dve, "state1_in_xs", f_, 1)
                    wait(dve, "xa", f_, 4)
                    dve.tensor_tensor(seq(m.sx), m.xs[:, :, :, 0:L], m.xs[:, :, :, 1:E],
                                      ALU.subtract).then_inc(sem("shift"), 1)
                    wait(dve, "shift", f_, 1)
                    for c in range(C):
                        dve.scalar_tensor_tensor(seq(m.xx)[:, c], seq(m.sx)[:, c], vec("maa_x", c), m.xs[:, c, :, 1:E],
                                                 ALU.mult, ALU.add).then_inc(sem("xa_shifted"), 1)
                if front and n == 11:
                    mix_term(0)
                if front and n == 13:
                    mix_term(1)
            if front:
                wait(dve, "k_sum", f_, 1)
                dve.tensor_copy(two(m.k), wide[2]).then_inc(sem("k"), 1)
            if back:
                wait(dve, "r_states_sum", i, 8)
                dve.tensor_tensor(two(m.og), wide[3], two(m.bon), ALU.add).then_inc(sem("head_out"), 1)
                wait(dve, "head_out", i, 1)
                wait(dve, "head_mean", i, 1)
                dve.tensor_tensor(two(m.oc), two(m.og), wide[0], ALU.subtract).then_inc(sem("head_centred"), 1)
            if front:
                mix_term(2)
            if back:
                wait(dve, "head_rstd", i, 1)
                dve.tensor_tensor(m.oc, m.oc, m.ors, ALU.mult).then_inc(sem("head_normed"), 1)
            if front:
                mix_term(3)
            if back:
                wait(dve, "head_affine", i, 4)
                dve.scalar_tensor_tensor(m.og2, m.oc, 0.5, m.g, ALU.mult, ALU.mult).then_inc(sem("gated"), 1)
                wait(dve, "out_sum", i, 1)
                dve.tensor_tensor(xg(g), psum[:, 0:2, 0:2 * N].rearrange("p a (b n) -> p a b n", b=2), xg(g),
                                  ALU.add).then_inc(sem("x1"), 1)
            if front:
                mix_term(4)
            if back:
                wait(dve, "x1", i, 1)
                m.n2.dve_center(dve, xg(g), i)
                dve.tensor_copy(m.xs2[:, :, :, 0], core.st[:, :, 0, ds(g, NB)]).then_inc(sem("state0_in_xs2"), 1)
            if front:
                wait(dve, "v", f_, 2)
                dve.tensor_tensor(m.v_low[:], m.v, m.v_high[:].bitcast(F32), ALU.subtract).then_inc(sem("v_low"), 1)
            if back:
                m.n2.dve_scale(dve, i)
                wait(dve, "state0_in_xs2", i, 1)
                wait(dve, "xc", i, 4)
                dve.tensor_tensor(seq(m.sx2), m.xs2[:, :, :, 0:L], m.xs2[:, :, :, 1:E],
                                  ALU.subtract).then_inc(sem("shift2"), 1)
                wait(dve, "shift2", i, 1)
                for v, n in ((m.xk2, "ffn_maa_k"), (m.xr2, "ffn_maa_r")):
                    for c in range(C):
                        dve.scalar_tensor_tensor(seq(v)[:, c], seq(m.sx2)[:, c], vec(n, c), m.xs2[:, c, :, 1:E],
                                                 ALU.mult, ALU.add).then_inc(sem("ffn_mix"), 1)
            if front:
                wait(dve, "r_sum", f_, 1)
                dve.tensor_copy(two(m.r), wide[3]).then_inc(sem("r"), 1)
                wait(dve, "k", f_, 1)
                wait(dve, "r", f_, 1)
                for c in range(C):
                    dve.scalar_tensor_tensor(m.rk[:, c, :], m.r[:, c, :], vec("u", c), m.k[:, c, :],
                                             ALU.mult, ALU.mult).then_inc(sem("ruk"), 1)
                wait(dve, "gate_tanh", f_, 1)
                dve.scalar_tensor_tensor(two(m.g), two(m.gt), 1.0, wide[2], ALU.add, ALU.mult).then_inc(sem("gate"), 1)
            if back:
                wait(dve, "ffn_relu", i, 1)
                dve.tensor_tensor(m.kk, m.ff, m.ff, ALU.mult).then_inc(sem("ffn_squared"), 1)
            if front:
                wait(dve, "bonus_sum", f_, 1)
                dve.tensor_tensor(two(m.bon), wide[3], two(m.v), ALU.mult).then_inc(sem("bonus"), 1)
            if back:
                wait(dve, "ffn_squared", i, 1)
                wait(dve, "ffn_tanh", i, 1)
                wait(dve, "ffn_v_sum", i, 1)
                dve.scalar_tensor_tensor(two(m.ff), two(m.thr), 1.0, wide[0], ALU.add, ALU.mult).then_inc(
                    sem("ffn_gated"), 1)
                wait(dve, "ffn_gated", i, 1)
                dve.scalar_tensor_tensor(xg(g), m.ff, 0.5, xg(g), ALU.mult, ALU.add).then_inc(sem("group_done"), 1)

        if occ == 0:
            dve.wait_ge(sem("spread_in"), m.s["spread_in"].at(1))
            dve.tensor_copy(m.spread_w[:].rearrange("p j n -> p (j n)"), m.spread_in).then_inc(sem("spread"), 1)
        wait(dve, "weights", occ + 1)
        dve.memset(m.we.rearrange("p c j (b e) -> p (c j b) e", b=NB)[:, :, 0:1], 0.0).then_inc(sem("decay_zeros"), 2)
        turns(dve, body)

    def scalar(act):
        def body(i, g, back, front):
            f_ = i + 1
            if front:
                m.n1.act_square(act, f_)
                m.n1.act_rstd(act, f_)
                m.n1.wait_scaled(act, f_)
                wait(act, "mixed", f_)
                for c in range(C):
                    act.activation(m.xs[:, c, :, 1:E], seq(m.n1.yc)[:, c], ACT.Identity, bias=vec("ln1_b", c),
                                   scale=vec("ln1_w", c)).then_inc(sem("xa"), 1)
                wait(act, "mix_hidden_sum", f_, 1)
                act.activation(m.tha, part(2, 0), ACT.Tanh).then_inc(sem("mix_hidden"), 1)
                act.activation(m.thb[0:DM, :], part(2, 2, DM), ACT.Tanh).then_inc(sem("mix_hidden"), 1)
            if back:
                wait(act, "head_centred", i, 1)
                act.activation(m.osq, m.oc, ACT.Square).then_inc(sem("head_squares"), 1)
            if front:
                wait(act, "decay_hidden_sum", f_, 1)
                act.activation(m.tdh[0:DD, :], part(3, 0, DD), ACT.Tanh).then_inc(sem("decay_hidden"), 1)
            if back:
                wait(act, "head_var", i, 1)
                act.activation(two(m.ors), wide[1], ACT.Ln, bias=core.epsc[:, 0:1]).then_inc(sem("head_log_var"), 1)
                wait(act, "head_log_var", i, 1)
                act.activation(m.ors, m.ors, ACT.Exp, scale=-0.5).then_inc(sem("head_rstd"), 1)
                wait(act, "head_normed", i, 1)
                for c in range(C):
                    act.activation(m.oc[:, c, :], m.oc[:, c, :], ACT.Identity, bias=vec("gn_b", c),
                                   scale=vec("gn_w", c)).then_inc(sem("head_affine"), 1)
            if front:
                wait(act, "decay_sum", f_, 1)
                for c in range(C):
                    act.activation(m.e1[:, c, :], part(2, c), ACT.Exp, bias=vec("time_decay", c)).then_inc(
                        sem("decay_rate"), 1)
                wait(act, "decay_zeros", occ + 1)
                wait(act, "decay_rate", f_, 4)
                wait(act, "states", f_)
                for cc in range(2):
                    for h in range(2):
                        dst = m.we[:, cc, 2 * h:2 * h + 2].rearrange("p c (b e) -> p (c b) e", b=NB)[:, :, 1:E]
                        act.activation(dst, pairs(m.e1, cc), ACT.Exp, scale=-1.0).then_inc(sem("decay"), 1)
            if back:
                m.n2.act_square(act, i)
            if front:
                wait(act, "v_sum", f_, 1)
                act.activation(two(m.v), wide[2], ACT.Copy).then_inc(sem("v"), 1)
                act.activation(two(m.v_high[:]), wide[2], ACT.Copy).then_inc(sem("v"), 1)
            if back:
                m.n2.act_rstd(act, i)
                m.n2.wait_scaled(act, i)
                for c in range(C):
                    act.activation(m.xs2[:, c, :, 1:E], seq(m.n2.yc)[:, c], ACT.Identity, bias=vec("ln2_b", c),
                                   scale=vec("ln2_w", c)).then_inc(sem("xc"), 1)
            if front:
                wait(act, "gate_sum", f_, 1)
                act.activation(two(m.gt), wide[2], ACT.Tanh, scale=0.5).then_inc(sem("gate_tanh"), 1)
            if back:
                wait(act, "ffn_k_sum", i, 1)
                act.activation(two(m.ff), wide[0], ACT.Relu).then_inc(sem("ffn_relu"), 1)
                wait(act, "ffn_r_sum", i, 1)
                act.activation(two(m.thr), wide[1], ACT.Tanh, scale=0.5).then_inc(sem("ffn_tanh"), 1)

        turns(act, body)

    def gpsimd(pool):
        def body(i, g, back, front):
            def add_token(f):
                wait(pool, "mix_term", i + 1, 4 * f + 4)
                pool.tensor_tensor(seq(m.xm[f]), seq(m.xm[f]), m.xs[:, :, :, 1:E], ALU.add).then_inc(sem("mixed"), 1)

            if back:
                wait(pool, "r", i, 1)
            for n in range(16):
                if back:
                    sv = m.ring[n % 4].rearrange("p (h c) (b e) -> p h (c b) e", h=2, b=NB)[:, :, :, 0:L]
                    rb = pairs(m.r, n // 8).unsqueeze(1).broadcast_to([P, 2, 2 * NB, L])
                    wait(pool, "states", i, n + 1)
                    pool.tensor_tensor(sv, sv, rb, ALU.mult).then_inc(sem("r_states"), 1)
                if front and n == 13:
                    add_token(0)
            if front:
                for f in range(1, 5):
                    add_token(f)

        turns(pool, body)

    return Layer(sync, tensor, vector, scalar, gpsimd, (sem("group_done"), m.s["group_done"].at(base + G)))


def attention(core, name, after):
    X, part, dram, bank, ident = core.X, core.part, core.dram, core.bank, core.ident
    s = lambda n, per=1: core.new_signal(name + "_" + n, per)
    gqa = name == "L0"
    KC = 1 if gqa else C
    KV = KC * P
    NBLK = 8 if gqa else 4
    NB2 = 2 * NBLK
    NQ = 8 if gqa else 4
    TURNS = B // 2
    ORDER = (0, 2, 4, 6, 1, 3, 5, 7)
    scale = -1.0 / np.sqrt(D // (32 if gqa else 16))
    hm = core.hmask if gqa else core.qmask
    AVS = 4 if gqa else NB2

    r = Region(core.arena, core.own)
    w0 = r.at
    Wo = r.take(C, D)
    vec = r.take(26, C)
    w1 = r.at
    qT = r.take(C, T)
    told = norm_signals(core, name)
    norms = [Norm(core, told, u, u, 1 if gqa else 0).memory(r) for u in range(2)]
    behind = 0 if gqa else G // 2
    over = r.at
    Wq = r.take(C, D)
    Wk = r.take(C, KV)
    Wv = r.take(C, KV)
    w2 = r.at
    ctxt = [r.take(C, S) for _ in range(2)]
    kT = [r.take(KC, S) for _ in range(2)]
    raw = r.take(S) if gqa else None
    nmask = [r.take(S) for _ in range(2)]
    qm = [r.take(NQ, C, L) for _ in range(2)]
    vs = [r.take(3, NQ if gqa else 4, 32 if gqa else P) for _ in range(2)]
    s2 = [n.s2.rearrange("p c n -> p (c n)") for n in norms]
    sm = [s2[0][:, 0:S], s2[0][:, S:2 * S], s2[1][:, 0:S]]
    pr = [r.take(4, S) for _ in range(3)]
    pT = [r.take(3, 4, L) for _ in range(4)]
    nmx = r.take(4 * NB2)
    den = r.take(4 * NB2)
    rden = r.take(4 * NB2)
    carry = r.take(4 * NB2)
    if not gqa:
        r2 = Region(core.arena, over)
        fc = r2.take(C, F)
        pj = r2.take(F // P, D)
        hid = [r2.take(F // P, N) for _ in range(2)]
    if not gqa:
        masks = r.take(B * S // 4).bitcast(MASK)

    VN = (["bq", "bk", "bv", "bo", "gamma", "beta"] if gqa else
          ["ln1_w", "ln1_b", "q_b", "k_b", "v_b", "cproj_b", "ln2_w", "ln2_b", "proj_b"])

    def vec_(n, c):
        return vec[:, VN.index(n), c:c + 1]

    bq, bk, bv, bo = ("bq", "bk", "bv", "bo") if gqa else ("q_b", "k_b", "v_b", "cproj_b")
    gam, bet = ("gamma", "beta") if gqa else ("ln2_w", "ln2_b")

    weights = s("weights", 64)
    qp = s("qp", 2)
    qd = [s(f"qd{u}", 4) for u in range(2)]
    ctx_in = [s(f"ctx{u}", 16) for u in range(2)]
    mask_in = [s(f"mask{u}", 16) for u in range(2)] if gqa else s("mask", 16)
    nm, qmd = s("nm", 2), s("qm", 2 * NQ)
    kp, vp, kev = s("kp", 2 * KC), s("vp", 2 * 3), s("kev", 2 * KC)
    vev = s("vev", 2 * (4 if gqa else 3))
    if gqa:
        vzero = s("vzero", 2)
    else:
        wfc, wpj, yn, fcp, gel, pjp, fin = s("wfc", 64), s("wpj", 64), s("yn", 8), s("fcp", 8), s("gel", 32), s("pjp", 2), s("fin", 8)
    sc_, ttr, ex = s("scores", 4 * NB2), s("ttr", 4 * NB2), s("exp", 4 * NB2)
    rd, pn, tr, tea, ted = s("rd", NB2), s("pn", 4 * NB2), s("tr", NB2), s("tea", 2 * NB2), s("ted", NB2)
    av, oev = s("av", AVS), s("oev", 2 if gqa else 8)
    op, res, aff = s("op", 2), s("res", 8), s("aff", 8)
    OEV = 1 if gqa else 4
    VEV = 4 if gqa else 3
    pairs = G // 2

    def xg(j):
        return X[:, :, ds(j, N)]

    def spans(a, b, n):
        step = -(-(b - a) // n)
        return [(a + k * step, min(b, a + (k + 1) * step)) for k in range(n)]

    def sync(sp):
        if after:
            sp.wait_ge(*after)
        for at, (c, d) in ((0, (w0, w1)), (w1 - w0, (over, w2))):
            for a, b in spans(c, d, 2):
                sp.dma_start(core.arena[:, a:b], dram[name + "_w"][:, at + a - c:at + b - c]).then_inc(weights.sem, 16)
        if not gqa:
            sp.dma_start(masks[0:L], dram["mask2"].rearrange("b s -> (b s)").unsqueeze(0).broadcast_to([L, B * S])).then_inc(mask_in.sem, 16)
        with sp.Fori(0, TURNS) as t:
            for u in range(2):
                b = sp.snap(2 * t + u)
                sp.wait_ge(vp.sem, vp.at(t))
                sp.dma_start(ctxt[u], dram["ctxT"][bass.ds(b, 1)].rearrange("o p c s -> p (o c) s")).then_inc(ctx_in[u].sem, 16)
                if gqa:
                    sp.wait_ge(nm.sem, nm.at(t, u))
                    sp.dma_start(raw[0:L], dram["mask0"][bass.ds(b, 1)].rearrange("o l s -> (o l) s")).then_inc(mask_in[u].sem, 16)
        if not gqa:
            sp.wait_ge(oev.sem, oev.at(TURNS))
            for v, n, done in ((fc, "L2_fc", wfc), (pj, "L2_pj", wpj)):
                src = dram[n].rearrange("p (a b) -> p a b", b=v.shape[2])
                q = v.shape[1] // 4
                for j in range(4):
                    sp.dma_start(v[:, q * j:q * j + q], src[:, q * j:q * j + q]).then_inc(done.sem, 16)

    def tensor(pe):
        pe.wait_ge(weights.sem, weights.at(1))
        with pe.Fori(0, pairs) as t:
            if not gqa:
                for u in range(2):
                    pe.wait_ge(norms[u].nrm.sem, norms[u].nrm.at(t))
                    norms[u].pe_mean(pe, lambda c: X[:, c, bass.ds(t * (2 * N) + u * N, N)], t)
                for u in range(2):
                    norms[u].pe_var(pe, t)
            for u in range(2):
                pe.wait_ge(qd[u].sem, qd[u].at(t))
                if gqa:
                    src = lambda k: X[:, k, bass.ds(t * (2 * N) + u * N, N)]
                else:
                    pe.wait_ge(yn.sem, yn.at(t, 4 * u + 4))
                    src = lambda k: norms[u].yc[:, k, :]
                project(pe, core, 2 + u, Wq, src).then_inc(qp.sem, 1)
        for u in range(2):
            pe.wait_ge(qd[u].sem, qd[u].at(pairs))

        def keys_values(t, u):
            pe.wait_ge(ctx_in[u].sem, ctx_in[u].at(t, 16))
            for c in range(KC):
                if c >= 2:
                    pe.wait_ge(kev.sem, kev.at(t, u * KC + c - 1))
                elif u == 0:
                    pe.wait_ge(vev.sem, vev.at(t))
                else:
                    pe.wait_ge(vev.sem, vev.at(t, VEV))
                for k in range(C):
                    mm = pe.matmul(bank[6 + c % 2][:, 0:S], Wk[:, k, c * P:(c + 1) * P], ctxt[u][:, k, :],
                                   start=k == 0, stop=k == C - 1)
                mm.then_inc(kp.sem, 1)
            for j, (a, n) in enumerate(SC):
                if gqa:
                    o = bank[7][0:n, j * P:(j + 1) * P]
                    if j == 0:
                        pe.wait_ge(vev.sem, vev.at(t, u * VEV))
                else:
                    o = bank[6 + j % 2][0:n, :]
                    if j < 2:
                        pe.wait_ge(kev.sem, kev.at(t, u * KC + 3 + j))
                    else:
                        pe.wait_ge(vev.sem, vev.at(t, u * VEV + j - 1))
                for k in range(C):
                    mm = pe.matmul(o, ctxt[u][:, k, a:a + n], Wv[:, k, :], start=k == 0, stop=k == C - 1)
                mm.then_inc(vp.sem, 1)

        with pe.Fori(0, TURNS) as t:
            keys_values(t, 0)
            for n in range(NB2 + 3):
                if n < NB2:
                    u, nl = n // NBLK, n % NBLK
                    if nl == 0:
                        pe.wait_ge(qmd.sem, qmd.at(t, NQ * (u + 1)))
                        pe.wait_ge(kev.sem, kev.at(t, KC * (u + 1)))
                    for x in range(4):
                        k = 4 * n + x
                        if k >= 2:
                            pe.wait_ge(ttr.sem, ttr.at(t, k - 1))
                        q = qm[u][:, ORDER[nl], x, :] if gqa else qm[u][:, x, nl, :]
                        pe.matmul(bank[k % 2][0:L, 0:S], q, kT[u][:, 0 if gqa else nl, :], start=True,
                                  stop=True).then_inc(sc_.sem, 1)
                if n == 1:
                    keys_values(t, 1)
                m = n - 2
                if 0 <= m < NB2:
                    pe.wait_ge(pn.sem, pn.at(t, 4 * m + 4))
                    if m >= 1:
                        pe.wait_ge(tea.sem, tea.at(t, 2 * m))
                        pe.wait_ge(ted.sem, ted.at(t, m))
                    for j, (a, w) in enumerate(SC):
                        for x in range(4):
                            mm = pe.transpose(bank[2 + j][0:w, x * L:(x + 1) * L], pr[m % 3][0:L, x, a:a + w],
                                              ident[0:L, 0:L])
                    mm.then_inc(tr.sem, 1)
                m = n - 3
                if m < 0 or m >= NB2:
                    continue
                u, nl = m // NBLK, m % NBLK
                if gqa and nl % 4 != 3:
                    continue
                pe.wait_ge(tea.sem, tea.at(t, 2 * m + 2))
                pe.wait_ge(ted.sem, ted.at(t, m + 1))
                if nl == (3 if gqa else 0):
                    pe.wait_ge(vev.sem, vev.at(t, VEV * (u + 1)))
                    pe.wait_ge(oev.sem, oev.at(t, OEV * u))
                for j, (a, w) in enumerate(SC):
                    for x in range(4):
                        if gqa:
                            kv = ORDER[nl - 3 + x]
                            mm = pe.matmul(bank[5][32 * x:32 * x + 32, 0:4 * L], vs[u][0:w, j, kv, :],
                                           pT[(m - 3 + x) % 4][0:w, j].rearrange("p h l -> p (h l)"),
                                           start=nl == 3 and j == 0, stop=nl == 7 and j == 2)
                        else:
                            mm = pe.matmul(bank[5][32 * x:32 * x + 32, nl * L:(nl + 1) * L],
                                           vs[u][0:w, j, nl, 32 * x:32 * x + 32], pT[m % 4][0:w, j, x, :],
                                           start=j == 0, stop=j == 2)
                mm.then_inc(av.sem, 1)
        pe.wait_ge(oev.sem, oev.at(TURNS))
        with pe.Fori(0, pairs) as t:
            def xs(u):
                return lambda c: X[:, c, bass.ds(t * (2 * N) + u * N, N)]

            for u in range(2):
                if not gqa:
                    pe.wait_ge(gel.sem, gel.at(t))
                    pe.wait_ge(fin.sem, fin.at(t))
                pe.wait_ge(res.sem, res.at(t))
                project(pe, core, 2 + u, Wo, lambda k: qT[:, k, bass.ds(t * (2 * N) + u * N, N)]).then_inc(op.sem, 1)
            for u in range(2):
                pe.wait_ge(res.sem, res.at(t, 4 * u + 4))
                norms[u].pe_mean(pe, xs(u), t + behind)
            for u in range(2):
                norms[u].pe_var(pe, t + behind)
            if not gqa:
                for q in range(8):
                    u = q // 4
                    if q == 0:
                        pe.wait_ge(wfc.sem, wfc.at(1))
                        pe.wait_ge(gel.sem, gel.at(t))
                    if q % 4 == 0:
                        pe.wait_ge(aff.sem, aff.at(t, 4 * u + 4))
                    if q >= 2:
                        pe.wait_ge(gel.sem, gel.at(t, 4 * (q - 1)))
                    for m in range(4):
                        for k in range(C):
                            mm = pe.matmul(part(2 + q % 2, m), fc[:, k, ((q % 4) * 4 + m) * P:((q % 4) * 4 + m + 1) * P],
                                           norms[u].yc[:, k, :], start=k == 0, stop=k == C - 1)
                    mm.then_inc(fcp.sem, 1)
                pe.wait_ge(wpj.sem, wpj.at(1))
                for u in range(2):
                    pe.wait_ge(gel.sem, gel.at(t, 16 * (u + 1)))
                    project(pe, core, u, pj, lambda k: hid[u][:, k, :], k_chunks=F // P).then_inc(pjp.sem, 1)

    def vector(dve):
        dve.wait_ge(weights.sem, weights.at(1))
        for u in range(2):
            if gqa:
                dve.memset(vs[u], 0.0).then_inc(vzero.sem, 1)
        with dve.Fori(0, pairs) as t:
            if not gqa:
                for u in range(2):
                    dve.wait_ge(qp.sem, qp.at(t))
                    norms[u].dve_center(dve, X[:, :, bass.ds(t * (2 * N) + u * N, N)], t)
                for u in range(2):
                    norms[u].dve_scale(dve, t)
            for u in range(2):
                dve.wait_ge(qp.sem, qp.at(t, u + 1))
                for c in range(C):
                    dve.tensor_scalar(qT[:, c, bass.ds(t * (2 * N) + u * N, N)], part(2 + u, c), vec_(bq, c), scale,
                                      ALU.add, ALU.mult).then_inc(qd[u].sem, 1)
        with dve.Fori(0, TURNS) as t:
            def mask(u):
                if gqa:
                    dve.wait_ge(mask_in[u].sem, mask_in[u].at(t, 16))
                    dve.tensor_scalar(nmask[u][0:L], raw[0:L], -1.0, None, ALU.mult).then_inc(nm.sem, 1)
                else:
                    if u == 0:
                        dve.wait_ge(mask_in.sem, mask_in.at(1))
                    dve.tensor_scalar(nmask[u][0:L], masks[0:L, bass.ds(t * (2 * S) + u * S, S)], -FLT, FLT, ALU.mult, ALU.add).then_inc(nm.sem, 1)

            def values(u):
                if gqa:
                    if u == 0:
                        dve.wait_ge(vzero.sem, vzero.at(1))
                    for j0, j1, w in ((0, 2, P), (2, 3, SC[2][1])):
                        dve.wait_ge(vp.sem, vp.at(t, 3 * u + 3))
                        for odd in range(2):
                            src = bank[7][0:w, j0 * P:j1 * P].rearrange("p (j a o d) -> p j a o d", a=4, o=2, d=16)[:, :, :, odd]
                            dst = vs[u][0:w, j0:j1].rearrange("p j (a o) d -> p j a o d", o=2)[:, :, :, odd, 16 * odd:16 * odd + 16]
                            dve.tensor_copy(dst, src).then_inc(vev.sem, 1)
                else:
                    for j, (a, w) in enumerate(SC):
                        dve.wait_ge(vp.sem, vp.at(t, 3 * u + j + 1))
                        dve.tensor_copy(vs[u][0:w, j].rearrange("p a b -> p (a b)"), bank[6 + j % 2][0:w, :]).then_inc(vev.sem, 1)

            mask(0)
            mask(1)
            values(0)
            for n in range(NB2 + 4):
                if n < NB2:
                    u = n // NBLK
                    if n % NBLK == 0:
                        dve.wait_ge(nm.sem, nm.at(t, 2))
                    for x in range(4):
                        k = 4 * n + x
                        if k >= 3:
                            dve.wait_ge(ex.sem, ex.at(t, k - 2))
                        dve.wait_ge(sc_.sem, sc_.at(t, k + 1))
                        dve.memset(carry[0:1, k:k + 1], 0.0)
                        dve.tensor_tensor_reduce(out=sm[k % 3][0:L], in0=bank[k % 2][0:L, 0:S], in1=nmask[u][0:L],
                                                 scale=1.0, scalar=FLT, op0=ALU.add, op1=ALU.min,
                                                 accum_out=nmx[0:L, k:k + 1]).then_inc(ttr.sem, 1)
                if n == 1:
                    values(1)
                m = n - 1
                if 0 <= m < NB2:
                    dve.wait_ge(ex.sem, ex.at(t, 4 * m + 4))
                    dve.reciprocal(rden[0:L, 4 * m:4 * m + 4], den[0:L, 4 * m:4 * m + 4]).then_inc(rd.sem, 1)
                    dve.wait_ge(rd.sem, rd.at(t, m + 1))
                    for x in range(4):
                        p = pr[m % 3][0:L, x, :]
                        dve.tensor_scalar(p, p, rden[0:L, 4 * m + x:4 * m + x + 1], None, ALU.mult).then_inc(pn.sem, 1)
                m = n - 2
                if 0 <= m < NB2:
                    dve.wait_ge(tr.sem, tr.at(t, m + 1))
                    free_pt(dve, t, m)
                    w = SC[2][1]
                    dve.tensor_copy(pT[m % 4][0:w, 2].rearrange("p h l -> p (h l)"), bank[4][0:w, 0:4 * L]).then_inc(ted.sem, 1)
                m = n - 3
                if 0 <= m < NB2 and m % NBLK == NBLK - 1:
                    u = m // NBLK
                    dve.wait_ge(av.sem, av.at(t, AVS // 2 * (u + 1)))
                    o = bass.ds(t * (2 * L) + u * L, L)
                    if gqa:
                        dve.tensor_scalar(qT[:, :, o], bank[5][:, 0:4 * L].rearrange("p (h l) -> p h l", h=4),
                                          vec_(bv, 0), None, ALU.add).then_inc(oev.sem, 1)
                    else:
                        for c in range(C):
                            dve.tensor_scalar(qT[:, c, o], bank[5][:, c * L:(c + 1) * L], vec_(bv, c), None,
                                              ALU.add).then_inc(oev.sem, 1)
        with dve.Fori(0, pairs) as t:
            def xo(u):
                return bass.ds(t * (2 * N) + u * N, N)

            for u in range(2):
                dve.wait_ge(op.sem, op.at(t, u + 1))
                for c in range(C):
                    dve.scalar_tensor_tensor(X[:, c, xo(u)], part(2 + u, c), vec_(bo, c), X[:, c, xo(u)], ALU.add,
                                             ALU.add).then_inc(res.sem, 1)
            for u in range(2):
                dve.wait_ge(res.sem, res.at(t, 4 * u + 4))
                dve.wait_ge((aff if gqa else fcp).sem, (aff if gqa else fcp).at(t))
                norms[u].dve_center(dve, X[:, :, xo(u)], t + behind)
            for u in range(2):
                norms[u].dve_scale(dve, t + behind)
            if not gqa:
                for u in range(2):
                    dve.wait_ge(pjp.sem, pjp.at(t, u + 1))
                    for c in range(C):
                        dve.scalar_tensor_tensor(X[:, c, xo(u)], part(u, c), vec_("proj_b", c), X[:, c, xo(u)],
                                                 ALU.add, ALU.add).then_inc(fin.sem, 1)

    def free_pt(eng, t, m):
        if m >= 4:
            eng.wait_ge(av.sem, av.at(t, m // 4 if gqa else m - 3))

    def scalar(act):
        act.wait_ge(weights.sem, weights.at(1))
        if not gqa:
            with act.Fori(0, pairs) as t:
                for u in range(2):
                    norms[u].act_square(act, t)
                for u in range(2):
                    norms[u].act_rstd(act, t)
                for u in range(2):
                    norms[u].wait_scaled(act, t)
                    for c in range(C):
                        y = norms[u].yc[:, c, :]
                        act.activation(y, y, ACT.Identity, bias=vec_("ln1_b", c),
                                       scale=vec_("ln1_w", c)).then_inc(yn.sem, 1)
        with act.Fori(0, TURNS) as t:
            def keys(u):
                for c in range(KC):
                    act.wait_ge(kp.sem, kp.at(t, KC * u + c + 1))
                    act.activation(kT[u][:, c, :], bank[6 + c % 2][:, 0:S], ACT.Identity,
                                   bias=vec_(bk, c)).then_inc(kev.sem, 1)

            keys(0)
            for n in range(NB2 + 2):
                if n < NB2:
                    for x in range(4):
                        k = 4 * n + x
                        act.wait_ge(ttr.sem, ttr.at(t, k + 1))
                        if x == 0 and n >= 3:
                            act.wait_ge(tr.sem, tr.at(t, n - 2))
                        act.activation(pr[n % 3][0:L, x, :], sm[k % 3][0:L], ACT.Exp, bias=nmx[0:L, k:k + 1],
                                       scale=-1.0, accum_out=den[0:L, k:k + 1]).then_inc(ex.sem, 1)
                if n == 1:
                    keys(1)
                m = n - 2
                if 0 <= m < NB2:
                    act.wait_ge(tr.sem, tr.at(t, m + 1))
                    free_pt(act, t, m)
                    for j in range(2):
                        act.activation(pT[m % 4][:, j].rearrange("p h l -> p (h l)"), bank[2 + j][:, 0:4 * L],
                                       ACT.Copy).then_inc(tea.sem, 1)
        with act.Fori(0, pairs) as t:
            for u in range(2):
                norms[u].act_square(act, t + behind)
            for u in range(2):
                norms[u].act_rstd(act, t + behind)
            for u in range(2):
                norms[u].wait_scaled(act, t + behind)
                for c in range(C):
                    y = norms[u].yc[:, c, :]
                    o = X[:, c, bass.ds(t * (2 * N) + u * N, N)] if gqa else y
                    act.activation(o, y, ACT.Identity, bias=vec_(bet, c), scale=vec_(gam, c)).then_inc(aff.sem, 1)
            if not gqa:
                for q in range(8):
                    act.wait_ge(fcp.sem, fcp.at(t, q + 1))
                    for m in range(4):
                        j = (q % 4) * 4 + m
                        act.activation(hid[q // 4][:, j, :], part(2 + q % 2, m), GELU,
                                       bias=vec[:, 9 + j // 4, j % 4:j % 4 + 1]).then_inc(gel.sem, 1)

    def gpsimd(pool):
        for u in range(2):
            pool.wait_ge(qd[u].sem, qd[u].at(pairs))
        with pool.Fori(0, TURNS) as t:
            pool.wait_ge(sc_.sem, sc_.at(t))
            for u in range(2):
                for h in range(NQ):
                    pool.tensor_tensor(qm[u][:, h], qT[:, :, bass.ds(t * (2 * L) + u * L, L)],
                                       hm[:, h:h + 1].unsqueeze(2).broadcast_to([P, C, L]), ALU.mult).then_inc(qmd.sem, 1)

    last = aff if gqa else fin
    return Layer(sync, tensor, vector, scalar, gpsimd, (last.sem, last.at(pairs)))



def cols(v):
    return np.ascontiguousarray(v.reshape(C, P).T)


def rows(w):
    return w.reshape(-1, P, w.shape[1]).transpose(1, 0, 2)


PERM = np.arange(D).reshape(C, HC, HS).transpose(0, 2, 1).reshape(-1)


def pack(parts):
    outs = []
    for a in parts:
        a = a.reshape(a.shape[0], -1)
        n = -(-a.shape[1] // 8) * 8
        b = np.zeros((P, n), np.float32)
        b[:a.shape[0], :a.shape[1]] = a
        outs.append(b)
    return np.concatenate(outs, 1)


def rwkv_weights(d, n, ctx):
    w = {k[len(f"L{n}_xattn_"):]: v for k, v in d.items() if k.startswith(f"L{n}_xattn_")}
    parts = [rows(w["Wr"].T), rows(w["Wk"].T), rows(w["Wv"].T[:, PERM]), rows(w["Wg"].T[:, PERM]),
             rows(w["Wo"].T[PERM]), rows(w["Wfr"].T), rows(w["Wfk"].T), rows(w["Wfv"].T), rows(w["maa_w1"])]
    w2 = np.zeros((P, 4, D), np.float32)
    for f in range(4):
        w2[DM * f:DM * f + DM, f] = w["maa_w2"][f]
    parts += [w2, w["maa_w2"][4], rows(w["td_w1"]), w["td_w2"]]
    u = np.broadcast_to(w["u"].reshape(-1), (D,))
    table = {"ln1_w": w["ln1_w"], "ln1_b": w["ln1_b"], "maa_x": w["maa_x"], "time_decay": w["time_decay"], "u": u,
             "gn_w": w["gn_w"][PERM], "gn_b": w["gn_b"][PERM], "ln2_w": w["ln2_w"], "ln2_b": w["ln2_b"],
             "ffn_maa_k": w["ffn_maa_k"], "ffn_maa_r": w["ffn_maa_r"], "zero": np.zeros(D, np.float32)}
    for f in range(5):
        table[f"stack{f}"] = w["maa_stack"].reshape(5, D)[f]
    parts.append(np.stack([cols(table[k]) for k in VEC], 1))
    s0 = ctx[:, 2:2 + HS].reshape(B, C, P, HS)
    parts.append(s0.transpose(2, 1, 3, 0))
    return pack(parts)


def constants(ctx):
    p = np.arange(P)
    ident = np.eye(P, dtype=np.float32)
    mean_w = np.full((P, P), 1 / D, np.float32)
    gmean = (p[:, None] % HC == p[None, :] % HC).astype(np.float32) / HS
    heads = (p[:, None] // HS == p[None, :] % HC).astype(np.float32)
    red = np.zeros((P, 56), np.float32)
    red[p, 24 + p // HS] = 1
    hm = (p[:, None] // 16 == np.arange(8)[None]).astype(np.float32)
    qm = (p[:, None] // 32 == np.arange(4)[None]).astype(np.float32)
    eps = np.broadcast_to(np.array([1e-5, 1e-6], np.float32), (P, 2))
    st = ctx[:, 0:2].reshape(B, 2, C, P).transpose(3, 2, 1, 0)
    return pack([ident, mean_w, gmean, heads, red, hm, qm, eps, st])


def spread():
    p, j = np.arange(P), np.arange(HS)
    return pack([(p[:, None, None] == HC * j[:, None] + p // HS).astype(np.float32)])


def attention_weights(w, names, q_perm, o_perm, vectors, fc_b=None):
    q, k, v, o = (w[n] for n in names)
    vec = np.zeros((P, 26, C), np.float32)
    for j, b in enumerate(vectors):
        c = b.reshape(-1, P).T
        vec[:, j, :c.shape[1]] = c
    if fc_b is not None:
        vec[:, 9:13] = fc_b.reshape(C, C, P).transpose(2, 0, 1)
    return pack([rows(o[o_perm]), vec, rows(q[:, q_perm]), rows(k), rows(v)])


GQA = np.arange(D).reshape(8, 4, 16).transpose(1, 0, 2).reshape(-1)


def lay_out(inputs):
    d = {k: np.asarray(v) for k, v in inputs.items()}
    ctx = d["ctx_2048"]
    w0 = {k[9:]: v for k, v in d.items() if k.startswith("L0_xattn_")}
    w2 = {k[9:]: v for k, v in d.items() if k.startswith("L2_xattn_")}
    same = np.arange(D)
    return {
        "ctxT": np.ascontiguousarray(ctx.reshape(B, S, C, P).transpose(0, 3, 2, 1)),
        "mask0": np.ascontiguousarray(d["mask_Bx1xSxS2_ff0"].reshape(B, L, S)),
        "mask2": np.ascontiguousarray(d["mask_BxS2_bf1"]),
        "L0_w": attention_weights(w0, ("Wq", "Wk", "Wv", "Wo"), GQA, GQA,
                                  [w0["bq"][GQA], w0["bk"], w0["bv"], w0["bo"], w0["gamma"], w0["beta"]]),
        "L2_w": attention_weights(w2, ("q_w", "k_w", "v_w", "cproj_w"), same, same,
                                  [w2[n] for n in ("ln1_w", "ln1_b", "q_b", "k_b", "v_b", "cproj_b", "ln2_w", "ln2_b",
                                                   "proj_b")], w2["fc_b"]),
        "L2_fc": pack([rows(w2["fc_w"])]),
        "L2_pj": pack([rows(w2["proj_w"])]),
        "xT": np.ascontiguousarray(d["x"].reshape(T, C, P).transpose(2, 1, 0)).reshape(P, C * T),
        "const": constants(ctx),
        "spread": spread(),
        "L1_w": rwkv_weights(d, 1, ctx),
        "L3_w": rwkv_weights(d, 3, ctx),
    }


LAYERS = (0, 1, 2, 3)


def kernel(**inputs):
    import concourse.bacc as _bacc
    from concourse.bass_utils import run_bass_kernel_spmd as _run

    nc = _bacc.Bacc("TRN2", target_bir_lowering=False, num_devices=1)
    arrays = lay_out(inputs)
    dram = {n: nc.dram_tensor(n, a.shape, mybir.dt.from_np(a.dtype), kind="ExternalInput").ap()
            for n, a in arrays.items()}
    out = nc.dram_tensor("outT", [P, C * T], F32, kind="ExternalOutput").ap()
    program(nc, dram, out, LAYERS)
    r = _run(nc, [arrays], core_ids=[0])
    got = np.asarray(r.results[0]["outT"])
    return np.ascontiguousarray(got.reshape(P, C, T).transpose(2, 1, 0)).reshape(B, L, D)
```

```python
from contextlib import ExitStack

import numpy as np

import concourse.bass as bass
from concourse import mybir

F32 = mybir.dt.float32
F32R = mybir.dt.float32r
MASK = mybir.dt.from_np(np.dtype(bool))
ALU = mybir.AluOpType
ACT = mybir.ActivationFunctionType

B, L, S, D = 16, 100, 361, 512
P = 128
C = D // P
T = B * L
NB = 2
N = NB * L
G = B // NB
E = L + 1
HS = 16
HC = P // HS
DM, DD = 32, 64
F = 2048
SC = [(0, 128), (128, 128), (256, S - 256)]
FLT = float(np.finfo(np.float32).max)
ARENA = 49552
GELU = ACT.Gelu_apprx_tanh


class Signal:

    def __init__(self, sem, per):
        self.sem, self.per = sem, per

    def at(self, i, n=0):
        return i * self.per + n + 1


def ds(i, n):
    return bass.ds(i * n, n)


class Region:

    def __init__(self, arena, start):
        self.arena, self.at = arena, start

    def take(self, *shape):
        n = int(np.prod(shape))
        v = self.arena[:, self.at:self.at + n]
        self.at += (n + 7) // 8 * 8
        assert self.at <= ARENA, self.at
        if len(shape) == 2:
            v = v.rearrange("p (a b) -> p a b", a=shape[0])
        elif len(shape) == 3:
            v = v.rearrange("p (a b c) -> p a b c", a=shape[0], b=shape[1])
        elif len(shape) == 4:
            v = v.rearrange("p (a b c d) -> p a b c d", a=shape[0], b=shape[1], c=shape[2])
        return v


class Core:

    def __init__(self, nc, ctx, dram):
        self.nc, self.ctx, self.dram, self.signals = nc, ctx, dram, []
        self.arena = ctx.enter_context(nc.sbuf_tensor("arena", [P, ARENA], F32))
        r = Region(self.arena, 0)
        self.X = r.take(C, T)
        self.ident = r.take(P)
        self.mean_w = r.take(P)
        self.gmean_w = r.take(P)
        self.heads_w = r.take(P)
        self.red_w = r.take(56)
        self.hmask = r.take(8)
        self.qmask = r.take(4)
        self.epsc = r.take(2)
        self.st = r.take(C, 2, B)
        self.own = r.at
        self.psum = ctx.enter_context(nc.psum_tensor("psum", [P, 8, 512], F32))
        self.bank = [self.psum[:, i, :] for i in range(8)]
        self.wide = [self.psum[:, 2 * i:2 * i + 2, 0:2 * N] for i in range(4)]
        self.input_head = self.new_signal("input_head", 16)
        self.input_rest = self.new_signal("input_rest", 48)
        self.constants = self.new_signal("constants", 16)
        self.stored = self.new_signal("stored", 16)

    def new_signal(self, name, per=1):
        self.signals.append(Signal(self.ctx.enter_context(self.nc.semaphore(name)), per))
        return self.signals[-1]

    def part(self, w, m, rows=P):
        return self.psum[0:rows, 2 * w + m // 2, (m % 2) * N:(m % 2) * N + N]

    def load(self, sp, quarters):
        x = self.dram["xT"].rearrange("p (c t) -> p c t", c=C)
        for q in quarters:
            tokens = slice(q * 2 * N, (q + 1) * 2 * N)
            told = self.input_rest if q else self.input_head
            sp.dma_start(self.X[:, :, tokens], x[:, :, tokens]).then_inc(told.sem, 16)
            if q == 1:
                sp.dma_start(self.arena[:, C * T:self.own], self.dram["const"]).then_inc(self.constants.sem, 16)

    def load_weights(self, sp, after, spans, source, told):
        waited = 0
        for n, (a, b) in enumerate(spans):
            if after:
                if b <= after.left and waited == 0:
                    sp.wait_ge(*after.early)
                    waited = 1
                if b > after.left and waited < 2:
                    sp.wait_ge(*after.done)
                    waited = 2
            sp.dma_start(self.arena[:, a:b], source(a, b)).then_inc(told(n), 16)
        if after and waited < 2:
            sp.wait_ge(*after.done)
        if not after:
            self.load(sp, (1, 2, 3))

    def lead(self, sp):
        for s in self.signals:
            sp.sem_inc(s.sem, 1)

    def wait_before(self, eng, after):
        if after:
            eng.wait_ge(*after.done)
        else:
            eng.wait_ge(self.input_head.sem, self.input_head.at(1))
            eng.wait_ge(self.input_rest.sem, self.input_rest.at(1))
            eng.wait_ge(self.constants.sem, self.constants.at(1))


class Layer:

    def __init__(self, sync, tensor, vector, scalar, gpsimd, done, early, left, pieces):
        self.sync, self.tensor, self.vector, self.scalar, self.gpsimd = sync, tensor, vector, scalar, gpsimd
        self.done, self.early, self.left, self.pieces = done, early, left, pieces


def two(v):
    return v.rearrange("p (a b) n -> p a (b n)", a=2)


def program(nc, dram, out_dram, layers=(0, 1, 2, 3)):
    with ExitStack() as ctx:
        core = Core(nc, ctx, dram)
        shared = RwkvMemory(core)
        stack, after = [], None
        for n in layers:
            if n % 2 == 0:
                stack.append(attention(core, f"L{n}", after))
            else:
                stack.append(rwkv(core, shared, f"L{n}", 0 if n == 1 else G, after))
            after = stack[-1]
        block = ctx.enter_context(nc.Block())

        @block.sync
        def _(sp):
            core.load(sp, (0,))
            core.lead(sp)
            for layer in stack:
                layer.sync(sp)
            n, done = after.pieces
            x = out_dram.rearrange("p (c t) -> p c t", c=C)
            with sp.Fori(0, n) as g:
                sp.wait_ge(*done(g))
                sp.dma_start(x[:, :, ds(g, T // n)], core.X[:, :, ds(g, T // n)]).then_inc(core.stored.sem, 16)
            sp.wait_ge(core.stored.sem, core.stored.at(n))

        @block.gpsimd
        def _(pool):
            for layer in stack:
                layer.gpsimd(pool)

        @block.tensor
        def _(pe):
            for layer in stack:
                layer.tensor(pe)

        @block.vector
        def _(dve):
            for layer in stack:
                layer.vector(dve)

        @block.scalar
        def _(act):
            for layer in stack:
                layer.scalar(act)



def norm_signals(core, name, per=2):
    return [core.new_signal(f"{name}_{n}", per) for n in ("mu", "cen", "sq", "var", "lnv", "rstd", "nrm")]


class Norm:

    def __init__(self, core, told, nth, w, eps):
        self.core, self.nth, self.w, self.eps = core, nth + 1, w, eps
        self.mu, self.cen, self.sq, self.var, self.lnv, self.rstd, self.nrm = told

    def memory(self, r, rs=None):
        self.yc, self.s2 = r.take(C, N), r.take(C, N)
        self.rs = r.take(N) if rs is None else rs
        return self

    def pe_mean(self, pe, src, i):
        for c in range(C):
            mm = pe.matmul(self.core.part(self.w, 0), self.core.mean_w, src(c), start=c == 0, stop=c == C - 1)
        mm.then_inc(self.mu.sem, 1)

    def dve_center(self, dve, src, i):
        dve.wait_ge(self.mu.sem, self.mu.at(i, self.nth))
        mu = self.core.part(self.w, 0).unsqueeze(1).broadcast_to([P, C, N])
        dve.tensor_tensor(self.yc, src, mu, ALU.subtract).then_inc(self.cen.sem, 1)

    def act_square(self, act, i):
        act.wait_ge(self.cen.sem, self.cen.at(i, self.nth))
        act.activation(self.s2, self.yc, ACT.Square).then_inc(self.sq.sem, 1)

    def pe_var(self, pe, i):
        pe.wait_ge(self.sq.sem, self.sq.at(i, self.nth))
        for c in range(C):
            mm = pe.matmul(self.core.part(self.w, 2), self.core.mean_w, self.s2[:, c, :], start=c == 0,
                           stop=c == C - 1)
        mm.then_inc(self.var.sem, 1)

    def act_rstd(self, act, i):
        act.wait_ge(self.var.sem, self.var.at(i, self.nth))
        act.activation(self.rs, self.core.part(self.w, 2), ACT.Ln,
                       bias=self.core.epsc[:, self.eps:self.eps + 1]).then_inc(self.lnv.sem, 1)
        act.wait_ge(self.lnv.sem, self.lnv.at(i, self.nth))
        act.activation(self.rs, self.rs, ACT.Exp, scale=-0.5).then_inc(self.rstd.sem, 1)

    def scale(self, eng, i):
        eng.wait_ge(self.rstd.sem, self.rstd.at(i, self.nth))
        rs = self.rs.unsqueeze(1).broadcast_to([P, C, N])
        eng.tensor_tensor(self.yc, self.yc, rs, ALU.mult).then_inc(self.nrm.sem, 1)

    def wait_scaled(self, eng, i):
        eng.wait_ge(self.nrm.sem, self.nrm.at(i, self.nth))


def project(pe, core, w, weight, src, k_chunks=C, m_chunks=range(C)):
    for m in m_chunks:
        for k in range(k_chunks):
            mm = pe.matmul(core.part(w, m), weight[:, k, m * P:(m + 1) * P], src(k), start=k == 0,
                           stop=k == k_chunks - 1)
    return mm



VEC = ["ln1_w", "ln1_b", "maa_x", "stack0", "stack1", "stack2", "stack3", "stack4", "time_decay", "u", "gn_w",
       "gn_b", "ln2_w", "ln2_b", "ffn_maa_k", "ffn_maa_r", "zero"]
RWKV_SIGNALS = dict(
    weights=16 * 5, weights_back=16 * 4, spread_in=16, spread=1, decay_zeros=2,
    state1_in_xs=1, xa=4, shift=1, xa_shifted=4, mix_hidden_sum=1, mix_hidden=2, mix_sum=5, mix_term=20, mixed=5,
    r_sum=1, k_sum=1, v_sum=1, gate_sum=1, decay_hidden_sum=1, decay_sum=1, r=1, k=1, v=2, v_low=1, gate_tanh=1,
    gate=1, decay_hidden=1, decay_rate=4, decay=4, ruk=4, bonus_sum=1, bonus=1,
    v_spread=16, ring_start=16, kv=16, states=16, r_states=16, r_states_sum=8,
    head_out=1, head_mean=1, head_centred=1, head_squares=1, head_var=1, head_log_var=1, head_rstd=1,
    head_normed=1, head_affine=4, gated=1, out_sum=1, x1=1,
    state0_in_xs2=1, xc=4, shift2=1, ffn_mix=8, ffn_r_sum=1, ffn_k_sum=1, ffn_tanh=1, ffn_relu=1, ffn_squared=1,
    ffn_v_sum=1, ffn_gated=1, group_done=1)


class RwkvMemory:

    def __init__(self, core):
        r = Region(core.arena, core.own)
        start = r.at
        self.W = {}
        for n in ("r", "k", "v", "g"):
            self.W[n] = r.take(C, D)
        self.w1 = r.take(C, 5 * DM)
        self.w2 = r.take(4, D)
        self.w2b = r.take(D)
        self.td1 = r.take(C, DD)
        self.td2 = r.take(D)
        self.vec = r.take(17, C)
        middle = r.at
        self.s0 = r.take(C, 16, B)
        for n in ("o", "fr", "fk", "fv"):
            self.W[n] = r.take(C, D)
        self.start, q = start, C * D
        cuts = [start, start + q, start + 2 * q, start + 3 * q, start + 4 * q, middle]
        self.front_spans = list(zip(cuts[:-1], cuts[1:]))
        cuts = [middle + (r.at - middle) * n // 4 for n in range(5)]
        self.back_spans = list(zip(cuts[:-1], cuts[1:]))
        self.left_early = start + 4 * q + C * 5 * DM
        self.n1 = Norm(core, norm_signals(core, "rw1", 1), 0, 2, 0).memory(r)
        self.xs = r.take(C, NB, E)
        self.sx, self.xx = r.take(C, N), r.take(C, N)
        self.tha, self.thb, self.tdh = r.take(N), r.take(N), r.take(N)
        self.xm = [r.take(C, N) for _ in range(5)]
        self.rk, self.gt, self.e1 = self.xx, self.n1.s2, self.xm[1]
        self.r, self.k, self.v, self.g, self.bon = (r.take(C, N) for _ in range(5))
        self.we = r.take(2, 4, NB * E)
        self.ring_at = r.at
        self.ring = [r.take(4, NB * E) for _ in range(4)]
        self.n2 = Norm(core, norm_signals(core, "rw2", 1), 0, 1, 0).memory(r, self.n1.rs)
        self.xs2 = r.take(C, NB, E)
        self.thr = r.take(C, N)
        a, b, c, d = (v.rearrange("p a b -> p (a b)")[:, 0:C * N].rearrange("p (c n) -> p c n", c=C) for v in self.ring)
        self.og, self.oc, self.osq, self.ors, self.og2 = a, self.n2.yc, self.n2.s2, b, c
        self.sx2, self.xk2, self.xr2, self.ff, self.kk = d, a, self.n2.yc, c, self.n2.s2
        self.v_high, self.v_low = (core.ctx.enter_context(core.nc.sbuf_tensor(n, [P, C, N], F32R))
                                   for n in ("v_high", "v_low"))
        self.spread_w = core.ctx.enter_context(core.nc.sbuf_tensor("spread_w", [P, HS, P], F32R))
        self.spread_in = core.arena[:, self.ring_at:self.ring_at + HS * P]
        self.s = {n: core.new_signal("rw_" + n, per) for n, per in RWKV_SIGNALS.items()}


def rwkv(core, m, name, base, after):
    X, part, wide, dram, psum = core.X, core.part, core.wide, core.dram, core.psum

    def vec(n, c):
        j = VEC.index(n)
        return m.vec[:, j, c:c + 1]

    def wait(eng, n, i, k=0):
        eng.wait_ge(m.s[n].sem, m.s[n].at(i, k))

    def sem(n):
        return m.s[n].sem

    def xg(g):
        return X[:, :, ds(g, N)]

    def seq(v):
        return v.rearrange("p c (b t) -> p c b t", b=NB)

    def pairs(v, cc):
        return v[:, 2 * cc:2 * cc + 2, :].rearrange("p c (b t) -> p (c b) t", b=NB)

    def item(n):
        cc, q, odd = n // 8, n % 8 // 2, n % 2
        return cc, q, 8 * odd + q, 2 * odd

    def sync(sp):
        n = len(m.front_spans)
        core.load_weights(sp, after, m.front_spans + m.back_spans,
                          lambda a, b: dram[name + "_w"][:, a - m.start:b - m.start],
                          lambda k: sem("weights" if k < n else "weights_back"))
        if occ == 0:
            sp.dma_start(m.spread_in, dram["spread"]).then_inc(sem("spread_in"), 16)

    occ = base // G

    def turns(eng, body):
        core.wait_before(eng, after)
        wait(eng, "weights", occ + 1)
        body(base - 1, -1, back=False, front=True, tail=False)
        wait(eng, "weights_back", occ + 1)
        body(base, 0, back=True, front=True, tail=False)
        with eng.Fori(1, G - 1) as g:
            body(g + base, g, back=True, front=True, tail=True)
        body(base + G - 1, G - 1, back=True, front=False, tail=True)
        body(base + G, G, back=False, front=False, tail=True)

    def tensor(pe):
        def body(i, g, back, front, tail):
            f_ = i + 1

            def mix(f):
                w = (2, 2, 2, 3, 3)[f]
                for c in range(C):
                    if f < 4:
                        mm = pe.matmul(part(w, c), m.w2[:, f, c * P:(c + 1) * P], m.tha, start=True, stop=True)
                    else:
                        mm = pe.matmul(part(w, c), m.w2b[0:DM, c * P:(c + 1) * P], m.thb[0:DM, :], start=True,
                                       stop=True)
                mm.then_inc(sem("mix_sum"), 1)

            def spread(i, n):
                cc, _, j0, _ = item(n)
                w = (n + 1) % 2
                for h in range(2):
                    sel = m.spread_w[:, j0 + 4 * h, :]
                    o = psum[:, 2 * w + h, 0:2 * N]
                    for v, first in ((m.v_high, True), (m.v_low, False)):
                        mv = v[:, 2 * cc:2 * cc + 2, :].rearrange("p c n -> p (c n)")
                        mm = pe.matmul(o, sel, mv, start=first, stop=not first)
                mm.then_inc(sem("v_spread"), 1)

            def reduce(pair):
                wait(pe, "r_states", i, 2 * pair + 2)
                for n in (2 * pair, 2 * pair + 1):
                    cc, q, _, t0 = item(n)
                    rv = m.ring[n % 4].rearrange("p (h c) (b e) -> p h (c b) e", h=2, b=NB)
                    for h in range(2):
                        r0 = 32 * (t0 + h)
                        mm = pe.matmul(psum[r0:r0 + 32, 6 + cc, 0:2 * N], core.red_w[:, 24 - 8 * q:56 - 8 * q],
                                       rv[:, h, :, 0:L], start=q == 0, stop=q == 3)
                mm.then_inc(sem("r_states_sum"), 1)

            for n in range(17):
                if back and 2 <= n < 16:
                    wait(pe, "kv", i, n - 1)
                    spread(i, n)
                if tail and n == 2:
                    wait(pe, "ffn_tanh", i)
                    wait(pe, "ffn_squared", i)
                    project(pe, core, 3, m.W["fv"], lambda k: m.kk[:, k, :], m_chunks=(0, 1))
                if tail and n == 3:
                    project(pe, core, 3, m.W["fv"], lambda k: m.kk[:, k, :], m_chunks=(2, 3)).then_inc(
                        sem("ffn_v_sum"), 1)
                if back and n == 4:
                    wait(pe, "bonus", i, 1)
                    wait(pe, "ffn_gated", i)
                if back and n >= 4 and n % 2 == 0 and n < 16:
                    reduce(n // 2 - 2)
                if front and n == 1:
                    wait(pe, "gate", f_)
                    m.n1.pe_mean(pe, lambda c: X[:, c, ds(g + 1, N)], f_)
                if front and n == 4:
                    m.n1.pe_var(pe, f_)
                if front and n == 10:
                    wait(pe, "xa_shifted", f_, 4)
                    for k in range(C):
                        pe.matmul(part(2, 0), m.w1[:, k, 0:P], m.xx[:, k, :], start=k == 0, stop=k == C - 1)
                    for k in range(C):
                        mm = pe.matmul(part(2, 2, DM), m.w1[:, k, P:P + DM], m.xx[:, k, :], start=k == 0,
                                       stop=k == C - 1)
                    mm.then_inc(sem("mix_hidden_sum"), 1)
                if front and n == 11:
                    wait(pe, "mix_hidden", f_, 2)
                    mix(0)
                if front and n == 13:
                    wait(pe, "mix_term", f_, 4)
                    mix(1)
            if front:
                wait(pe, "mixed", f_, 1)
                wait(pe, "mix_term", f_, 8)
                project(pe, core, 2, m.W["k"], lambda k: m.xm[0][:, k, :], m_chunks=(0, 1))
            if back:
                reduce(6)
                reduce(7)
            if front:
                project(pe, core, 2, m.W["k"], lambda k: m.xm[0][:, k, :], m_chunks=(2, 3)).then_inc(sem("k_sum"), 1)
            if back:
                wait(pe, "head_out", i, 1)
                for c in range(C):
                    mm = pe.matmul(part(0, c), core.gmean_w, m.og[:, c, :], start=True, stop=True)
                mm.then_inc(sem("head_mean"), 1)
            if front:
                wait(pe, "mixed", f_, 2)
                for k in range(C):
                    mm = pe.matmul(part(3, 0, DD), m.td1[:, k, :], m.xm[1][:, k, :], start=k == 0, stop=k == C - 1)
                mm.then_inc(sem("decay_hidden_sum"), 1)
            if back:
                wait(pe, "head_squares", i, 1)
                for c in range(C):
                    mm = pe.matmul(part(1, c), core.gmean_w, m.osq[:, c, :], start=True, stop=True)
                mm.then_inc(sem("head_var"), 1)
            if front:
                wait(pe, "k", f_, 1)
                mix(2)
                wait(pe, "decay_hidden", f_, 1)
                mix(3)
                wait(pe, "mix_term", f_, 12)
                for c in range(C):
                    mm = pe.matmul(part(2, c), m.td2[0:DD, c * P:(c + 1) * P], m.tdh[0:DD, :], start=True, stop=True)
                mm.then_inc(sem("decay_sum"), 1)
                wait(pe, "mix_term", f_, 16)
                mix(4)
            if back:
                wait(pe, "gated", i, 1)
                project(pe, core, 0, m.W["o"], lambda k: m.og2[:, k, :]).then_inc(sem("out_sum"), 1)
            if front:
                wait(pe, "mixed", f_, 3)
                wait(pe, "decay_rate", f_, 4)
                project(pe, core, 2, m.W["v"], lambda k: m.xm[2][:, k, :], m_chunks=(0, 1))
            if back:
                wait(pe, "x1", i, 1)
                m.n2.pe_mean(pe, lambda c: X[:, c, ds(g, N)], i)
            if front:
                project(pe, core, 2, m.W["v"], lambda k: m.xm[2][:, k, :], m_chunks=(2, 3)).then_inc(sem("v_sum"), 1)
            if back:
                m.n2.pe_var(pe, i)
            if front:
                wait(pe, "mixed", f_, 4)
                wait(pe, "mix_term", f_, 20)
                project(pe, core, 3, m.W["r"], lambda k: m.xm[3][:, k, :]).then_inc(sem("r_sum"), 1)
                wait(pe, "mixed", f_, 5)
                wait(pe, "v", f_, 2)
                project(pe, core, 2, m.W["g"], lambda k: m.xm[4][:, k, :]).then_inc(sem("gate_sum"), 1)
            if back:
                wait(pe, "ffn_mix", i, 4)
                project(pe, core, 0, m.W["fk"], lambda k: m.xk2[:, k, :]).then_inc(sem("ffn_k_sum"), 1)
            if front:
                wait(pe, "r", f_, 1)
                wait(pe, "ruk", f_, 4)
                for c in range(C):
                    mm = pe.matmul(part(3, c), core.heads_w, m.rk[:, c, :], start=True, stop=True)
                mm.then_inc(sem("bonus_sum"), 1)
            if front:
                wait(pe, "v_low", f_, 1)
                pe.wait_ge(sem("spread"), m.s["spread"].at(1))
                if back:
                    pe.wait_ge(m.n2.lnv.sem, m.n2.lnv.at(i, 1))
                spread(f_, 0)
                if back:
                    wait(pe, "ffn_relu", i, 1)
                spread(f_, 1)
            if back:
                wait(pe, "ffn_mix", i, 8)
                if front:
                    wait(pe, "bonus", f_, 1)
                project(pe, core, 3, m.W["fr"], lambda k: m.xr2[:, k, :]).then_inc(sem("ffn_r_sum"), 1)

        turns(pe, body)

    def vector(dve):
        def body(i, g, back, front, tail):
            f_ = i + 1

            def mix_term(f):
                wait(dve, "mix_sum", f_, f + 1)
                for c in range(C):
                    dve.scalar_tensor_tensor(m.xm[f][:, c, :], part((2, 2, 2, 3, 3)[f], c), vec(f"stack{f}", c),
                                             m.sx[:, c, :], ALU.add, ALU.mult).then_inc(sem("mix_term"), 1)

            def step(n):
                cc, _, j0, _ = item(n)
                if n >= 4:
                    wait(dve, "r_states_sum", i, (n - 4) // 2 + 1)
                wait(dve, "v_spread", i, n + 1)
                w = (n + 1) % 2
                kb = pairs(m.k, cc).unsqueeze(1).broadcast_to([P, 2, 2 * NB, L])
                vb = psum[:, 2 * w:2 * w + 2, 0:2 * N].rearrange("p h (a t) -> p h a t", t=L)
                dst = m.ring[n % 4].rearrange("p (h c) (b e) -> p h (c b) e", h=2, b=NB)[:, :, :, 1:E]
                dve.tensor_tensor(dst, kb, vb, ALU.mult).then_inc(sem("kv"), 1)
                wait(dve, "kv", i, n + 1)
                wait(dve, "ring_start", i, n + 1)
                if n % 8 == 0:
                    wait(dve, "decay", i, 2 * cc + 2)
                flat = m.ring[n % 4].rearrange("p j e -> p (j e)")
                dve.tensor_tensor_scan(flat, m.we[:, cc].rearrange("p j e -> p (j e)"), flat, 0.0,
                                       ALU.mult, ALU.add).then_inc(sem("states"), 1)

            for n in range(16):
                if back:
                    step(n)
                if tail and n == 3:
                    wait(dve, "ffn_tanh", i)
                    wait(dve, "ffn_v_sum", i)
                    dve.scalar_tensor_tensor(two(m.thr), two(m.thr), 1.0, wide[3], ALU.add, ALU.mult).then_inc(
                        sem("ffn_gated"), 1)
                    wait(dve, "ffn_gated", i)
                    dve.scalar_tensor_tensor(xg(g - 1), m.thr, 0.5, xg(g - 1), ALU.mult, ALU.add).then_inc(
                        sem("group_done"), 1)
                if front and n == 1:
                    dve.tensor_copy(m.xs[:, :, :, 0], core.st[:, :, 1, ds(g + 1, NB)]).then_inc(sem("state1_in_xs"), 1)
                    m.n1.dve_center(dve, xg(g + 1), f_)
                if front and n == 5:
                    m.n1.scale(dve, f_)
                if front and n == 8:
                    wait(dve, "state1_in_xs", f_, 1)
                    wait(dve, "xa", f_, 4)
                    dve.tensor_tensor(seq(m.sx), m.xs[:, :, :, 0:L], m.xs[:, :, :, 1:E],
                                      ALU.subtract).then_inc(sem("shift"), 1)
                    wait(dve, "shift", f_, 1)
                    for c in range(C):
                        dve.scalar_tensor_tensor(seq(m.xx)[:, c], seq(m.sx)[:, c], vec("maa_x", c), m.xs[:, c, :, 1:E],
                                                 ALU.mult, ALU.add).then_inc(sem("xa_shifted"), 1)
                if front and n == 11:
                    mix_term(0)
                if front and n == 13:
                    mix_term(1)
            if back:
                wait(dve, "r_states_sum", i, 8)
                dve.tensor_tensor(two(m.og), wide[3], two(m.bon), ALU.add).then_inc(sem("head_out"), 1)
                wait(dve, "head_out", i, 1)
                wait(dve, "head_mean", i, 1)
                dve.tensor_tensor(two(m.oc), two(m.og), wide[0], ALU.subtract).then_inc(sem("head_centred"), 1)
            if front:
                wait(dve, "k_sum", f_, 1)
                dve.tensor_copy(two(m.k), wide[2]).then_inc(sem("k"), 1)
                mix_term(2)
            if back:
                wait(dve, "head_rstd", i, 1)
                dve.tensor_tensor(m.oc, m.oc, m.ors, ALU.mult).then_inc(sem("head_normed"), 1)
            if front:
                mix_term(3)
            if back:
                wait(dve, "head_affine", i, 4)
                dve.scalar_tensor_tensor(m.og2, m.oc, 0.5, m.g, ALU.mult, ALU.mult).then_inc(sem("gated"), 1)
                wait(dve, "out_sum", i, 1)
                dve.tensor_tensor(xg(g), psum[:, 0:2, 0:2 * N].rearrange("p a (b n) -> p a b n", b=2), xg(g),
                                  ALU.add).then_inc(sem("x1"), 1)
            if front:
                mix_term(4)
            if back:
                wait(dve, "x1", i, 1)
                m.n2.dve_center(dve, xg(g), i)
                dve.tensor_copy(m.xs2[:, :, :, 0], core.st[:, :, 0, ds(g, NB)]).then_inc(sem("state0_in_xs2"), 1)
            if front:
                wait(dve, "v", f_, 2)
                dve.tensor_tensor(m.v_low[:], m.v, m.v_high[:].bitcast(F32), ALU.subtract).then_inc(sem("v_low"), 1)
            if back:
                m.n2.scale(dve, i)
                wait(dve, "state0_in_xs2", i, 1)
                wait(dve, "xc", i, 4)
                dve.tensor_tensor(seq(m.sx2), m.xs2[:, :, :, 0:L], m.xs2[:, :, :, 1:E],
                                  ALU.subtract).then_inc(sem("shift2"), 1)
                wait(dve, "shift2", i, 1)
                for v, n in ((m.xk2, "ffn_maa_k"), (m.xr2, "ffn_maa_r")):
                    for c in range(C):
                        dve.scalar_tensor_tensor(seq(v)[:, c], seq(m.sx2)[:, c], vec(n, c), m.xs2[:, c, :, 1:E],
                                                 ALU.mult, ALU.add).then_inc(sem("ffn_mix"), 1)
            if front:
                wait(dve, "r_sum", f_, 1)
                dve.tensor_copy(two(m.r), wide[3]).then_inc(sem("r"), 1)
                wait(dve, "k", f_, 1)
                wait(dve, "r", f_, 1)
                for c in range(C):
                    dve.scalar_tensor_tensor(m.rk[:, c, :], m.r[:, c, :], vec("u", c), m.k[:, c, :],
                                             ALU.mult, ALU.mult).then_inc(sem("ruk"), 1)
                wait(dve, "gate_tanh", f_, 1)
                dve.scalar_tensor_tensor(two(m.g), two(m.gt), 1.0, wide[2], ALU.add, ALU.mult).then_inc(sem("gate"), 1)
            if back:
                wait(dve, "ffn_relu", i, 1)
                dve.tensor_tensor(m.kk, m.ff, m.ff, ALU.mult).then_inc(sem("ffn_squared"), 1)
            if front:
                wait(dve, "bonus_sum", f_, 1)
                dve.tensor_tensor(two(m.bon), wide[3], two(m.v), ALU.mult).then_inc(sem("bonus"), 1)
        core.wait_before(dve, after)
        if occ == 0:
            dve.wait_ge(sem("spread_in"), m.s["spread_in"].at(1))
            dve.tensor_copy(m.spread_w[:].rearrange("p j n -> p (j n)"), m.spread_in).then_inc(sem("spread"), 1)
        wait(dve, "weights", occ + 1)
        dve.memset(m.we.rearrange("p c j (b e) -> p (c j b) e", b=NB)[:, :, 0:1], 0.0).then_inc(sem("decay_zeros"), 2)
        turns(dve, body)

    def scalar(act):
        def body(i, g, back, front, tail):
            f_ = i + 1

            def start(n, g):
                cc, _, j0, _ = item(n)
                dst = m.ring[n % 4].rearrange("p (h c) (b e) -> p h c b e", h=2, b=NB)[:, :, :, :, 0]
                src = m.s0[:, 2 * cc:2 * cc + 2, j0:j0 + 5:4, ds(g, NB)].rearrange("p c h b -> p h c b")
                act.activation(dst, src, ACT.Copy).then_inc(sem("ring_start"), 1)

            for n in range(16):
                if back and n >= 2:
                    if n == 2:
                        wait(act, "ffn_squared", i)
                    elif n >= 4:
                        wait(act, "r_states_sum", i, (n - 4) // 2 + 1)
                    start(n, g)
                if front and n == 3:
                    m.n1.act_square(act, f_)
                if front and n == 5:
                    m.n1.act_rstd(act, f_)
                if front and n == 7:
                    m.n1.wait_scaled(act, f_)
                    wait(act, "mixed", f_)
                    for c in range(C):
                        act.activation(m.xs[:, c, :, 1:E], seq(m.n1.yc)[:, c], ACT.Identity, bias=vec("ln1_b", c),
                                       scale=vec("ln1_w", c)).then_inc(sem("xa"), 1)
                if front and n == 11:
                    wait(act, "mix_hidden_sum", f_, 1)
                    act.activation(m.tha, part(2, 0), ACT.Tanh).then_inc(sem("mix_hidden"), 1)
                    act.activation(m.thb[0:DM, :], part(2, 2, DM), ACT.Tanh).then_inc(sem("mix_hidden"), 1)
            if back:
                wait(act, "head_centred", i, 1)
                act.activation(m.osq, m.oc, ACT.Square).then_inc(sem("head_squares"), 1)
            if front:
                wait(act, "decay_hidden_sum", f_, 1)
                act.activation(m.tdh[0:DD, :], part(3, 0, DD), ACT.Tanh).then_inc(sem("decay_hidden"), 1)
            if back:
                wait(act, "head_var", i, 1)
                act.activation(two(m.ors), wide[1], ACT.Ln, bias=core.epsc[:, 0:1]).then_inc(sem("head_log_var"), 1)
                wait(act, "head_log_var", i, 1)
                act.activation(m.ors, m.ors, ACT.Exp, scale=-0.5).then_inc(sem("head_rstd"), 1)
                wait(act, "head_normed", i, 1)
                for c in range(C):
                    act.activation(m.oc[:, c, :], m.oc[:, c, :], ACT.Identity, bias=vec("gn_b", c),
                                   scale=vec("gn_w", c)).then_inc(sem("head_affine"), 1)
            if front:
                wait(act, "decay_sum", f_, 1)
                for c in range(C):
                    act.activation(m.e1[:, c, :], part(2, c), ACT.Exp, bias=vec("time_decay", c)).then_inc(
                        sem("decay_rate"), 1)
                wait(act, "decay_zeros", occ + 1)
                wait(act, "decay_rate", f_, 4)
                wait(act, "states", f_)
                for cc in range(2):
                    for h in range(2):
                        dst = m.we[:, cc, 2 * h:2 * h + 2].rearrange("p c (b e) -> p (c b) e", b=NB)[:, :, 1:E]
                        act.activation(dst, pairs(m.e1, cc), ACT.Exp, scale=-1.0).then_inc(sem("decay"), 1)
            if back:
                m.n2.act_square(act, i)
            if front:
                wait(act, "v_sum", f_, 1)
                act.activation(two(m.v), wide[2], ACT.Copy).then_inc(sem("v"), 1)
                act.activation(two(m.v_high[:]), wide[2], ACT.Copy).then_inc(sem("v"), 1)
            if back:
                m.n2.act_rstd(act, i)
                m.n2.wait_scaled(act, i)
                for c in range(C):
                    act.activation(m.xs2[:, c, :, 1:E], seq(m.n2.yc)[:, c], ACT.Identity, bias=vec("ln2_b", c),
                                   scale=vec("ln2_w", c)).then_inc(sem("xc"), 1)
            if front:
                wait(act, "gate_sum", f_, 1)
                act.activation(two(m.gt), wide[2], ACT.Tanh, scale=0.5).then_inc(sem("gate_tanh"), 1)
            if back:
                wait(act, "ffn_k_sum", i, 1)
                act.activation(two(m.ff), wide[0], ACT.Relu).then_inc(sem("ffn_relu"), 1)
            if front:
                if not back:
                    wait(act, "weights_back", occ + 1)
                start(0, g + 1)
                start(1, g + 1)
            if back:
                wait(act, "ffn_r_sum", i, 1)
                wait(act, "group_done", i)
                act.activation(two(m.thr), wide[3], ACT.Tanh, scale=0.5).then_inc(sem("ffn_tanh"), 1)

        turns(act, body)

    def gpsimd(pool):
        def body(i, g, back, front, tail):
            def add_token(f):
                wait(pool, "mix_term", i + 1, 4 * f + 4)
                pool.tensor_tensor(seq(m.xm[f]), seq(m.xm[f]), m.xs[:, :, :, 1:E], ALU.add).then_inc(sem("mixed"), 1)

            if back:
                wait(pool, "r", i, 1)
            for n in range(16):
                if back:
                    sv = m.ring[n % 4].rearrange("p (h c) (b e) -> p h (c b) e", h=2, b=NB)[:, :, :, 0:L]
                    rb = pairs(m.r, n // 8).unsqueeze(1).broadcast_to([P, 2, 2 * NB, L])
                    wait(pool, "states", i, n + 1)
                    pool.tensor_tensor(sv, sv, rb, ALU.mult).then_inc(sem("r_states"), 1)
                if front and n == 12:
                    add_token(0)
            if front:
                for f in range(1, 5):
                    add_token(f)

        turns(pool, body)

    return Layer(sync, tensor, vector, scalar, gpsimd, (sem("group_done"), m.s["group_done"].at(base + G)),
                 (sem("gate_sum"), m.s["gate_sum"].at(base + G)), m.left_early,
                 (G, lambda g: (sem("group_done"), m.s["group_done"].at(g + base, 1))))


def attention(core, name, after):
    X, part, dram, bank, ident = core.X, core.part, core.dram, core.bank, core.ident
    s = lambda n, per=1: core.new_signal(name + "_" + n, per)
    gqa = name == "L0"
    KC = 1 if gqa else C
    KV = KC * P
    NBLK = 8 if gqa else 4
    NB2 = 2 * NBLK
    H = 4 * NB2
    NQ = 8 if gqa else 4
    TURNS = B // 2
    ORDER = (0, 2, 4, 6, 1, 3, 5, 7)
    scale = -1.0 / np.sqrt(D // (32 if gqa else 16))
    hm = core.hmask if gqa else core.qmask
    SUMS = 4 if gqa else NB2

    r = Region(core.arena, core.own)
    start = r.at
    Wq = r.take(C, D)
    Wk = r.take(C, KV)
    Wv = r.take(C, KV)
    left = r.at

    def for_all():
        Wo = r.take(C, D)
        vec = r.take(26, C)
        w_end = r.at
        qT = r.take(C, T)
        told = norm_signals(core, name)
        return Wo, vec, w_end, qT, [Norm(core, told, u, u, 1 if gqa else 0).memory(r) for u in range(2)]

    if not gqa:
        Wo, vec, w_end, qT, norms = for_all()
    over = r.at
    ctxt = [r.take(C, S) for _ in range(2)]
    kT = [r.take(KC, S) for _ in range(2)]
    raw = r.take(S) if gqa else None
    nmask = [r.take(S) for _ in range(2)]
    qm = [r.take(NQ, C, L) for _ in range(2)]
    vs = [r.take(3, NQ if gqa else 4, 32 if gqa else P) for _ in range(2)]
    pr = [r.take(S) for _ in range(8)]
    pT = [r.take(3, 4, L) for _ in range(4)]
    nmx, den, rden, carry = (r.take(H) for _ in range(4))
    if gqa:
        left = r.at
        Wo, vec, w_end, qT, norms = for_all()
    else:
        masks = r.take(B * S // 4).bitcast(MASK)
        r2 = Region(core.arena, over)
        fc = r2.take(C, F)
        pj = r2.take(F // P, D)
        hid = [r2.take(F // P, N) for _ in range(2)]
    w_at = left if gqa else start + C * D + 2 * C * KV
    behind = 0 if gqa else G // 2
    if not gqa:
        yq = [v.rearrange("p a b c -> p (a b c)")[:, 0:C * N].rearrange("p (c n) -> p c n", c=C) for v in qm]
    s2 = [n.s2.rearrange("p c n -> p (c n)") for n in norms]
    sm = [s2[0][:, 0:S], s2[0][:, S:2 * S], s2[1][:, 0:S], s2[1][:, S:2 * S]]

    VN = (["bq", "bk", "bv", "bo", "gamma", "beta"] if gqa else
          ["ln1_w", "ln1_b", "q_b", "k_b", "v_b", "cproj_b", "ln2_w", "ln2_b", "proj_b"])

    def vec_(n, c):
        return vec[:, VN.index(n), c:c + 1]

    bq, bk, bv, bo = ("bq", "bk", "bv", "bo") if gqa else ("q_b", "k_b", "v_b", "cproj_b")
    gam, bet = ("gamma", "beta") if gqa else ("ln2_w", "ln2_b")

    weights = s("weights", 64)
    q_sum = s("q_sum", 2)
    q_ready = [s(f"q_ready{u}", 4) for u in range(2)]
    ctx_in = [s(f"ctx{u}", 16) for u in range(2)]
    mask_in = [s(f"mask{u}", 16) for u in range(2)] if gqa else s("mask", 16)
    mask_ready, q_masked = s("mask_ready", 2), s("qm", 2 * NQ)
    k_sum, v_sum, k_ready = s("k_sum", 2 * KC), s("v_sum", 2 * 3), s("k_ready", 2 * KC)
    v_ready = s("v_ready", 2 * (4 if gqa else 3))
    if gqa:
        v_zeroed = s("v_zeroed", 2)
    else:
        fc_in, proj_in, q_normed = s("fc_in", 64), s("proj_in", 64), s("q_normed", 8)
        fc_sum, hidden_ready, proj_sum, mlp_added = s("fc_sum", 8), s("hidden", 32), s("proj_sum", 2), s("mlp", 8)
    scores_ready, scores_masked, exp_ready = s("scores", 4 * NB2), s("scores_masked", 4 * NB2), s("exp", 4 * NB2)
    reciprocal_ready, probs_ready, probs_transposed = s("reciprocal", NB2), s("probs", H), s("probs_transposed", H)
    copied_by_act, copied_by_dve = s("copied_by_act", 3 * NB2), s("copied_by_dve", NB2)
    weighted_sum, attention_ready = s("weighted_sum", SUMS), s("attention_ready", 2 if gqa else 8)
    out_sum, residual_added, norm_ready = s("out_sum", 2), s("residual_added", 8), s("norm_ready", 8)
    OUT_COPIES = 1 if gqa else 4
    V_COPIES = 4 if gqa else 3
    pairs = G // 2

    def xg(j):
        return X[:, :, ds(j, N)]

    def spans(a, b, n):
        step = -(-(b - a) // n)
        return [(a + k * step, min(b, a + (k + 1) * step)) for k in range(n)]

    LAG_NORMALISE, LAG_TRANSPOSE, LAG_WEIGHTED = 5, 7, 12
    if gqa:
        PROJECT = {4: [("k", 1, 0)], 14: [("v", 1, 0)], 17: [("v", 1, 1)], 20: [("v", 1, 2)],
                   36: [("k", 2, 0)], 44: [("v", 2, 0)], 47: [("v", 2, 1)], 50: [("v", 2, 2)]}
    else:
        PROJECT = {2: [("k", 1, 0)], 5: [("k", 1, 1)], 8: [("k", 1, 2)], 11: [("k", 1, 3)],
                   13: [("v", 1, 0)], 15: [("v", 1, 1)], 17: [("v", 1, 2)],
                   19: [("k", 2, 0)], 21: [("k", 2, 1)], 23: [("k", 2, 2)], 25: [("k", 2, 3)],
                   27: [("v", 2, 0)], 29: [("v", 2, 1)], 30: [("v", 2, 2)]}

    TURNED = (2, 3, 4, 7) if gqa else (2, 3)

    def there(h, first):
        return h < H and (h >= 0 or not first)

    def turns(eng, step):
        for k in range(H):
            step(0, k, True, False)
        with eng.Fori(1, TURNS - 1) as t:
            for k in range(H):
                step(t, k, False, False)
        for k in range(H + LAG_WEIGHTED + 2):
            step(TURNS - 1, k, False, True)

    def sync(sp):
        n = C * D + 2 * C * KV
        core.load_weights(sp, after, spans(start, start + n, 2) + spans(w_at, w_end, 2),
                          lambda a, b: dram[name + "_w"][:, a - start:b - start] if b <= start + n else
                          dram[name + "_w"][:, n + a - w_at:n + b - w_at], lambda k: weights.sem)
        if not gqa:
            every = dram["mask2"].rearrange("b s -> (b s)").unsqueeze(0).broadcast_to([L, B * S])
            sp.dma_start(masks[0:L], every).then_inc(mask_in.sem, 16)

        def loads(t, b, u, first):
            if not first:
                sp.wait_ge(v_sum.sem, v_sum.at(t, 3 * u - 3))
            sp.dma_start(ctxt[u], dram["ctxT"][bass.ds(b, 1)].rearrange("o p c s -> p (o c) s")).then_inc(
                ctx_in[u].sem, 16)
            if gqa:
                if not first or u:
                    sp.wait_ge(mask_ready.sem, mask_ready.at(t, u))
                sp.dma_start(raw[0:L], dram["mask0"][bass.ds(b, 1)].rearrange("o l s -> (o l) s")).then_inc(
                    mask_in[u].sem, 16)

        for u in range(2):
            loads(0, u, u, True)
        with sp.Fori(1, TURNS) as t:
            for u in range(2):
                loads(t, sp.snap(2 * t + u), u, False)
        if not gqa:
            sp.wait_ge(attention_ready.sem, attention_ready.at(TURNS))
            for v, n, done in ((fc, "L2_fc", fc_in), (pj, "L2_pj", proj_in)):
                src = dram[n].rearrange("p (a b) -> p a b", b=v.shape[2])
                q = v.shape[1] // 4
                for j in range(4):
                    sp.dma_start(v[:, q * j:q * j + q], src[:, q * j:q * j + q]).then_inc(done.sem, 16)

    def tensor(pe):
        if not gqa or after:
            core.wait_before(pe, after)
        pe.wait_ge(weights.sem, weights.at(1))

        def statistics(t):
            for u in range(2):
                pe.wait_ge(norms[u].nrm.sem, norms[u].nrm.at(t))
                norms[u].pe_mean(pe, lambda c: X[:, c, bass.ds(t * (2 * N) + u * N, N)], t)
            for u in range(2):
                norms[u].pe_var(pe, t)

        def queries(t):
            for u in range(2):
                pe.wait_ge(q_ready[u].sem, q_ready[u].at(t))
                if gqa:
                    src = lambda k: X[:, k, bass.ds(t * (2 * N) + u * N, N)]
                else:
                    pe.wait_ge(q_normed.sem, q_normed.at(t, 4 * u + 4))
                    src = lambda k: yq[u][:, k, :]
                project(pe, core, 2 + u, Wq, src).then_inc(q_sum.sem, 1)

        if gqa:
            if not after:
                pe.wait_ge(core.input_head.sem, core.input_head.at(1))
            queries(0)
            core.wait_before(pe, after)
            with pe.Fori(1, pairs) as t:
                queries(t)
        else:
            statistics(0)
            with pe.Fori(0, pairs - 1) as t:
                statistics(t + 1)
                queries(t)
            queries(pairs - 1)
        for u in range(2):
            pe.wait_ge(q_ready[u].sem, q_ready[u].at(pairs))
        def keys(t, u, c):
            if c == 0:
                n = ctx_in[u % 2]
                pe.wait_ge(n.sem, n.at(t, 16 * (1 + u // 2)))
            if c >= 2:
                pe.wait_ge(k_ready.sem, k_ready.at(t, u * KC + c - 1))
            else:
                pe.wait_ge(v_ready.sem, v_ready.at(t, u * V_COPIES))
            for k in range(C):
                mm = pe.matmul(bank[6 + c % 2][:, 0:S], Wk[:, k, c * P:(c + 1) * P], ctxt[u % 2][:, k, :],
                               start=k == 0, stop=k == C - 1)
            mm.then_inc(k_sum.sem, 1)

        def values(t, u, j):
            a, n = SC[j]
            if gqa:
                o = bank[6][0:n, j * P:(j + 1) * P]
                if j == 0:
                    pe.wait_ge(k_ready.sem, k_ready.at(t, u + 1))
            else:
                o = bank[6 + j % 2][0:n, :]
                if j < 2:
                    pe.wait_ge(k_ready.sem, k_ready.at(t, u * KC + 3 + j))
                else:
                    pe.wait_ge(v_ready.sem, v_ready.at(t, u * V_COPIES + 1))
            for k in range(C):
                mm = pe.matmul(o, ctxt[u % 2][:, k, a:a + n], Wv[:, k, :], start=k == 0, stop=k == C - 1)
            mm.then_inc(v_sum.sem, 1)

        def weighted(t, m):
            back, mt = (1 if m < 0 else 0), m % NB2
            u, nl = mt // NBLK, mt % NBLK
            if gqa and nl % 4 != 3:
                return
            copied(pe, t, 4 * m + 2)
            copied(pe, t, 4 * m + 3)
            if nl == (3 if gqa else 0):
                pe.wait_ge(v_ready.sem, v_ready.at(t, V_COPIES * (u + 1 - 2 * back)))
                pe.wait_ge(attention_ready.sem, attention_ready.at(t, OUT_COPIES * (u - 2 * back)))
            for j, (a, w) in enumerate(SC):
                for x in range(4):
                    if gqa:
                        kv = ORDER[nl - 3 + x]
                        mm = pe.matmul(bank[5][32 * x:32 * x + 32, 0:4 * L], vs[u][0:w, j, kv, :],
                                       pT[(m - 3 + x) % 4][0:w, j].rearrange("p h l -> p (h l)"),
                                       start=nl == 3 and j == 0, stop=nl == 7 and j == 2)
                    else:
                        mm = pe.matmul(bank[5][32 * x:32 * x + 32, nl * L:(nl + 1) * L],
                                       vs[u][0:w, j, nl, 32 * x:32 * x + 32], pT[m % 4][0:w, j, x, :],
                                       start=j == 0, stop=j == 2)
            mm.then_inc(weighted_sum.sem, 1)

        def step(t, k, first, last):
            if k < H:
                n, x, u = k // 4, k % 4, k // (H // 2)
                nl = n % NBLK
                if k % (H // 2) == 0:
                    pe.wait_ge(q_masked.sem, q_masked.at(t, NQ * (u + 1)))
                    pe.wait_ge(k_ready.sem, k_ready.at(t, KC * (u + 1)))
                if k >= 2 or not first:
                    pe.wait_ge(scores_masked.sem, scores_masked.at(t, k - 1))
                q = qm[u][:, ORDER[nl], x, :] if gqa else qm[u][:, x, nl, :]
                pe.matmul(bank[k % 2][0:L, 0:S], q, kT[u][:, 0 if gqa else nl, :], start=True,
                          stop=True).then_inc(scores_ready.sem, 1)
            h = k - LAG_TRANSPOSE
            if there(h, first):
                pe.wait_ge(probs_ready.sem, probs_ready.at(t, h + 1))
                if h >= len(TURNED) or not first:
                    copied(pe, t, h - len(TURNED))
                for j, (a, w) in enumerate(SC):
                    mm = pe.transpose(bank[TURNED[h % len(TURNED)]][0:w, j * L:(j + 1) * L], pr[h % 8][0:L, a:a + w],
                                      ident[0:L, 0:L])
                mm.then_inc(probs_transposed.sem, 1)
            h = k - LAG_WEIGHTED
            if there(h, first) and h % 4 == 0:
                weighted(t, h // 4)
            for what, u, c in PROJECT.get(k, []):
                if not (last and u == 2):
                    (keys if what == "k" else values)(t, u, c)

        for c in range(KC):
            keys(0, 0, c)
        for j in range(3):
            values(0, 0, j)
        turns(pe, step)
        pe.wait_ge(attention_ready.sem, attention_ready.at(TURNS))

        def output(t):
            for u in range(2):
                if not gqa:
                    pe.wait_ge(hidden_ready.sem, hidden_ready.at(t))
                pe.wait_ge(residual_added.sem, residual_added.at(t))
                src = lambda k: qT[:, k, bass.ds(t * (2 * N) + u * N, N)]
                project(pe, core, 2 + u, Wo, src).then_inc(out_sum.sem, 1)

        def behind_it(t, more):
            for u in range(2):
                pe.wait_ge(residual_added.sem, residual_added.at(t, 4 * u + 4))
                if not gqa:
                    pe.wait_ge(mlp_added.sem, mlp_added.at(t))
                norms[u].pe_mean(pe, lambda c: X[:, c, bass.ds(t * (2 * N) + u * N, N)], t + behind)
            for u in range(2):
                norms[u].pe_var(pe, t + behind)
            if more:
                pe_next_output(t)
            if gqa:
                return
            for q in range(8):
                u = q // 4
                if q == 0:
                    pe.wait_ge(fc_in.sem, fc_in.at(1))
                if q < 2:
                    pe.wait_ge(residual_added.sem, residual_added.at(t + 1 if more else t, 4 * q + 4))
                if q % 4 == 0:
                    pe.wait_ge(norm_ready.sem, norm_ready.at(t, 4 * u + 4))
                if q >= 2:
                    pe.wait_ge(hidden_ready.sem, hidden_ready.at(t, 4 * (q - 1)))
                for m in range(4):
                    j = (q % 4) * 4 + m
                    for k in range(C):
                        mm = pe.matmul(part(2 + q % 2, m), fc[:, k, j * P:(j + 1) * P], norms[u].yc[:, k, :],
                                       start=k == 0, stop=k == C - 1)
                mm.then_inc(fc_sum.sem, 1)
            pe.wait_ge(proj_in.sem, proj_in.at(1))
            for u in range(2):
                pe.wait_ge(hidden_ready.sem, hidden_ready.at(t, 16 * (u + 1)))
                project(pe, core, u, pj, lambda k: hid[u][:, k, :], k_chunks=F // P).then_inc(proj_sum.sem, 1)

        def pe_next_output(t):
            for u in range(2):
                if not gqa:
                    pe.wait_ge(hidden_ready.sem, hidden_ready.at(t))
                pe.wait_ge(residual_added.sem, residual_added.at(t, 4 * u + 4))
                project(pe, core, 2 + u, Wo,
                        lambda k: qT[:, k, bass.ds(t * (2 * N) + 2 * N + u * N, N)]).then_inc(out_sum.sem, 1)

        output(0)
        with pe.Fori(0, pairs - 1) as t:
            behind_it(t, True)
        behind_it(pairs - 1, False)

    def vector(dve):
        core.wait_before(dve, after)
        dve.wait_ge(weights.sem, weights.at(1))
        for u in range(2):
            if gqa:
                dve.memset(vs[u], 0.0).then_inc(v_zeroed.sem, 1)

        def norm_ahead(t):
            for u in range(2):
                dve.wait_ge(q_normed.sem, q_normed.at(t))
                norms[u].dve_center(dve, X[:, :, bass.ds(t * (2 * N) + u * N, N)], t)
            for u in range(2):
                norms[u].scale(dve, t)

        def queries(t):
            for u in range(2):
                dve.wait_ge(q_sum.sem, q_sum.at(t, u + 1))
                for c in range(C):
                    dve.tensor_scalar(qT[:, c, bass.ds(t * (2 * N) + u * N, N)], part(2 + u, c), vec_(bq, c), scale,
                                      ALU.add, ALU.mult).then_inc(q_ready[u].sem, 1)

        if gqa:
            with dve.Fori(0, pairs) as t:
                queries(t)
        else:
            norm_ahead(0)
            with dve.Fori(0, pairs - 1) as t:
                norm_ahead(t + 1)
                queries(t)
            queries(pairs - 1)

        def mask(t, u):
            v = nmask[u % 2][0:L]
            if gqa:
                n = mask_in[u % 2]
                dve.wait_ge(n.sem, n.at(t, 16 * (1 + u // 2)))
                dve.tensor_scalar(v, raw[0:L], -1.0, None, ALU.mult).then_inc(mask_ready.sem, 1)
            else:
                dve.tensor_scalar(v, masks[0:L, bass.ds(t * (2 * S) + u * S, S)], -FLT, FLT, ALU.mult,
                                  ALU.add).then_inc(mask_ready.sem, 1)

        def values(t, u):
            v = vs[u % 2]
            if gqa:
                dve.wait_ge(v_sum.sem, v_sum.at(t, 3 * u + 3))
                for j0, j1, w in ((0, 2, P), (2, 3, SC[2][1])):
                    for odd in range(2):
                        src = bank[6][0:w, j0 * P:j1 * P].rearrange("p (j a o d) -> p j a o d", a=4, o=2, d=16)
                        dst = v[0:w, j0:j1].rearrange("p j (a o) d -> p j a o d", o=2)
                        dve.tensor_copy(dst[:, :, :, odd, 16 * odd:16 * odd + 16],
                                        src[:, :, :, odd]).then_inc(v_ready.sem, 1)
            else:
                for j, (a, w) in enumerate(SC):
                    value_chunk(t, u, j, w)

        def value_chunk(t, u, j, w):
            dve.wait_ge(v_sum.sem, v_sum.at(t, 3 * u + j + 1))
            dve.tensor_copy(vs[u % 2][0:w, j].rearrange("p a b -> p (a b)"),
                            bank[6 + j % 2][0:w, :]).then_inc(v_ready.sem, 1)

        def step(t, k, first, last):
            if k < H:
                u = k // (H // 2)
                if k % (H // 2) == 0:
                    dve.wait_ge(mask_ready.sem, mask_ready.at(t, u + 1))
                if k >= 4 or not first:
                    dve.wait_ge(exp_ready.sem, exp_ready.at(t, k - 3))
                dve.wait_ge(scores_ready.sem, scores_ready.at(t, k + 1))
                dve.memset(carry[0:1, k:k + 1], 0.0)
                dve.tensor_tensor_reduce(out=sm[k % 4][0:L], in0=bank[k % 2][0:L, 0:S], in1=nmask[u][0:L],
                                         scale=1.0, scalar=FLT, op0=ALU.add, op1=ALU.min,
                                         accum_out=nmx[0:L, k:k + 1]).then_inc(scores_masked.sem, 1)
            h = k - LAG_NORMALISE
            if there(h, first):
                c = h % H
                if h % 4 == 0:
                    dve.wait_ge(exp_ready.sem, exp_ready.at(t, h + 4))
                    dve.reciprocal(rden[0:L, c:c + 4], den[0:L, c:c + 4]).then_inc(reciprocal_ready.sem, 1)
                    dve.wait_ge(reciprocal_ready.sem, reciprocal_ready.at(t, h // 4 + 1))
                p = pr[h % 8][0:L]
                dve.tensor_scalar(p, p, rden[0:L, c:c + 1], None, ALU.mult).then_inc(probs_ready.sem, 1)
            h = k - LAG_TRANSPOSE
            if there(h, first) and h % 4 == 3:
                dve.wait_ge(probs_transposed.sem, probs_transposed.at(t, h + 1))
                free_pt(dve, t, h, first)
                for dst, src in transposed(h):
                    ins = dve.tensor_copy(dst, src)
                ins.then_inc(copied_by_dve.sem, 1)
            h = k - LAG_WEIGHTED - 1
            if there(h, first) and h % 4 == 0 and (h // 4) % NBLK == NBLK - 1:
                m = h // 4
                u = m // NBLK
                dve.wait_ge(weighted_sum.sem, weighted_sum.at(t, SUMS // 2 * (u + 1)))
                o = bass.ds(t * (2 * L) + u * L, L)
                if gqa:
                    dve.tensor_scalar(qT[:, :, o], bank[5][:, 0:4 * L].rearrange("p (h l) -> p h l", h=4),
                                      vec_(bv, 0), None, ALU.add).then_inc(attention_ready.sem, 1)
                else:
                    for c in range(C):
                        dve.tensor_scalar(qT[:, c, o], bank[5][:, c * L:(c + 1) * L], vec_(bv, c), None,
                                          ALU.add).then_inc(attention_ready.sem, 1)
            if k == 2:
                mask(t, 1)
            if k == H // 2 + 2 and not last:
                mask(t, 2)
            for what, u, j in PROJECT.get(k - 1, []):
                if what == "v" and not (last and u == 2):
                    if not gqa:
                        value_chunk(t, u, j, SC[j][1])
                    elif j == 2:
                        values(t, u)

        if gqa:
            dve.wait_ge(v_zeroed.sem, v_zeroed.at(1))
        else:
            dve.wait_ge(mask_in.sem, mask_in.at(1))
        mask(0, 0)
        values(0, 0)
        turns(dve, step)

        def xo(t, u):
            return X[:, :, bass.ds(t * (2 * N) + u * N, N)]

        def residual(t):
            for u in range(2):
                dve.wait_ge(out_sum.sem, out_sum.at(t, u + 1))
                x = xo(t, u)
                for c in range(C):
                    dve.scalar_tensor_tensor(x[:, c, :], part(2 + u, c), vec_(bo, c), x[:, c, :], ALU.add,
                                             ALU.add).then_inc(residual_added.sem, 1)

        def behind_it(t, more):
            for u in range(2):
                dve.wait_ge(residual_added.sem, residual_added.at(t, 4 * u + 4))
                used = norm_ready if gqa else fc_sum
                dve.wait_ge(used.sem, used.at(t))
                norms[u].dve_center(dve, xo(t, u), t + behind)
            for u in range(2):
                norms[u].scale(dve, t + behind)
            if more:
                residual(t + 1)
            if not gqa:
                for u in range(2):
                    x = xo(t, u)
                    dve.wait_ge(proj_sum.sem, proj_sum.at(t, u + 1))
                    for c in range(C):
                        dve.scalar_tensor_tensor(x[:, c, :], part(u, c), vec_("proj_b", c), x[:, c, :],
                                                 ALU.add, ALU.add).then_inc(mlp_added.sem, 1)

        residual(0)
        with dve.Fori(0, pairs - 1) as t:
            behind_it(t, True)
        behind_it(pairs - 1, False)

    def transposed(h):
        w, b, v = SC[2][1], bank[TURNED[h % len(TURNED)]], pT[h // 4 % 4]
        return ((v[:, 0:2, h % 4, :], b[:, 0:2 * L].rearrange("p (j l) -> p j l", j=2)),
                (v[0:w, 2, h % 4, :], b[0:w, 2 * L:3 * L]))

    def copied(eng, t, h):
        if h % 4 == 3:
            eng.wait_ge(copied_by_dve.sem, copied_by_dve.at(t, h // 4 + 1))
        else:
            eng.wait_ge(copied_by_act.sem, copied_by_act.at(t, 3 * (h // 4) + h % 4 + 1))

    def free_pt(eng, t, h, first):
        m = h // 4
        if h % 4 in (0, 3) and (m >= 4 or not first):
            eng.wait_ge(weighted_sum.sem, weighted_sum.at(t, m // 4 if gqa else m - 3))

    def scalar(act):
        core.wait_before(act, after)
        act.wait_ge(weights.sem, weights.at(1))
        if not gqa:
            def norm_ahead(t, first):
                for u in range(2):
                    norms[u].act_square(act, t)
                for u in range(2):
                    norms[u].act_rstd(act, t)
                for u in range(2):
                    norms[u].wait_scaled(act, t)
                    if not first:
                        act.wait_ge(q_sum.sem, q_sum.at(t, u - 1))
                    for c in range(C):
                        act.activation(yq[u][:, c, :], norms[u].yc[:, c, :], ACT.Identity, bias=vec_("ln1_b", c),
                                       scale=vec_("ln1_w", c)).then_inc(q_normed.sem, 1)

            norm_ahead(0, True)
            with act.Fori(1, pairs) as t:
                norm_ahead(t, False)

        def keys(t, u, c):
            act.wait_ge(k_sum.sem, k_sum.at(t, KC * u + c + 1))
            act.activation(kT[u % 2][:, c, :], bank[6 + c % 2][:, 0:S], ACT.Identity,
                           bias=vec_(bk, c)).then_inc(k_ready.sem, 1)

        def step(t, k, first, last):
            if k < H:
                act.wait_ge(scores_masked.sem, scores_masked.at(t, k + 1))
                if k >= 8 or not first:
                    act.wait_ge(probs_transposed.sem, probs_transposed.at(t, k - 7))
                act.activation(pr[k % 8][0:L], sm[k % 4][0:L], ACT.Exp, bias=nmx[0:L, k:k + 1],
                               scale=-1.0, accum_out=den[0:L, k:k + 1]).then_inc(exp_ready.sem, 1)
            h = k - LAG_TRANSPOSE
            if there(h, first) and h % 4 != 3:
                act.wait_ge(probs_transposed.sem, probs_transposed.at(t, h + 1))
                free_pt(act, t, h, first)
                for dst, src in transposed(h):
                    ins = act.activation(dst, src, ACT.Copy)
                ins.then_inc(copied_by_act.sem, 1)
            for what, u, c in PROJECT.get(k - 1, []):
                if what == "k" and not (last and u == 2):
                    keys(t, u, c)

        for c in range(KC):
            keys(0, 0, c)
        turns(act, step)
        with act.Fori(0, pairs) as t:
            for u in range(2):
                norms[u].act_square(act, t + behind)
            for u in range(2):
                norms[u].act_rstd(act, t + behind)
            for u in range(2):
                norms[u].wait_scaled(act, t + behind)
                for c in range(C):
                    y = norms[u].yc[:, c, :]
                    o = X[:, c, bass.ds(t * (2 * N) + u * N, N)] if gqa else y
                    act.activation(o, y, ACT.Identity, bias=vec_(bet, c),
                                   scale=vec_(gam, c)).then_inc(norm_ready.sem, 1)
            if not gqa:
                for q in range(8):
                    act.wait_ge(fc_sum.sem, fc_sum.at(t, q + 1))
                    for m in range(4):
                        j = (q % 4) * 4 + m
                        act.activation(hid[q // 4][:, j, :], part(2 + q % 2, m), GELU,
                                       bias=vec[:, 9 + j // 4, j % 4:j % 4 + 1]).then_inc(hidden_ready.sem, 1)

    def gpsimd(pool):
        for u in range(2):
            pool.wait_ge(q_ready[u].sem, q_ready[u].at(pairs))

        def masked(t, u):
            for h in range(NQ):
                pool.tensor_tensor(qm[u][:, h], qT[:, :, bass.ds(t * (2 * L) + u * L, L)],
                                   hm[:, h:h + 1].unsqueeze(2).broadcast_to([P, C, L]),
                                   ALU.mult).then_inc(q_masked.sem, 1)

        for u in range(2):
            masked(0, u)
        with pool.Fori(1, TURNS) as t:
            for u in range(2):
                pool.wait_ge(scores_ready.sem, scores_ready.at(t, H // 2 * (u - 1)))
                masked(t, u)

    last = norm_ready if gqa else mlp_added
    return Layer(sync, tensor, vector, scalar, gpsimd, (last.sem, last.at(pairs)),
                 (attention_ready.sem, attention_ready.at(TURNS)), left,
                 (pairs, lambda t: (last.sem, last.at(t, 8))))



def cols(v):
    return np.ascontiguousarray(v.reshape(C, P).T)


def rows(w):
    return w.reshape(-1, P, w.shape[1]).transpose(1, 0, 2)


PERM = np.arange(D).reshape(C, HC, HS).transpose(0, 2, 1).reshape(-1)


def pack(parts):
    outs = []
    for a in parts:
        a = a.reshape(a.shape[0], -1)
        n = -(-a.shape[1] // 8) * 8
        b = np.zeros((P, n), np.float32)
        b[:a.shape[0], :a.shape[1]] = a
        outs.append(b)
    return np.concatenate(outs, 1)


def rwkv_weights(d, n, ctx):
    w = {k[len(f"L{n}_xattn_"):]: v for k, v in d.items() if k.startswith(f"L{n}_xattn_")}
    parts = [rows(w["Wr"].T), rows(w["Wk"].T), rows(w["Wv"].T[:, PERM]), rows(w["Wg"].T[:, PERM]),
             rows(w["maa_w1"])]
    w2 = np.zeros((P, 4, D), np.float32)
    for f in range(4):
        w2[DM * f:DM * f + DM, f] = w["maa_w2"][f]
    parts += [w2, w["maa_w2"][4], rows(w["td_w1"]), w["td_w2"]]
    u = np.broadcast_to(w["u"].reshape(-1), (D,))
    table = {"ln1_w": w["ln1_w"], "ln1_b": w["ln1_b"], "maa_x": w["maa_x"], "time_decay": w["time_decay"], "u": u,
             "gn_w": w["gn_w"][PERM], "gn_b": w["gn_b"][PERM], "ln2_w": w["ln2_w"], "ln2_b": w["ln2_b"],
             "ffn_maa_k": w["ffn_maa_k"], "ffn_maa_r": w["ffn_maa_r"], "zero": np.zeros(D, np.float32)}
    for f in range(5):
        table[f"stack{f}"] = w["maa_stack"].reshape(5, D)[f]
    parts.append(np.stack([cols(table[k]) for k in VEC], 1))
    s0 = ctx[:, 2:2 + HS].reshape(B, C, P, HS)
    parts += [s0.transpose(2, 1, 3, 0), rows(w["Wo"].T[PERM]), rows(w["Wfr"].T), rows(w["Wfk"].T), rows(w["Wfv"].T)]
    return pack(parts)


def constants(ctx):
    p = np.arange(P)
    ident = np.eye(P, dtype=np.float32)
    mean_w = np.full((P, P), 1 / D, np.float32)
    gmean = (p[:, None] % HC == p[None, :] % HC).astype(np.float32) / HS
    heads = (p[:, None] // HS == p[None, :] % HC).astype(np.float32)
    red = np.zeros((P, 56), np.float32)
    red[p, 24 + p // HS] = 1
    hm = (p[:, None] // 16 == np.arange(8)[None]).astype(np.float32)
    qm = (p[:, None] // 32 == np.arange(4)[None]).astype(np.float32)
    eps = np.broadcast_to(np.array([1e-5, 1e-6], np.float32), (P, 2))
    st = ctx[:, 0:2].reshape(B, 2, C, P).transpose(3, 2, 1, 0)
    return pack([ident, mean_w, gmean, heads, red, hm, qm, eps, st])


def spread():
    p, j = np.arange(P), np.arange(HS)
    return pack([(p[:, None, None] == HC * j[:, None] + p // HS).astype(np.float32)])


def attention_weights(w, names, q_perm, o_perm, vectors, fc_b=None):
    q, k, v, o = (w[n] for n in names)
    vec = np.zeros((P, 26, C), np.float32)
    for j, b in enumerate(vectors):
        c = b.reshape(-1, P).T
        vec[:, j, :c.shape[1]] = c
    if fc_b is not None:
        vec[:, 9:13] = fc_b.reshape(C, C, P).transpose(2, 0, 1)
    return pack([rows(q[:, q_perm]), rows(k), rows(v), rows(o[o_perm]), vec])


GQA = np.arange(D).reshape(8, 4, 16).transpose(1, 0, 2).reshape(-1)


def lay_out(inputs):
    d = {k: np.asarray(v) for k, v in inputs.items()}
    ctx = d["ctx_2048"]
    w0 = {k[9:]: v for k, v in d.items() if k.startswith("L0_xattn_")}
    w2 = {k[9:]: v for k, v in d.items() if k.startswith("L2_xattn_")}
    same = np.arange(D)
    return {
        "ctxT": np.ascontiguousarray(ctx.reshape(B, S, C, P).transpose(0, 3, 2, 1)),
        "mask0": np.ascontiguousarray(d["mask_Bx1xSxS2_ff0"].reshape(B, L, S)),
        "mask2": np.ascontiguousarray(d["mask_BxS2_bf1"]),
        "L0_w": attention_weights(w0, ("Wq", "Wk", "Wv", "Wo"), GQA, GQA,
                                  [w0["bq"][GQA], w0["bk"], w0["bv"], w0["bo"], w0["gamma"], w0["beta"]]),
        "L2_w": attention_weights(w2, ("q_w", "k_w", "v_w", "cproj_w"), same, same,
                                  [w2[n] for n in ("ln1_w", "ln1_b", "q_b", "k_b", "v_b", "cproj_b", "ln2_w", "ln2_b",
                                                   "proj_b")], w2["fc_b"]),
        "L2_fc": pack([rows(w2["fc_w"])]),
        "L2_pj": pack([rows(w2["proj_w"])]),
        "xT": np.ascontiguousarray(d["x"].reshape(T, C, P).transpose(2, 1, 0)).reshape(P, C * T),
        "const": constants(ctx),
        "spread": spread(),
        "L1_w": rwkv_weights(d, 1, ctx),
        "L3_w": rwkv_weights(d, 3, ctx),
    }


LAYERS = (0, 1, 2, 3)


def kernel(**inputs):
    import concourse.bacc as _bacc
    from concourse.bass_utils import run_bass_kernel_spmd as _run

    nc = _bacc.Bacc("TRN2", target_bir_lowering=False, num_devices=1)
    arrays = lay_out(inputs)
    dram = {n: nc.dram_tensor(n, a.shape, mybir.dt.from_np(a.dtype), kind="ExternalInput").ap()
            for n, a in arrays.items()}
    out = nc.dram_tensor("outT", [P, C * T], F32, kind="ExternalOutput").ap()
    program(nc, dram, out, LAYERS)
    r = _run(nc, [arrays], core_ids=[0])
    got = np.asarray(r.results[0]["outT"])
    return np.ascontiguousarray(got.reshape(P, C, T).transpose(2, 1, 0)).reshape(B, L, D)
```
